# Optimizing a Trainium2 kernel written in Bass

```python
import numpy as np
import jax
import jax.numpy as jnp

def _softmax(x, axis=-1):
    return jax.nn.softmax(x, axis=axis)

def _gelu(x):
    return jax.nn.gelu(x, approximate=True)

def _silu(x):
    return jax.nn.silu(x)

def _sigmoid(x):
    return jax.nn.sigmoid(x)

def _layernorm(x, axis=-1, eps=1e-05):
    m = jnp.mean(x, axis=axis, keepdims=True)
    v = jnp.var(x, axis=axis, keepdims=True)
    return (x - m) / jnp.sqrt(v + eps)

def _scatter_add(tgt, idx, src, axis=0):
    return tgt.at[idx].add(src)

def _segment_sum(src, seg, n):
    return jax.ops.segment_sum(src, seg, n)
kernel_name = 'mk_decoder_postln_d2_seqx_r4_035017'

def setup_inputs(seed: int=0):
    np.random.seed(seed)
    _w = jnp.asarray

    def _rec_inputs():
        import jax
        import jax.numpy as jnp
        _rk = jax.random.key(seed)
        x = -0.0003929 + 0.9999 * jax.random.normal(jax.random.fold_in(_rk, 1), (8, 256, 256), jnp.float32)
        _lenS = 256 - jax.random.randint(jax.random.fold_in(_rk, 7), (8,), 0, max(1, 256 // 4) + 1, jnp.int32)
        _lenS2 = 256 - jax.random.randint(jax.random.fold_in(_rk, 8), (8,), 0, max(1, 256 // 4) + 1, jnp.int32)
        _ctx_768P = jax.random.normal(jax.random.fold_in(_rk, 11), (8, 16, 192), jnp.float32)
        _ctx_768c = jax.random.dirichlet(jax.random.fold_in(_rk, 511), 0.3 * jnp.ones((16,), jnp.float32), (8, 256))
        _ctx_768t = jnp.einsum('bsk,bkd->bsd', _ctx_768c, _ctx_768P)
        _ctx_768t = _ctx_768t * jax.lax.rsqrt(jnp.mean(jnp.square(_ctx_768t)) + 1e-12) * 0.953939
        ctx_768 = -7.36909e-05 + 0.999899 * (_ctx_768t + 0.3 * jax.random.normal(jax.random.fold_in(_rk, 611), (8, 256, 192), jnp.float32))
        return (x, ctx_768)
    x, ctx_768 = _rec_inputs()

    def _L0_attn_setup():
        import jax, jax.numpy as jnp
        from jax import lax
        import numpy as np
        D_MODEL = 256
        D_STATE = 16
        D_CONV = 4
        EXPAND = 2
        D_INNER = D_MODEL * EXPAND
        EPS = 1e-05
        key = jax.random.key(seed)
        ks = jax.random.split(key, 12)
        B, L = (2, 512)
        x = jax.random.normal(ks[0], (B, L, D_MODEL), jnp.float32)
        s = 0.02
        ln_g = jnp.ones((D_MODEL,), jnp.float32)
        ln_b = jnp.zeros((D_MODEL,), jnp.float32)
        W_in = jax.random.normal(ks[1], (D_MODEL, 2 * D_INNER), jnp.float32) * s
        conv_w = jax.random.normal(ks[2], (D_INNER, D_CONV), jnp.float32) * 0.2
        conv_b = jnp.zeros((D_INNER,), jnp.float32)
        W_xp = jax.random.normal(ks[3], (D_INNER, 2 * D_STATE + 1), jnp.float32) * s
        W_dt = jax.random.normal(ks[4], (1, D_INNER), jnp.float32) * s
        dt = jnp.exp(jax.random.uniform(ks[5], (D_INNER,)) * (np.log(0.1) - np.log(0.001)) + np.log(0.001))
        b_dt = dt + jnp.log(-jnp.expm1(-dt))
        A_log = jnp.log(jnp.broadcast_to(jnp.arange(1, D_STATE + 1, dtype=jnp.float32)[None, :], (D_INNER, D_STATE)))
        D = jnp.ones((D_INNER,), jnp.float32)
        W_out = jax.random.normal(ks[6], (D_INNER, D_MODEL), jnp.float32) * s
        return {'x': x, 'ln_g': ln_g, 'ln_b': ln_b, 'W_in': W_in, 'conv_w': conv_w, 'conv_b': conv_b, 'W_xp': W_xp, 'W_dt': W_dt, 'b_dt': b_dt, 'A_log': A_log, 'D': D, 'W_out': W_out}
    _L0_attn_all = _L0_attn_setup()
    _L0_attn_in = {k: v for k, v in _L0_attn_all.items() if k in ('ln_g', 'ln_b', 'W_in', 'conv_w', 'conv_b', 'W_xp', 'W_dt', 'b_dt', 'A_log', 'D', 'W_out')}
    del _L0_attn_all

    def _L0_xattn_setup():
        import jax, jax.numpy as jnp
        import numpy as np
        EPS = 1e-08
        key = jax.random.key(seed)
        kv, kt, k1, k2, k3, k4 = jax.random.split(key, 6)
        B, S = (16, 256)
        VD, TD, H = (256, 192, 128)
        visual_features = jax.random.normal(kv, (B, S, VD), dtype=jnp.float32)
        text_features = jax.random.normal(kt, (B, S, TD), dtype=jnp.float32)
        Wv = jax.random.normal(k1, (H, VD), dtype=jnp.float32) * (1.0 / np.sqrt(VD))
        bv = jax.random.normal(k2, (H,), dtype=jnp.float32) * 0.01
        Wt = jax.random.normal(k3, (H, TD), dtype=jnp.float32) * (1.0 / np.sqrt(TD))
        bt = jax.random.normal(k4, (H,), dtype=jnp.float32) * 0.01
        return {'visual_features': visual_features, 'text_features': text_features, 'Wv': Wv, 'bv': bv, 'Wt': Wt, 'bt': bt}
    _L0_xattn_all = _L0_xattn_setup()
    _L0_xattn_in = {k: v for k, v in _L0_xattn_all.items() if k in ('Wv', 'bv', 'Wt', 'bt')}
    del _L0_xattn_all

    def _L0_ffn_setup():
        import jax, jax.numpy as jnp
        import numpy as np
        TOP_K = 2
        key = jax.random.key(seed)
        ks = jax.random.split(key, 7)
        B_, S, D, F, E, R = (2, 512, 256, 1024, 4, 4)
        x = jax.random.normal(ks[0], (B_, S, D), dtype=jnp.float32)
        Wg = jax.random.normal(ks[1], (E, D), dtype=jnp.float32) * (1.0 / np.sqrt(D))
        bg = jnp.zeros((E,), dtype=jnp.float32)
        Wi = jax.random.normal(ks[2], (F, D), dtype=jnp.float32) * (1.0 / np.sqrt(D))
        Wo = jax.random.normal(ks[3], (D, F), dtype=jnp.float32) * (1.0 / np.sqrt(F))
        A = jax.random.normal(ks[4], (E, R, D), dtype=jnp.float32) * (1.0 / np.sqrt(D))
        Bm = jax.random.normal(ks[5], (E, F, R), dtype=jnp.float32) * 0.01
        return {'x': x, 'Wg': Wg, 'bg': bg, 'Wi': Wi, 'Wo': Wo, 'A': A, 'B': Bm}
    _L0_ffn_all = _L0_ffn_setup()
    _L0_ffn_in = {k: v for k, v in _L0_ffn_all.items() if k in ('Wg', 'bg', 'Wi', 'Wo', 'A', 'B')}
    del _L0_ffn_all

    def _L1_attn_setup():
        import jax, jax.numpy as jnp
        import numpy as np
        B, S, H = (2, 512, 256)
        NQ, NKV, HD, RANK = (16, 4, 64, 8)
        THETA = 10000.0
        LORA_SCALE = 16 / RANK
        ATTN_SCALE = 1.0 / np.sqrt(HD)

        def _lora_proj(x, W, A, Bm):
            return x @ W.T + x @ A.T @ Bm.T * LORA_SCALE

        def _rope(x, cos_h, sin_h):
            x1, x2 = (x[..., ::2], x[..., 1::2])
            return jnp.concatenate([x1 * cos_h - x2 * sin_h, x1 * sin_h + x2 * cos_h], axis=-1)

        def _forward(x, Wq, Wk, Wv, Wo, qA, qB, kA, kB, vA, vB, oA, oB):
            b, s, _ = x.shape
            q = _lora_proj(x, Wq, qA, qB).reshape(b, s, NQ, HD).transpose(0, 2, 1, 3)
            k = _lora_proj(x, Wk, kA, kB).reshape(b, s, NKV, HD).transpose(0, 2, 1, 3)
            v = _lora_proj(x, Wv, vA, vB).reshape(b, s, NKV, HD).transpose(0, 2, 1, 3)
            inv_freq = 1.0 / THETA ** (jnp.arange(0, HD, 2, dtype=jnp.float32) / HD)
            freqs = jnp.arange(s, dtype=jnp.float32)[:, None] * inv_freq[None, :]
            cos_h = jnp.cos(freqs)[None, None]
            sin_h = jnp.sin(freqs)[None, None]
            q = _rope(q, cos_h, sin_h)
            k = _rope(k, cos_h, sin_h)
            rep = NQ // NKV
            k = jnp.repeat(k, rep, axis=1)
            v = jnp.repeat(v, rep, axis=1)
            attn = jax.nn.softmax(jnp.einsum('bhqd,bhkd->bhqk', q, k) * ATTN_SCALE, axis=-1)
            out = jnp.einsum('bhqk,bhkd->bhqd', attn, v)
            out = out.transpose(0, 2, 1, 3).reshape(b, s, NQ * HD)
            return _lora_proj(out, Wo, oA, oB)
        key = jax.random.key(seed)
        ks = jax.random.split(key, 14)
        n = lambda k, shape, s: jax.random.normal(k, shape, jnp.float32) * s
        return {'x': n(ks[0], (B, S, H), 1.0), 'Wq': n(ks[1], (NQ * HD, H), 0.02), 'Wk': n(ks[2], (NKV * HD, H), 0.02), 'Wv': n(ks[3], (NKV * HD, H), 0.02), 'Wo': n(ks[4], (H, NQ * HD), 0.02), 'qA': n(ks[5], (RANK, H), 0.05), 'qB': n(ks[6], (NQ * HD, RANK), 0.05), 'kA': n(ks[7], (RANK, H), 0.05), 'kB': n(ks[8], (NKV * HD, RANK), 0.05), 'vA': n(ks[9], (RANK, H), 0.05), 'vB': n(ks[10], (NKV * HD, RANK), 0.05), 'oA': n(ks[11], (RANK, NQ * HD), 0.05), 'oB': n(ks[12], (H, RANK), 0.05)}
    _L1_attn_all = _L1_attn_setup()
    _L1_attn_in = {k: v for k, v in _L1_attn_all.items() if k in ('Wq', 'Wk', 'Wv', 'Wo', 'qA', 'qB', 'kA', 'kB', 'vA', 'vB', 'oA', 'oB')}
    del _L1_attn_all

    def _L1_xattn_setup():
        import jax, jax.numpy as jnp
        import numpy as np
        EPS = 1e-05

        def layernorm(x, g, b):
            mu = jnp.mean(x, axis=-1, keepdims=True)
            var = jnp.mean(jnp.square(x - mu), axis=-1, keepdims=True)
            return (x - mu) * jax.lax.rsqrt(var + EPS) * g + b
        key = jax.random.key(seed)
        ks = jax.random.split(key, 12)
        B, L1, L2 = (8, 512, 512)
        D1, D2, E = (256, 192, 256)
        s1, s2, se = (D1 ** (-0.5), D2 ** (-0.5), E ** (-0.5))
        return {'modality1': jax.random.normal(ks[0], (B, L1, D1), jnp.float32), 'modality2': jax.random.normal(ks[1], (B, L2, D2), jnp.float32), 'ln1_g': jnp.ones((D1,), jnp.float32), 'ln1_b': jnp.zeros((D1,), jnp.float32), 'ln2_g': jnp.ones((D2,), jnp.float32), 'ln2_b': jnp.zeros((D2,), jnp.float32), 'Wq': jax.random.normal(ks[2], (D1, E), jnp.float32) * s1, 'bq': jax.random.normal(ks[3], (E,), jnp.float32) * 0.01, 'Wk': jax.random.normal(ks[4], (D2, E), jnp.float32) * s2, 'bk': jax.random.normal(ks[5], (E,), jnp.float32) * 0.01, 'Wv': jax.random.normal(ks[6], (D2, E), jnp.float32) * s2, 'bv': jax.random.normal(ks[7], (E,), jnp.float32) * 0.01, 'Wo': jax.random.normal(ks[8], (E, D1), jnp.float32) * se, 'bo': jax.random.normal(ks[9], (D1,), jnp.float32) * 0.01}
    _L1_xattn_all = _L1_xattn_setup()
    _L1_xattn_in = {k: v for k, v in _L1_xattn_all.items() if k in ('ln1_g', 'ln1_b', 'ln2_g', 'ln2_b', 'Wq', 'bq', 'Wk', 'bk', 'Wv', 'bv', 'Wo', 'bo')}
    del _L1_xattn_all

    def _L1_ffn_setup():
        import jax, jax.numpy as jnp
        import numpy as np
        from jax import lax
        T, B, I, M, O = (64, 64, 256, 256, 256)

        def _xavier(key, shape):
            fan_out, fan_in = shape
            limit = float(np.sqrt(6.0 / (fan_in + fan_out)))
            return jax.random.uniform(key, shape, jnp.float32, -limit, limit)
        key = jax.random.key(seed)
        ks = jax.random.split(key, 9)
        x = jax.random.normal(ks[0], (T, B, I), jnp.float32)
        return {'x': x, 'wf': _xavier(ks[1], (M, I)), 'uf': _xavier(ks[2], (M, M)), 'bf': jnp.zeros((M,), jnp.float32), 'wi': _xavier(ks[3], (M, I)), 'ui': _xavier(ks[4], (M, M)), 'bi': jnp.zeros((M,), jnp.float32), 'wc': _xavier(ks[5], (M, I)), 'uc': _xavier(ks[6], (M, M)), 'bc': jnp.zeros((M,), jnp.float32), 'wo': _xavier(ks[7], (O, I)), 'uo': _xavier(ks[8], (O, M)), 'bo': jnp.zeros((O,), jnp.float32), 'in_c': jnp.zeros((M,), jnp.float32)}
    _L1_ffn_all = _L1_ffn_setup()
    _L1_ffn_in = {k: v for k, v in _L1_ffn_all.items() if k in ('wf', 'uf', 'bf', 'wi', 'ui', 'bi', 'wc', 'uc', 'bc', 'wo', 'uo', 'bo', 'in_c')}
    del _L1_ffn_all
    return {'x': x, 'ctx_768': ctx_768, 'L0_attn_ln_g': _L0_attn_in['ln_g'], 'L0_attn_ln_b': _L0_attn_in['ln_b'], 'L0_attn_W_in': _L0_attn_in['W_in'], 'L0_attn_conv_w': _L0_attn_in['conv_w'], 'L0_attn_conv_b': _L0_attn_in['conv_b'], 'L0_attn_W_xp': _L0_attn_in['W_xp'], 'L0_attn_W_dt': _L0_attn_in['W_dt'], 'L0_attn_b_dt': _L0_attn_in['b_dt'], 'L0_attn_A_log': _L0_attn_in['A_log'], 'L0_attn_D': _L0_attn_in['D'], 'L0_attn_W_out': _L0_attn_in['W_out'], 'L0_xattn_Wv': _L0_xattn_in['Wv'], 'L0_xattn_bv': _L0_xattn_in['bv'], 'L0_xattn_Wt': _L0_xattn_in['Wt'], 'L0_xattn_bt': _L0_xattn_in['bt'], 'L0_ffn_Wg': _L0_ffn_in['Wg'], 'L0_ffn_bg': _L0_ffn_in['bg'], 'L0_ffn_Wi': _L0_ffn_in['Wi'], 'L0_ffn_Wo': _L0_ffn_in['Wo'], 'L0_ffn_A': _L0_ffn_in['A'], 'L0_ffn_B': _L0_ffn_in['B'], 'L1_attn_Wq': _L1_attn_in['Wq'], 'L1_attn_Wk': _L1_attn_in['Wk'], 'L1_attn_Wv': _L1_attn_in['Wv'], 'L1_attn_Wo': _L1_attn_in['Wo'], 'L1_attn_qA': _L1_attn_in['qA'], 'L1_attn_qB': _L1_attn_in['qB'], 'L1_attn_kA': _L1_attn_in['kA'], 'L1_attn_kB': _L1_attn_in['kB'], 'L1_attn_vA': _L1_attn_in['vA'], 'L1_attn_vB': _L1_attn_in['vB'], 'L1_attn_oA': _L1_attn_in['oA'], 'L1_attn_oB': _L1_attn_in['oB'], 'L1_xattn_ln1_g': _L1_xattn_in['ln1_g'], 'L1_xattn_ln1_b': _L1_xattn_in['ln1_b'], 'L1_xattn_ln2_g': _L1_xattn_in['ln2_g'], 'L1_xattn_ln2_b': _L1_xattn_in['ln2_b'], 'L1_xattn_Wq': _L1_xattn_in['Wq'], 'L1_xattn_bq': _L1_xattn_in['bq'], 'L1_xattn_Wk': _L1_xattn_in['Wk'], 'L1_xattn_bk': _L1_xattn_in['bk'], 'L1_xattn_Wv': _L1_xattn_in['Wv'], 'L1_xattn_bv': _L1_xattn_in['bv'], 'L1_xattn_Wo': _L1_xattn_in['Wo'], 'L1_xattn_bo': _L1_xattn_in['bo'], 'L1_ffn_wf': _L1_ffn_in['wf'], 'L1_ffn_uf': _L1_ffn_in['uf'], 'L1_ffn_bf': _L1_ffn_in['bf'], 'L1_ffn_wi': _L1_ffn_in['wi'], 'L1_ffn_ui': _L1_ffn_in['ui'], 'L1_ffn_bi': _L1_ffn_in['bi'], 'L1_ffn_wc': _L1_ffn_in['wc'], 'L1_ffn_uc': _L1_ffn_in['uc'], 'L1_ffn_bc': _L1_ffn_in['bc'], 'L1_ffn_wo': _L1_ffn_in['wo'], 'L1_ffn_uo': _L1_ffn_in['uo'], 'L1_ffn_bo': _L1_ffn_in['bo'], 'L1_ffn_in_c': _L1_ffn_in['in_c']}

def reference(x, ctx_768, L0_attn_ln_g, L0_attn_ln_b, L0_attn_W_in, L0_attn_conv_w, L0_attn_conv_b, L0_attn_W_xp, L0_attn_W_dt, L0_attn_b_dt, L0_attn_A_log, L0_attn_D, L0_attn_W_out, L0_xattn_Wv, L0_xattn_bv, L0_xattn_Wt, L0_xattn_bt, L0_ffn_Wg, L0_ffn_bg, L0_ffn_Wi, L0_ffn_Wo, L0_ffn_A, L0_ffn_B, L1_attn_Wq, L1_attn_Wk, L1_attn_Wv, L1_attn_Wo, L1_attn_qA, L1_attn_qB, L1_attn_kA, L1_attn_kB, L1_attn_vA, L1_attn_vB, L1_attn_oA, L1_attn_oB, L1_xattn_ln1_g, L1_xattn_ln1_b, L1_xattn_ln2_g, L1_xattn_ln2_b, L1_xattn_Wq, L1_xattn_bq, L1_xattn_Wk, L1_xattn_bk, L1_xattn_Wv, L1_xattn_bv, L1_xattn_Wo, L1_xattn_bo, L1_ffn_wf, L1_ffn_uf, L1_ffn_bf, L1_ffn_wi, L1_ffn_ui, L1_ffn_bi, L1_ffn_wc, L1_ffn_uc, L1_ffn_bc, L1_ffn_wo, L1_ffn_uo, L1_ffn_bo, L1_ffn_in_c):
    import jax
    import jax.numpy as jnp

    def _L0_attn_ref(x, ln_g, ln_b, W_in, conv_w, conv_b, W_xp, W_dt, b_dt, A_log, D, W_out):
        import jax, jax.numpy as jnp
        from jax import lax
        import numpy as np
        D_MODEL = 256
        D_STATE = 16
        D_CONV = 4
        EXPAND = 2
        D_INNER = D_MODEL * EXPAND
        EPS = 1e-05
        B, L, _ = x.shape
        residual = x
        mu = jnp.mean(x, axis=-1, keepdims=True)
        var = jnp.mean(jnp.square(x - mu), axis=-1, keepdims=True)
        xn = (x - mu) * lax.rsqrt(var + EPS) * ln_g + ln_b
        xz = xn @ W_in
        xh, z = jnp.split(xz, 2, axis=-1)
        xt = jnp.moveaxis(xh, 1, 2)
        xp = jnp.pad(xt, ((0, 0), (0, 0), (D_CONV - 1, 0)))
        conv = conv_b[None, :, None]
        for k in range(D_CONV):
            conv = conv + conv_w[None, :, k, None] * xp[:, :, k:k + L]
        xc = jax.nn.silu(jnp.moveaxis(conv, 1, 2))
        A = -jnp.exp(A_log)
        xpj = xc @ W_xp
        Bm = xpj[..., :D_STATE]
        Cm = xpj[..., D_STATE:2 * D_STATE]
        dt = jax.nn.softplus(xpj[..., -1:] @ W_dt + b_dt)
        dA = jnp.exp(dt[..., None] * A)
        dBx = dt[..., None] * Bm[:, :, None, :] * xc[..., None]

        def step(h, inp):
            dAt, dBxt, Ct = inp
            h = dAt * h + dBxt
            y = jnp.einsum('bdn,bn->bd', h, Ct)
            return (h, y)
        h0 = jnp.zeros((B, D_INNER, D_STATE), x.dtype)
        _, ys = lax.scan(step, h0, (jnp.moveaxis(dA, 1, 0), jnp.moveaxis(dBx, 1, 0), jnp.moveaxis(Cm, 1, 0)))
        y = jnp.moveaxis(ys, 0, 1) + xc * D
        out = y * jax.nn.silu(z) @ W_out
        return out + residual

    def _L0_xattn_ref(visual_features, text_features, Wv, bv, Wt, bt):
        import jax, jax.numpy as jnp
        import numpy as np
        EPS = 1e-08
        v = jnp.einsum('bsd,hd->bsh', visual_features, Wv) + bv
        t = jnp.einsum('bsd,hd->bsh', text_features, Wt) + bt
        dots = jnp.einsum('bih,bjh->bij', v, t)
        vn = jnp.linalg.norm(v, axis=-1)
        tn = jnp.linalg.norm(t, axis=-1)
        denom = jnp.maximum(vn[:, :, None] * tn[:, None, :], EPS)
        return dots / denom

    def _L0_ffn_ref(x, Wg, bg, Wi, Wo, A, B):
        import jax, jax.numpy as jnp
        import numpy as np
        TOP_K = 2
        E = Wg.shape[0]
        logits = jnp.einsum('bsd,ed->bse', x, Wg) + bg
        scores = jax.nn.softmax(logits, axis=-1)
        topv, topi = jax.lax.top_k(scores, TOP_K)
        w = jnp.sum(jax.nn.one_hot(topi, E, dtype=x.dtype) * topv[..., None], axis=-2)
        base = jnp.einsum('bsd,fd->bsf', x, Wi)
        lora_low = jnp.einsum('bsd,erd->bser', x, A)
        lora = jnp.einsum('bser,efr->bsef', lora_low, B)
        h = jax.nn.relu(base[:, :, None, :] + lora)
        expert_out = jnp.einsum('bsef,df->bsed', h, Wo)
        out = jnp.einsum('bse,bsed->bsd', w, expert_out)
        return out

    def _L1_attn_ref(x, Wq, Wk, Wv, Wo, qA, qB, kA, kB, vA, vB, oA, oB):
        import jax, jax.numpy as jnp
        import numpy as np
        B, S, H = (2, 512, 256)
        NQ, NKV, HD, RANK = (16, 4, 64, 8)
        THETA = 10000.0
        LORA_SCALE = 16 / RANK
        ATTN_SCALE = 1.0 / np.sqrt(HD)

        def _lora_proj(x, W, A, Bm):
            return x @ W.T + x @ A.T @ Bm.T * LORA_SCALE

        def _rope(x, cos_h, sin_h):
            x1, x2 = (x[..., ::2], x[..., 1::2])
            return jnp.concatenate([x1 * cos_h - x2 * sin_h, x1 * sin_h + x2 * cos_h], axis=-1)

        def _forward(x, Wq, Wk, Wv, Wo, qA, qB, kA, kB, vA, vB, oA, oB):
            b, s, _ = x.shape
            q = _lora_proj(x, Wq, qA, qB).reshape(b, s, NQ, HD).transpose(0, 2, 1, 3)
            k = _lora_proj(x, Wk, kA, kB).reshape(b, s, NKV, HD).transpose(0, 2, 1, 3)
            v = _lora_proj(x, Wv, vA, vB).reshape(b, s, NKV, HD).transpose(0, 2, 1, 3)
            inv_freq = 1.0 / THETA ** (jnp.arange(0, HD, 2, dtype=jnp.float32) / HD)
            freqs = jnp.arange(s, dtype=jnp.float32)[:, None] * inv_freq[None, :]
            cos_h = jnp.cos(freqs)[None, None]
            sin_h = jnp.sin(freqs)[None, None]
            q = _rope(q, cos_h, sin_h)
            k = _rope(k, cos_h, sin_h)
            rep = NQ // NKV
            k = jnp.repeat(k, rep, axis=1)
            v = jnp.repeat(v, rep, axis=1)
            attn = jax.nn.softmax(jnp.einsum('bhqd,bhkd->bhqk', q, k) * ATTN_SCALE, axis=-1)
            out = jnp.einsum('bhqk,bhkd->bhqd', attn, v)
            out = out.transpose(0, 2, 1, 3).reshape(b, s, NQ * HD)
            return _lora_proj(out, Wo, oA, oB)
        return _forward(x, Wq, Wk, Wv, Wo, qA, qB, kA, kB, vA, vB, oA, oB)

    def _L1_xattn_ref(modality1, modality2, ln1_g, ln1_b, ln2_g, ln2_b, Wq, bq, Wk, bk, Wv, bv, Wo, bo):
        import jax, jax.numpy as jnp
        import numpy as np
        EPS = 1e-05

        def layernorm(x, g, b):
            mu = jnp.mean(x, axis=-1, keepdims=True)
            var = jnp.mean(jnp.square(x - mu), axis=-1, keepdims=True)
            return (x - mu) * jax.lax.rsqrt(var + EPS) * g + b
        E = Wq.shape[1]
        scaling = E ** (-0.5)
        x1 = layernorm(modality1, ln1_g, ln1_b)
        x2 = layernorm(modality2, ln2_g, ln2_b)
        q = x1 @ Wq + bq
        k = x2 @ Wk + bk
        v = x2 @ Wv + bv
        scores = jnp.einsum('bqe,bke->bqk', q, k) * scaling
        attn = jax.nn.softmax(scores, axis=-1)
        ctx = jnp.einsum('bqk,bke->bqe', attn, v)
        return ctx @ Wo + bo

    def _L1_ffn_ref(x, wf, uf, bf, wi, ui, bi, wc, uc, bc, wo, uo, bo, in_c):
        import jax, jax.numpy as jnp
        import numpy as np
        from jax import lax
        T, B, I, M, O = (64, 64, 256, 256, 256)

        def _xavier(key, shape):
            fan_out, fan_in = shape
            limit = float(np.sqrt(6.0 / (fan_in + fan_out)))
            return jax.random.uniform(key, shape, jnp.float32, -limit, limit)
        batch = x.shape[1]
        c0 = jnp.broadcast_to(in_c, (batch, in_c.shape[0]))

        def step(c, xt):
            ft = jax.nn.sigmoid(xt @ wf.T + c @ uf.T + bf)
            it = jax.nn.sigmoid(xt @ wi.T + c @ ui.T + bi)
            gt = jnp.tanh(xt @ wc.T + c @ uc.T + bc)
            c = ft * c + it * gt
            return (c, None)
        c_final, _ = lax.scan(step, c0, x)
        h = jnp.tanh(jnp.einsum('tbi,oi->tbo', x, wo) + c_final @ uo.T + bo)
        return h
    x = _layernorm(x + _L0_attn_ref(x, L0_attn_ln_g, L0_attn_ln_b, L0_attn_W_in, L0_attn_conv_w, L0_attn_conv_b, L0_attn_W_xp, L0_attn_W_dt, L0_attn_b_dt, L0_attn_A_log, L0_attn_D, L0_attn_W_out), axis=-1)
    x = _layernorm(x + _L0_xattn_ref(x, ctx_768, L0_xattn_Wv, L0_xattn_bv, L0_xattn_Wt, L0_xattn_bt), axis=-1)
    x = _layernorm(x + _L0_ffn_ref(x, L0_ffn_Wg, L0_ffn_bg, L0_ffn_Wi, L0_ffn_Wo, L0_ffn_A, L0_ffn_B), axis=-1)
    x = _layernorm(x + _L1_attn_ref(x, L1_attn_Wq, L1_attn_Wk, L1_attn_Wv, L1_attn_Wo, L1_attn_qA, L1_attn_qB, L1_attn_kA, L1_attn_kB, L1_attn_vA, L1_attn_vB, L1_attn_oA, L1_attn_oB), axis=-1)
    x = _layernorm(x + _L1_xattn_ref(x, ctx_768, L1_xattn_ln1_g, L1_xattn_ln1_b, L1_xattn_ln2_g, L1_xattn_ln2_b, L1_xattn_Wq, L1_xattn_bq, L1_xattn_Wk, L1_xattn_bk, L1_xattn_Wv, L1_xattn_bv, L1_xattn_Wo, L1_xattn_bo), axis=-1)
    x = _layernorm(x + _L1_ffn_ref(x, L1_ffn_wf, L1_ffn_uf, L1_ffn_bf, L1_ffn_wi, L1_ffn_ui, L1_ffn_bi, L1_ffn_wc, L1_ffn_uc, L1_ffn_bc, L1_ffn_wo, L1_ffn_uo, L1_ffn_bo, L1_ffn_in_c), axis=-1)
    return x

_drawn_inputs = setup_inputs


def setup_inputs(seed=0):
    import zlib

    import numpy as np

    out = dict(_drawn_inputs(seed))
    spreads = {'L0_attn_ln_g': (1.0, 0.6),
     'L0_attn_ln_b': (0.0, 0.8),
     'L0_attn_conv_b': (0.0, 0.8),
     'L0_attn_D': (1.0, 0.6),
     'L0_ffn_bg': (0.0, 0.8),
     'L1_xattn_ln1_g': (1.0, 0.2),
     'L1_xattn_ln1_b': (0.0, 0.438),
     'L1_xattn_ln2_g': (1.0, 0.2),
     'L1_xattn_ln2_b': (0.0, 0.1),
     'L1_ffn_bf': (0.0, 0.657),
     'L1_ffn_bi': (0.0, 0.684),
     'L1_ffn_bc': (0.0, 0.1),
     'L1_ffn_bo': (0.0, 0.1),
     'L1_ffn_in_c': (0.0, 0.8)}
    factors = {'L0_attn_W_in': 8.0,
     'L0_attn_conv_w': 8.0,
     'L0_attn_W_xp': 8.0,
     'L0_attn_W_dt': 8.0,
     'L0_attn_b_dt': 8.0,
     'L0_attn_A_log': 8.0,
     'L0_attn_W_out': 8.0,
     'L0_xattn_bv': 8.0,
     'L0_xattn_bt': 48.012,
     'L0_ffn_A': 8.0,
     'L0_ffn_B': 8.0,
     'L1_attn_Wq': 8.0,
     'L1_attn_Wk': 8.0,
     'L1_attn_qA': 8.0,
     'L1_attn_qB': 8.0,
     'L1_attn_kA': 8.0,
     'L1_attn_kB': 8.0,
     'L1_xattn_bq': 34.936,
     'L1_xattn_bk': 64.0,
     'L1_xattn_bv': 6.041,
     'L1_xattn_bo': 5.87}
    for name, (base, spread) in spreads.items():
        noise = np.random.default_rng([zlib.crc32(name.encode()), seed]).standard_normal(out[name].shape)
        drawn = base * np.exp(spread * noise) if base else spread * noise
        out[name] = jnp.asarray(drawn.astype(out[name].dtype))
    for name, factor in factors.items():
        out[name] = (out[name] * factor).astype(out[name].dtype)
    return out
```

```python
from contextlib import ExitStack

import numpy as np

import concourse.bass as bass
from concourse import mybir

F32 = mybir.dt.float32
ALU = mybir.AluOpType
ACT = mybir.ActivationFunctionType
AX = mybir.AxisListType.X

P = 128
NB, S, D = 8, 256, 256
T = S // P
KD = D // P
CTX = 192
CTX2 = CTX - P
DI, NS, TAPS = 512, 16, 4
EC = DI // P
HN = 4
VH = 128
NE, RK = 4, 4
NLOW = NE * RK
FF = 1024
FC = FF // P
NQ, NKV, HD = 16, 4, 64
GH = NQ // NKV
HH = HD // 2
LORA = 8
LSCALE = 2.0
E2 = 256
EPS = 1e-5
BIG = 1e8

UH = NS // HN
UNITS = [(c, h) for c in range(EC) for h in range(UH)]

COUNTED = """
loads_mamba loads_rest prep_pool prep_act prep_pe prep_evac
dve_own act_own pool_own
a_x a_var a_rstd a_norm a_xnT_ps a_xnT a_in_ps a_tap a_conv a_z_tanh a_silu_z a_xc_tanh a_xc
a_xpj_ps a_xpj a_store a_B a_C a_dtl_ps a_u a_ln a_dt a_dtx a_dA a_dBx a_scan a_hC a_y_ps a_gated a_out_ps
a1_var a1_rstd a1_norm
b_ctx b_cxT_ps b_cxT b_tT_ps b_tT b_xT_ps b_xT b_vT_ps b_vT b_ss_ps b_ss b_rn b_diag b_row_ps b_dots_ps
b1_var b1_rstd b1_norm
f_xT_ps f_xT f_gl_ps f_exp f_exp_in f_low f_lowT_ps f_lowT f_wdiag f_w_ps f_wrow f_z1_ps f_z2_ps f_r f_h f_out_ps
f1_var f1_rstd f1_norm
t_xT_ps t_xT t_k_ps t_rot t_kro t_kT t_v_ps t_v t_q_ps t_ro t_qT0 t_qT1 t_qT2 t_qT3 t_s_ps t_max t_p t_pT_ps t_pT t_o_ps t_o t_oT_ps t_oT
t_out_ps t1_var t1_rstd t1_norm
c_var c_rstd c_norm c2_var c2_rstd c2_norm c_xT_ps c_xT c_x2T_ps c_x2T c_q_ps c_q c_k_ps c_k c_v_ps c_v c_s_ps c_max c_p
c_pT_ps c_pT c_ctx_ps c_ctx c_out_ps c_x4b c1_var c1_rstd c1_norm
l_xT_ps l_xT l_g_ps l_tanh l_state l_xw_ps l_xw l_kept e_load_w0 e_load_w1 e_load_x0 e_load_x1
e_cu_ps e_sum e_tanh e_var e_rstd e_norm e_store
""".split()


class Own:

    def __init__(self, eng, sem):
        self.eng, self.sem, self.n = eng, sem, 0

    def did(self, ins):
        ins.then_inc(self.sem, 1)
        self.n += 1

    def wait(self):
        self.eng.wait_ge(self.sem, self.n)

    def link(self, ins):
        self.did(ins)
        self.wait()


def build(nc, A, out):
    with ExitStack() as ctx:
        def sb(name, shape):
            return ctx.enter_context(nc.sbuf_tensor(name, shape, F32))

        phase = ctx.enter_context(nc.semaphore("phase"))
        arrived = ctx.enter_context(nc.semaphore("arrived"))
        s = {n: ctx.enter_context(nc.semaphore(n)) for n in COUNTED}
        numbers = sorted(x.num for x in s.values())
        assert numbers == list(range(numbers[0], numbers[-1] + 1))
        bank = [ctx.enter_context(nc.psum_tensor(f"bank{i}", [P, 512], F32)) for i in range(8)]
        scratch = nc.dram_tensor("xpj_scratch", (2 * NS + 1, S), F32, kind="Internal").ap()
        kept_x = nc.dram_tensor("kept_x", (NB, P, T * D), F32, kind="Internal").ap()
        kept_w = nc.dram_tensor("kept_w", (NB, P, T * D), F32, kind="Internal").ap()

        w_in = sb("w_in", [P, KD, 2 * DI]); w_xp = sb("w_xp", [P, EC, 2 * NS + 1]); w_out = sb("w_out", [P, EC, D])
        conv_w = sb("conv_w", [P, EC, TAPS]); conv_wh = sb("conv_wh", [P, EC, TAPS])
        conv_b = sb("conv_b", [P, EC]); conv_bh = sb("conv_bh", [P, EC])
        ln_g = sb("ln_g", [P, KD]); ln_b = sb("ln_b", [P, KD])
        w_dt = sb("w_dt", [P, EC]); b_dt = sb("b_dt", [P, EC]); a_log = sb("a_log", [P, EC, NS]); a_neg = sb("a_neg", [P, EC, NS])
        d_skip = sb("d_skip", [P, EC])
        wv0 = sb("wv0", [P, KD, VH]); bv0 = sb("bv0", [P, 1]); wt0 = sb("wt0", [P, 2, VH]); bt0 = sb("bt0", [P, 1])
        w_gl = sb("w_gl", [P, KD, NE + NLOW]); b_gl = sb("b_gl", [P, NE]); w_b = sb("w_b", [NLOW, FF])
        w_i = sb("w_i", [P, KD, FF]); w_o = sb("w_o", [P, FC, D]); prio = sb("prio", [P, NE])
        w_q = sb("w_q", [P, KD, NQ * HD]); w_k = sb("w_k", [P, KD, NKV * HD]); w_v = sb("w_v", [P, KD, NKV * HD])
        w_ao = sb("w_ao", [P, 8, D])
        cs = sb("cs", [P, 4, S])
        ln1_g = sb("ln1_g", [P, KD]); ln1_b = sb("ln1_b", [P, KD]); ln2_g = sb("ln2_g", [P, 2]); ln2_b = sb("ln2_b", [P, 2])
        w_q1 = sb("w_q1", [P, KD, E2]); w_k1 = sb("w_k1", [P, 2, E2]); w_v1 = sb("w_v1", [P, 2, E2]); w_o1 = sb("w_o1", [P, 2, D])
        b_q1 = sb("b_q1", [P, 2]); b_q1s = sb("b_q1s", [P, 2]); b_k1 = sb("b_k1", [P, 2]); b_v1 = sb("b_v1", [P, E2]); b_o1 = sb("b_o1", [P, D])
        w_g = sb("w_g", [P, 3, KD, D]); u_g = sb("u_g", [P, 3, KD, D]); b_g = sb("b_g", [P, 3, KD]); b_gh = sb("b_gh", [P, 3, KD])
        w_ho = sb("w_ho", [P, KD, D]); u_ho = sb("u_ho", [P, KD, D]); b_ho = sb("b_ho", [P, D]); in_c = sb("in_c", [P, KD])
        ident = sb("ident", [P, P]); ones = sb("ones", [P, P]); neghalf = sb("neghalf", [P, 16])

        scans = sb("scans", [P, 4 * HN, S])
        heads = sb("heads", [P, 12, S])
        outs = sb("outs", [P, 8, S])
        turns = sb("turns", [P, 8, S])

        lora_ao = scans[0:LORA, 0:4, :].rearrange("p a b -> p (a b)")
        qb = scans[0:LORA, 4:8, :].rearrange("p a b -> p (a b)")
        lora_a = scans[0:LORA, 8:11, :]
        kb, vb, obm = scans[0:LORA, 11, :], scans[0:LORA, 12, :], scans[0:LORA, 13, :]

        x0 = sb("x0", [P, T, D])
        conv = sb("conv", [P, EC, S]); zg = sb("zg", [P, EC, S]); xc = sb("xc", [P, EC, S])
        xpj = sb("xpj", [2 * NS + 1, S]); dt = sb("dt", [P, EC, S]); dtx = conv
        Bb = sb("Bb", [P, NS, S]); Cb = sb("Cb", [P, NS, S])
        dA = [scans[:, i * HN:(i + 1) * HN, :] for i in range(2)]
        hb = [scans[:, (2 + i) * HN:(3 + i) * HN, :] for i in range(2)]
        zdt = hb[0]
        udt = tz = hb[1]
        xn = xT_free = Cb[:, 0:2, :]
        xnT = Cb[:, 2:4, :]
        res = dtx[:, 0:2, :]
        x1 = sb("x1", [P, T, D])
        x2 = sb("x2", [P, T, D]); x3 = sb("x3", [P, T, D]); x4 = x2; x5 = x3
        xT = sb("xT", [P, KD, S]); cx = sb("cx", [P, T, CTX]); cxT = sb("cxT", [P, 2, S])
        sq, rscale = outs[:, 0:2, :], outs[:, 2:4, :]
        tT, vT = outs[:, 4, :], outs[:, 5, :]
        ss = sb("ss", [P, 4]); rn = sb("rn", [P, 4]); diag = sb("diag", [P, 2, T, P])
        sm = sb("sm", [P, 12, T, NE]); sc2 = sb("sc2", [P, 8, T])
        low = sb("low", [P, 2, T, NLOW])
        lowT, wrow = heads[0:NLOW, 0:2, :], heads[:, 2:4, :]
        r1 = heads[:, 4:8, :].rearrange("p (j a) s -> p j a s", j=2)
        r2 = heads[:, 8:12, :].rearrange("p (j a) s -> p j a s", j=2)
        hT = turns
        rot = turns[:, 0:4, :].rearrange("p (j a) s -> p j a s", j=2)
        rot2 = turns[:, 4:8, :].rearrange("p (j a) s -> p j a s", j=2)
        ro = outs[:, 4:8, :].rearrange("p (j a) s -> p j a s", j=2)
        kT = heads[:, 0:4, :]
        qT = heads[:, 4:12, :].rearrange("p (g j) s -> p g j s", g=NKV)
        v1 = sb("v1", [P, T, NKV, HD + 1])
        nmax = sb("nmax", [P, 4, T]); 
        pe_ = turns[:, 0:4, :].rearrange("p (j a) s -> p j a s", j=2)
        pT = turns[:, 4:8, :].rearrange("p (j a) s -> p j a s", j=2)
        rs = sb("rs", [P, 2, T, 2])
        ob = outs[:, :, :].rearrange("p (t a) (h d) -> p t (a h) d", t=T, d=HD)
        oT = heads[:, 4:12, :]
        x1n, x4b, x2n = turns[:, 2:4, :], turns[:, 6:8, :], outs[:, 6:8, 0:CTX]
        x2T = cxT
        q1, k1, v1x, cT = outs[:, 0:2, :], outs[:, 2:4, :], outs[:, 4:6, :], outs[:, 6:8, :]
        sums = sb("sums", [P, T]); rsum = sb("rsum", [P, T])
        tg = heads[:, 0:6, :].rearrange("p (g k) s -> p g k s", g=3)
        ug = heads[:, 6:10, :].rearrange("p (g k) s -> p g k s", g=2)
        xw = heads[:, 10:12, :].rearrange("p a s -> p (a s)")
        state = sb("state", [P, KD, S])
        cu = x1[:, :, :].rearrange("p a s -> p (a s)")
        XS = Bb[:, :, :].rearrange("p (b t) s -> p b (t s)", t=T)
        XW = Cb[:, :, :].rearrange("p (b t) s -> p b (t s)", t=T)
        ln_st = sb("ln_st", [P, T, 6]); ln_mv = {}; ln_var = {}; ln_rs = {}
        for tag in ("a", "a1", "b1", "f1", "t1", "c", "c2", "c1"):
            ln_mv[tag] = sb(f"mv_{tag}", [P, T, 2]); ln_var[tag] = sb(f"var_{tag}", [P, T]); ln_rs[tag] = sb(f"rstd_{tag}", [P, T])
        e_st = sb("e_st", [P, NB * T, 6]); e_mv = sb("e_mv", [P, NB * T, 2]); e_var = sb("e_var", [P, NB * T]); e_rs = sb("e_rs", [P, NB * T])

        def stats(dve, own, src, tag):
            for t in range(T):
                own.did(dve.bn_stats(ln_st[:, t, :], src[:, t, :]))
            own.wait()
            for t in range(T):
                own.did(dve.bn_aggr(ln_mv[tag][:, t, :], ln_st[:, t, :]))
            own.wait()
            dve.tensor_scalar(ln_var[tag][:, :], ln_mv[tag][:, :, 1], EPS, None, ALU.add).then_inc(s[tag + "_var"], 1)

        def rstd(pool, tag):
            pool.wait_ge(s[tag + "_var"], 1)
            pool.tensor_tensor(ln_rs[tag][:, :], ln_var[tag][:, :], neghalf[:, 0:T], ALU.pow).then_inc(s[tag + "_rstd"], 1)

        def normal(dve, src, dst, tag):
            dve.wait_ge(s[tag + "_rstd"], 1)
            for t in range(T):
                dve.tensor_scalar(dst[:, t, :], src[:, t, :], ln_mv[tag][:, t, 0:1], ln_rs[tag][:, t:t + 1],
                                  ALU.subtract, ALU.mult).then_inc(s[tag + "_norm"], 1)

        def turn(pe, src, bk, sem):
            for k in range(KD):
                for t in range(T):
                    last = pe.transpose(bk[:, k * S + t * P:k * S + t * P + P], src[:, t, k * P:(k + 1) * P], ident[:, :])
            last.then_inc(s[sem], 1)

        def mm(pe, o, pairs, start=True):
            n = len(pairs)
            for i, (l, r) in enumerate(pairs):
                last = pe.matmul(o, l, r, start=(start and i == 0), stop=(i == n - 1), skip_group_check=True)
            return last

        def flat(ap):
            return ap.rearrange("p a b -> p (a b)")

        PA = bank[0:3]

        def a_sp(sp, b):
            sp.dma_start(x0[:, :, :], A["x"][bass.ds(b, 1), :, :].rearrange("a (t p) d -> p (a t) d", p=P)).then_inc(s["a_x"], 16)
            sp.wait_ge(s["a_xpj"], 1)
            sp.dma_start(scratch, xpj[:, :]).then_inc(s["a_store"], 16)
            sp.wait_ge(s["a_store"], 16)
            sp.dma_start(Bb[:, :, :], scratch[0:NS, :].partition_broadcast(P)).then_inc(s["a_B"], 16)
            sp.dma_start(Cb[:, :, :], scratch[NS:2 * NS, :].partition_broadcast(P)).then_inc(s["a_C"], 16)
            yield

        def a_dve(dve, own):
            dve.wait_ge(s["a_x"], 16)
            stats(dve, own, x0, "a")
            normal(dve, x0, xn, "a")
            yield
            for j in range(2):
                dve.wait_ge(s["a_tap"], 2 * j + 2)
                for k in range(TAPS - 1):
                    d = TAPS - 1 - k
                    for i in range(2):
                        e = 2 * j + i
                        ins = dve.scalar_tensor_tensor(conv[:, e, d:S], PA[1 + j][:, i * S:i * S + S - d], conv_wh[:, e, k:k + 1],
                                                       conv[:, e, d:S], ALU.mult, ALU.add)
                        if k == TAPS - 2:
                            ins.then_inc(s["a_conv"], 1)
                        else:
                            own.did(ins)
                    if k < TAPS - 2:
                        own.wait()
                if j == 0:
                    yield
            for j in range(2):
                dve.wait_ge(s["a_z_tanh"], j + 1)
                dve.scalar_tensor_tensor(flat(zg[:, 2 * j:2 * j + 2, :]), flat(tz[:, 2 * j:2 * j + 2, :]), 1.0, [PA[0], PA[1]][j][:, :],
                                         ALU.add, ALU.mult).then_inc(s["a_silu_z"], 1)
            dve.wait_ge(s["a_conv"], EC)
            for e in range(EC):
                dve.wait_ge(s["a_xc_tanh"], e + 1)
                dve.scalar_tensor_tensor(xc[:, e, :], xc[:, e, :], 1.0, conv[:, e, :], ALU.add, ALU.mult).then_inc(s["a_xc"], 1)
            yield
            dve.wait_ge(s["a_u"], 1)
            dve.wait_ge(s["a_xc"], EC)
            own.link(dve.tensor_scalar(flat(conv[:, :, :]), flat(udt[:, :, :]), 1.0, 1.0, ALU.add, ALU.subtract))
            own.link(dve.tensor_tensor(flat(conv[:, :, :]), flat(udt[:, :, :]), flat(conv[:, :, :]), ALU.subtract))
            dve.wait_ge(s["a_ln"], 1)
            own.link(dve.tensor_tensor(flat(conv[:, :, :]), flat(conv[:, :, :]), flat(dt[:, :, :]), ALU.add))
            dve.scalar_tensor_tensor(flat(dt[:, :, :]), flat(zdt[:, :, :]), 0.0, flat(conv[:, :, :]), ALU.max, ALU.add).then_inc(s["a_dt"], 1)
            dve.wait_ge(s["a_dt"], 1)
            dve.tensor_tensor(flat(dtx[:, :, :]), flat(dt[:, :, :]), flat(xc[:, :, :]), ALU.mult).then_inc(s["a_dtx"], 1)
            yield
            for u, (c, h) in enumerate(UNITS):
                H = hb[u % 2]
                dve.wait_ge(s["a_dA"], u + 1)
                dve.wait_ge(s["a_dBx"], u + 1)
                dve.tensor_tensor_scan(flat(H[:, :, :]), flat(dA[u % 2][:, :, :]), flat(H[:, :, :]), 0.0, ALU.mult, ALU.add).then_inc(s["a_scan"], 1)
                dve.wait_ge(s["a_scan"], u + 1)
                if u == 0:
                    dve.wait_ge(s["a_C"], 16)
                dve.tensor_tensor(flat(H[:, :, :]), flat(H[:, :, :]), flat(Cb[:, h * HN:(h + 1) * HN, :]), ALU.mult).then_inc(s["a_hC"], 1)
                if h == 1 and c >= 1:
                    skip(dve, own, c - 1)
                yield
            skip(dve, own, EC - 1)
            yield
            dve.wait_ge(s["a_out_ps"], 1)
            own.link(dve.scalar_tensor_tensor(flat(res[:, :, :]), flat(x0[:, :, :]), 2.0, PA[1][:, :], ALU.mult, ALU.add))
            stats(dve, own, res, "a1")
            normal(dve, res, x1, "a1")
            yield

        def skip(dve, own, c):
            dve.wait_ge(s["a_y_ps"], UH * (c + 1))
            own.link(dve.scalar_tensor_tensor(xc[:, c, :], xc[:, c, :], d_skip[:, c:c + 1], [PA[0], PA[2]][c % 2][:, 0:S], ALU.mult, ALU.add))
            dve.tensor_tensor(zg[:, c, :], xc[:, c, :], zg[:, c, :], ALU.mult).then_inc(s["a_gated"], 1)

        def a_pool(pool, own):
            rstd(pool, "a")
            yield
            pool.wait_ge(s["a_dtx"], 1)
            pool.wait_ge(s["a_B"], 16)
            for u, (c, h) in enumerate(UNITS):
                if u >= 2:
                    pool.wait_ge(s["a_y_ps"], u - 1)
                pool.tensor_tensor(hb[u % 2][:, :, :], dtx[:, c:c + 1, :].to_broadcast([P, HN, S]), Bb[:, h * HN:(h + 1) * HN, :],
                                   ALU.mult).then_inc(s["a_dBx"], 1)
                yield
            rstd(pool, "a1")
            yield

        def a_act(act, own):
            act.wait_ge(s["a_xnT_ps"], 1)
            for k in range(KD):
                act.activation(xnT[:, k, :], PA[0][:, k * S:(k + 1) * S], ACT.Identity, bias=ln_b[:, k:k + 1],
                               scale=ln_g[:, k:k + 1]).then_inc(s["a_xnT"], 1)
            yield
            for j in range(2):
                act.wait_ge(s["a_in_ps"], j + 1)
                for i in range(2):
                    e = 2 * j + i
                    act.activation(conv[:, e, :], PA[1 + j][:, i * S:(i + 1) * S], ACT.Identity, bias=conv_bh[:, e:e + 1],
                                   scale=conv_wh[:, e, TAPS - 1:TAPS]).then_inc(s["a_tap"], 1)
            yield
            for j in range(2):
                act.wait_ge(s["a_in_ps"], j + 3)
                act.activation(flat(tz[:, 2 * j:2 * j + 2, :]), [PA[0], PA[1]][j][:, :], ACT.Tanh).then_inc(s["a_z_tanh"], 1)
            for e in range(EC):
                act.wait_ge(s["a_conv"], e + 1)
                act.activation(xc[:, e, :], conv[:, e, :], ACT.Tanh).then_inc(s["a_xc_tanh"], 1)
            yield
            act.wait_ge(s["a_xpj_ps"], 1)
            act.activation(xpj[:, :], PA[2][0:2 * NS + 1, 0:S], ACT.Copy).then_inc(s["a_xpj"], 1)
            act.wait_ge(s["a_dtl_ps"], 1)
            for c in range(EC):
                own.did(act.activation(zdt[:, c, :], PA[0][:, 0:S], ACT.Identity, bias=b_dt[:, c:c + 1], scale=w_dt[:, c:c + 1]))
            own.wait()
            own.link(act.activation(flat(udt[:, :, :]), flat(zdt[:, :, :]), ACT.Abs))
            act.activation(flat(udt[:, :, :]), flat(udt[:, :, :]), ACT.Exp, scale=-1.0).then_inc(s["a_u"], 1)
            act.wait_ge(s["a_u"], 1)
            act.activation(flat(dt[:, :, :]), flat(udt[:, :, :]), ACT.Ln, bias=1.0).then_inc(s["a_ln"], 1)
            yield
            act.wait_ge(s["a_dt"], 1)
            for u, (c, h) in enumerate(UNITS):
                if u >= 2:
                    act.wait_ge(s["a_scan"], u - 1)
                for j in range(HN):
                    n = h * HN + j
                    ins = act.activation(dA[u % 2][:, j, 1:S], dt[:, c, 1:S], ACT.Exp, scale=a_neg[:, c, n:n + 1])
                ins.then_inc(s["a_dA"], 1)
                yield

        def a_pe(pe):
            pe.wait_ge(s["a_norm"], T)
            turn(pe, xn, PA[0], "a_xnT_ps")
            pe.wait_ge(s["a_xnT"], KD)
            yield
            for j, bk in enumerate([PA[1], PA[2], PA[0], PA[1]]):
                if j == 3:
                    pe.wait_ge(s["a_conv"], 2)
                for i in range(2):
                    e = 2 * j + i
                    last = mm(pe, bk[:, i * S:(i + 1) * S], [(w_in[:, k, e * P:(e + 1) * P], xnT[:, k, :]) for k in range(KD)])
                last.then_inc(s["a_in_ps"], 1)
                if j == 1:
                    yield
            yield
            pe.wait_ge(s["a_xc"], EC)
            mm(pe, PA[2][0:2 * NS + 1, 0:S], [(w_xp[:, c, :], xc[:, c, :]) for c in range(EC)]).then_inc(s["a_xpj_ps"], 1)
            pe.wait_ge(s["a_xpj"], 1)
            pe.wait_ge(s["a_silu_z"], 1)
            mm(pe, PA[0][:, 0:S], [(ones[2 * NS:2 * NS + 1, :], xpj[2 * NS:2 * NS + 1, :])]).then_inc(s["a_dtl_ps"], 1)
            yield
            pe.wait_ge(s["a_u"], 1)
            for u, (c, h) in enumerate(UNITS):
                pe.wait_ge(s["a_hC"], u + 1)
                if h == 0 and c >= 2:
                    pe.wait_ge(s["a_gated"], c - 1)
                for j in range(HN):
                    last = pe.matmul([PA[0], PA[2]][c % 2][:, 0:S], ident[:, :], hb[u % 2][:, j, :], start=(h == 0 and j == 0),
                                     stop=(h == UH - 1 and j == HN - 1))
                last.then_inc(s["a_y_ps"], 1)
                yield
            pe.wait_ge(s["a_gated"], EC)
            pe.wait_ge(s["a_silu_z"], 2)
            for t in range(T):
                last = mm(pe, PA[1][:, t * D:(t + 1) * D], [(zg[:, c, t * P:(t + 1) * P], w_out[:, c, :]) for c in range(EC)])
            last.then_inc(s["a_out_ps"], 1)
            yield

        def r_sp(sp, b):
            sp.dma_start(cx[:, :, :], A["ctx"][bass.ds(b, 1), :, :].rearrange("a (t p) d -> p (a t) d", p=P)).then_inc(s["b_ctx"], 16)
            yield
            sp.wait_ge(s["t_kro"], 2)
            for g in range(NKV):
                for half in range(2):
                    for i in range(2):
                        r = 64 * i + HH * half
                        sp.dma_start(kT[r:r + HH, g, :], ro[HH * g:HH * (g + 1), 0, half, :]).then_inc(s["t_kT"], 16)
            for g in range(NKV):
                sp.wait_ge(s["t_ro"], 2 * g + 2)
                for j in range(GH):
                    for half in range(2):
                        r = 64 * (j % 2) + HH * half
                        sp.dma_start(qT[r:r + HH, g, j // 2, :], ro[HH * j:HH * (j + 1), (g + 1) % 2, half, :]).then_inc(s[f"t_qT{g}"], 16)
            yield

        def b_pe(pe):
            b3, b4, b5, b6, b7 = bank[3:8]
            pe.wait_ge(s["b_ctx"], 16)
            for t in range(T):
                pe.transpose(b3[:, t * P:(t + 1) * P], cx[:, t, 0:P], ident[:, :])
            for t in range(T):
                last = pe.transpose(b3[0:CTX2, S + t * P:S + (t + 1) * P], cx[:, t, P:CTX], ident[:, :])
            last.then_inc(s["b_cxT_ps"], 1)
            pe.wait_ge(s["a1_norm"], T)
            turn(pe, x1, b5, "b_xT_ps")
            pe.wait_ge(s["b_cxT"], 2)
            mm(pe, b4[:, 0:S], [(wt0[:, 0, :], cxT[:, 0, :]), (wt0[0:CTX2, 1, :], cxT[0:CTX2, 1, :])]).then_inc(s["b_tT_ps"], 1)
            pe.wait_ge(s["b_xT"], 1)
            mm(pe, b6[:, 0:S], [(wv0[:, k, :], xT[:, k, :]) for k in range(KD)]).then_inc(s["b_vT_ps"], 1)
            pe.wait_ge(s["b_tT"], 2)
            pe.wait_ge(s["b_vT"], 2)
            for t in range(T):
                mm(pe, b4[:, t * S:(t + 1) * S], [(vT[:, t * P:(t + 1) * P], tT[:, :])]).then_inc(s["b_dots_ps"], 1)
            for i in range(2):
                for t in range(T):
                    last = pe.matmul(b7[:, 2 * i + t:2 * i + t + 1], sq[:, i, t * P:(t + 1) * P], ones[:, 0:1], start=True, stop=True)
            last.then_inc(s["b_ss_ps"], 1)
            pe.wait_ge(s["b_diag"], T)
            mm(pe, b7[:, 0:S], [(ones[:, :], diag[:, 0, :, :].rearrange("p a b -> p (a b)"))]).then_inc(s["b_row_ps"], 1)
            yield

        def b_act(act, own):
            b3, b4, b5, b6, b7 = bank[3:8]
            act.wait_ge(s["b_cxT_ps"], 1)
            act.activation(cxT[:, 0, :], b3[:, 0:S], ACT.Copy).then_inc(s["b_cxT"], 1)
            act.activation(cxT[0:CTX2, 1, :], b3[0:CTX2, S:2 * S], ACT.Copy).then_inc(s["b_cxT"], 1)
            act.wait_ge(s["b_xT_ps"], 1)
            act.activation(flat(xT[:, :, :]), b5[:, :], ACT.Copy).then_inc(s["b_xT"], 1)
            act.wait_ge(s["b_tT_ps"], 1)
            act.activation(tT[:, :], b4[:, 0:S], ACT.Identity, bias=bt0[:, :]).then_inc(s["b_tT"], 1)
            act.activation(sq[:, 1, :], b4[:, 0:S], ACT.Square, bias=bt0[:, :]).then_inc(s["b_tT"], 1)
            act.wait_ge(s["b_vT_ps"], 1)
            act.activation(vT[:, :], b6[:, 0:S], ACT.Identity, bias=bv0[:, :]).then_inc(s["b_vT"], 1)
            act.activation(sq[:, 0, :], b6[:, 0:S], ACT.Square, bias=bv0[:, :]).then_inc(s["b_vT"], 1)
            yield

        def b_dve(dve, own):
            b3, b4, b5, b6, b7 = bank[3:8]
            dve.wait_ge(s["b_ss_ps"], 1)
            dve.tensor_scalar(ss[:, :], b7[:, 0:4], 1e-38, None, ALU.max).then_inc(s["b_ss"], 1)
            dve.wait_ge(s["b_rn"], 1)
            for t in range(T):
                dve.tensor_scalar(diag[:, 0, t, :], ident[:, :], rn[:, 2 + t:3 + t], None, ALU.mult).then_inc(s["b_diag"], 1)
            dve.wait_ge(s["b_row_ps"], 1)
            for t in range(T):
                own.did(dve.tensor_scalar(rscale[:, t, :], b7[:, 0:S], rn[:, t:t + 1], BIG, ALU.mult, ALU.min))
            own.wait()
            dve.wait_ge(s["b_dots_ps"], T)
            own.link(dve.tensor_tensor(flat(rscale[:, :, :]), flat(rscale[:, :, :]), b4[:, :], ALU.mult))
            own.link(dve.tensor_tensor(flat(x2[:, :, :]), flat(rscale[:, :, :]), flat(x1[:, :, :]), ALU.add))
            stats(dve, own, x2, "b1")
            normal(dve, x2, x2, "b1")
            yield

        def b_pool(pool, own):
            pool.wait_ge(s["b_ss"], 1)
            pool.tensor_tensor(rn[:, :], ss[:, :], neghalf[:, 0:4], ALU.pow).then_inc(s["b_rn"], 1)
            rstd(pool, "b1")
            yield

        FB = bank[5:8]

        def f_pe(pe):
            b3, b4, b5, b6, b7 = bank[3:8]
            pe.wait_ge(s["b1_norm"], T)
            turn(pe, x2, b5, "f_xT_ps")
            pe.wait_ge(s["f_xT"], 1)
            for t in range(T):
                last = mm(pe, b3[:, t * 20:t * 20 + 20], [(xT[:, k, t * P:(t + 1) * P], w_gl[:, k, :]) for k in range(KD)])
            last.then_inc(s["f_gl_ps"], 1)
            pe.wait_ge(s["f_low"], 2)
            for i in range(2):
                for t in range(T):
                    last = pe.transpose(b3[0:NLOW, i * S + t * P:i * S + (t + 1) * P], low[:, i, t, :], ident[:, :])
            last.then_inc(s["f_lowT_ps"], 1)
            pe.wait_ge(s["f_wdiag"], 4)
            mm(pe, b4[:, :], [(ones[:, :], diag[:, :, :, :].rearrange("p a b c -> p (a b c)"))]).then_inc(s["f_w_ps"], 1)
            pe.wait_ge(s["f_lowT"], 1)
            yield

            def first(j):
                bk = FB[j % 3]
                if j >= 3:
                    pe.wait_ge(s["f_r"], 2 * (j - 3) + 2)
                if j == 0:
                    pass
                n = 0
                for i in range(2):
                    f = 2 * j + i
                    prs = [(w_i[:, k, f * P:(f + 1) * P], xT[:, k, :]) for k in range(KD)] + [(w_b[:, f * P:(f + 1) * P], lowT[:, 0, :])]
                    for l, r in prs:
                        last = pe.matmul(bk[:, i * S:(i + 1) * S], l, r, start=(n == 0), stop=False, skip_group_check=True)
                        n += 1
                last.then_inc(s["f_z1_ps"], 1)

            def second(j):
                bk = FB[j % 3]
                pe.wait_ge(s["f_r"], 2 * j + 1)
                for i in range(2):
                    f = 2 * j + i
                    last = pe.matmul(bk[:, i * S:(i + 1) * S], w_b[:, f * P:(f + 1) * P], lowT[:, 1, :], start=False, stop=True,
                                     skip_group_check=True)
                last.then_inc(s["f_z2_ps"], 1)

            for j in range(FC // 2 + 1):
                if j < FC // 2:
                    first(j)
                if j >= 1:
                    second(j - 1)
                yield
            for t in range(T):
                for f in range(FC):
                    if t == 0 and f % 2 == 0:
                        pe.wait_ge(s["f_h"], f // 2 + 1)
                    last = pe.matmul(b3[:, t * D:(t + 1) * D], hT[:, f, t * P:(t + 1) * P], w_o[:, f, :], start=(f == 0), stop=(f == FC - 1))
            last.then_inc(s["f_out_ps"], 1)
            yield

        def f_act(act, own):
            b3, b4, b5, b6, b7 = bank[3:8]
            act.wait_ge(s["f_xT_ps"], 1)
            act.activation(flat(xT[:, :, :]), b5[:, :], ACT.Copy).then_inc(s["f_xT"], 1)
            act.wait_ge(s["f_exp_in"], 1)
            act.activation(sm[:, 1, :, :], sm[:, 1, :, :], ACT.Exp).then_inc(s["f_exp"], 1)
            act.wait_ge(s["f_lowT_ps"], 1)
            act.activation(flat(lowT[:, :, :]), b3[0:NLOW, :], ACT.Copy).then_inc(s["f_lowT"], 1)
            act.wait_ge(s["f_w_ps"], 1)
            act.activation(flat(wrow[:, :, :]), b4[:, :], ACT.Copy).then_inc(s["f_wrow"], 1)
            yield

        def f_dve(dve, own):
            b3, b4, b5, b6, b7 = bank[3:8]
            dve.wait_ge(s["f_gl_ps"], 1)
            gl = b3[:, 0:2 * 20].rearrange("p (t n) -> p t n", t=T)
            per = [P, T, NE]

            def wide(col):
                return sc2[:, col, :].unsqueeze(2).to_broadcast(per)

            def tile_of(x):
                return x.unsqueeze(1).to_broadcast(per)

            own.did(dve.tensor_copy(low[:, 1, :, :], gl[:, :, NE:]))
            own.link(dve.tensor_tensor(sm[:, 0, :, :], gl[:, :, 0:NE], tile_of(b_gl[:, :]), ALU.add))
            own.link(dve.tensor_reduce(sc2[:, 0, :], sm[:, 0, :, :], AX, ALU.max))
            dve.tensor_tensor(sm[:, 1, :, :], sm[:, 0, :, :], wide(0), ALU.subtract).then_inc(s["f_exp_in"], 1)
            dve.wait_ge(s["f_exp"], 1)
            own.link(dve.tensor_reduce(sc2[:, 1, :], sm[:, 1, :, :], AX, ALU.add))
            own.link(dve.reciprocal(sc2[:, 2, :], sc2[:, 1, :]))
            own.link(dve.tensor_tensor(sm[:, 2, :, :], sm[:, 1, :, :], wide(2), ALU.mult))
            for i, (score, hit, rank, one) in enumerate([(2, 3, 4, 5), (6, 7, 8, 9)]):
                top, best = 3 + 2 * i, 4 + 2 * i
                own.link(dve.tensor_reduce(sc2[:, top, :], sm[:, score, :, :], AX, ALU.max))
                own.link(dve.tensor_tensor(sm[:, hit, :, :], sm[:, score, :, :], wide(top), ALU.is_equal))
                own.link(dve.tensor_tensor(sm[:, rank, :, :], sm[:, hit, :, :], tile_of(prio[:, :]), ALU.mult))
                own.link(dve.tensor_reduce(sc2[:, best, :], sm[:, rank, :, :], AX, ALU.max))
                own.link(dve.tensor_tensor(sm[:, one, :, :], sm[:, rank, :, :], wide(best), ALU.is_equal))
                if i == 0:
                    own.link(dve.scalar_tensor_tensor(sm[:, 6, :, :], sm[:, 5, :, :], -2.0, sm[:, 2, :, :], ALU.mult, ALU.add))
            own.link(dve.tensor_tensor(sm[:, 10, :, :], sm[:, 9, :, :], sm[:, 5, :, :], ALU.subtract))
            for t in range(T):
                for i, one in enumerate([5, 10]):
                    own_or = dve.tensor_tensor(low[:, i, t, :].rearrange("p (e r) -> p e r", e=NE),
                                               low[:, 1, t, :].rearrange("p (e r) -> p e r", e=NE),
                                               sm[:, one, t, :].unsqueeze(2).to_broadcast([P, NE, RK]), ALU.mult)
                    if t == T - 1:
                        own_or.then_inc(s["f_low"], 1)
                    else:
                        own.did(own_or)
            for i in range(2):
                for t in range(T):
                    dve.tensor_scalar(diag[:, i, t, :], ident[:, :], sc2[:, 3 + 2 * i, t:t + 1], None, ALU.mult).then_inc(s["f_wdiag"], 1)
            yield
            dve.wait_ge(s["f_wrow"], 1)
            for j in range(FC // 2):
                for i, (ps, dst) in enumerate([("f_z1_ps", r1), ("f_z2_ps", r2)]):
                    dve.wait_ge(s[ps], j + 1)
                    if j >= 2:
                        dve.wait_ge(s["f_h"], j - 1)
                    dve.scalar_tensor_tensor(dst[:, j % 2, :, :], FB[j % 3][:, :].rearrange("p (a b) -> p a b", a=2), 0.0,
                                             wrow[:, i:i + 1, :].to_broadcast([P, 2, S]), ALU.max, ALU.mult).then_inc(s["f_r"], 1)
                yield
            dve.wait_ge(s["f_out_ps"], 1)
            own.link(dve.tensor_tensor(flat(x3[:, :, :]), b3[:, :], flat(x2[:, :, :]), ALU.add))
            stats(dve, own, x3, "f1")
            normal(dve, x3, x3, "f1")
            yield

        def f_pool(pool, own):
            yield
            for j in range(FC // 2):
                pool.wait_ge(s["f_r"], 2 * j + 2)
                pool.tensor_tensor(flat(hT[:, 2 * j:2 * j + 2, :]), r1[:, j % 2, :, :].rearrange("p a b -> p (a b)"),
                                   r2[:, j % 2, :, :].rearrange("p a b -> p (a b)"), ALU.add).then_inc(s["f_h"], 1)
                yield
            rstd(pool, "f1")
            yield

        SB, TB, OB = [bank[3], bank[4]], [bank[5], bank[6]], bank[7]
        NH = NQ

        def t_pe(pe):
            b3, b4, b5, b6, b7 = bank[3:8]
            pe.wait_ge(s["f1_norm"], T)
            turn(pe, x3, b5, "t_xT_ps")
            pe.wait_ge(s["t_xT"], 1)
            for i in range(2):
                last = mm(pe, b3[:, i * S:(i + 1) * S], [(w_k[:, k, i * P:(i + 1) * P], xT[:, k, :]) for k in range(KD)])
            last.then_inc(s["t_k_ps"], 1)
            for t in range(T):
                last = mm(pe, b4[:, t * S:(t + 1) * S], [(xT[:, k, t * P:(t + 1) * P], w_v[:, k, :]) for k in range(KD)])
            last.then_inc(s["t_v_ps"], 1)
            for g in range(NKV):
                bk = [b5, b6][g % 2]
                if g >= 2:
                    pe.wait_ge(s["t_rot"], 2 * (g - 1) + 2)
                for i in range(2):
                    f = 2 * g + i
                    last = mm(pe, bk[:, i * S:(i + 1) * S], [(w_q[:, k, f * P:(f + 1) * P], xT[:, k, :]) for k in range(KD)])
                last.then_inc(s["t_q_ps"], 1)
            yield
            pe.wait_ge(s["t_kT"], 16 * 4 * NKV)
            pe.wait_ge(s["t_rot"], 2 * NKV + 2)
            pe.wait_ge(s["t_v"], 1)

            def scores(h):
                g, pair, r = h // GH, (h % GH) // 2, 64 * (h % 2)
                if h % GH == 0:
                    pe.wait_ge(s[f"t_qT{g}"], 16 * 8)
                if h >= 2:
                    pe.wait_ge(s["t_p"], 2 * (h - 1))
                for t in range(T):
                    last = pe.matmul(SB[h % 2][:, t * S:(t + 1) * S], qT[r:r + HD, g, pair, t * P:(t + 1) * P], kT[r:r + HD, g, :],
                                     start=True, stop=True)
                last.then_inc(s["t_s_ps"], 1)

            def turned(h):
                pe.wait_ge(s["t_p"], 2 * h + 2)
                if h >= 2:
                    pe.wait_ge(s["t_pT"], h - 1)
                for k in range(2):
                    for t in range(T):
                        last = pe.transpose(TB[h % 2][:, k * S + t * P:k * S + (t + 1) * P], pe_[:, h % 2, t, k * P:(k + 1) * P], ident[:, :])
                last.then_inc(s["t_pT_ps"], 1)

            def values(h):
                g = h // GH
                pe.wait_ge(s["t_pT"], h + 1)
                if h >= 2 and h % 2 == 0:
                    pe.wait_ge(s["t_o"], h // 2)
                for t in range(T):
                    o = (t * 2 + h % 2) * (HD + 1)
                    for k in range(2):
                        last = pe.matmul(OB[:, o:o + HD + 1], pT[:, h % 2, k, t * P:(t + 1) * P], v1[:, k, g, :], start=(k == 0), stop=(k == 1))
                last.then_inc(s["t_o_ps"], 1)

            for i in range(NH + 3):
                if i < NH:
                    scores(i)
                if 1 <= i <= NH:
                    turned(i - 1)
                if 3 <= i:
                    values(i - 3)
                yield
            pe.wait_ge(s["t_o"], NH // 2)
            for c in range(8):
                bk = [b3, b4, b5, b6][(c // 2) % 4]
                for t in range(T):
                    last = pe.transpose(bk[:, (c % 2) * S + t * P:(c % 2) * S + (t + 1) * P],
                                        ob[:, t, 2 * c:2 * c + 2, :].rearrange("p a b -> p (a b)"), ident[:, :])
                if c % 2 == 1:
                    last.then_inc(s["t_oT_ps"], 1)
            pe.wait_ge(s["t_oT"], 4)
            for t in range(T):
                last = mm(pe, b7[:, t * D:(t + 1) * D], [(oT[:, c, t * P:(t + 1) * P], w_ao[:, c, :]) for c in range(8)])
            last.then_inc(s["t_out_ps"], 1)
            yield

        def t_act(act, own):
            b3, b4, b5, b6, b7 = bank[3:8]
            act.wait_ge(s["t_xT_ps"], 1)
            act.activation(flat(xT[:, :, :]), b5[:, :], ACT.Copy).then_inc(s["t_xT"], 1)
            act.wait_ge(s["t_v_ps"], 1)
            act.activation(v1[:, :, :, 0:HD], b4[:, :].rearrange("p (t g d) -> p t g d", t=T, g=NKV), ACT.Copy).then_inc(s["t_v"], 1)
            yield
            act.wait_ge(s["t_ro"], 2 * NKV)
            for h in range(NH):
                act.wait_ge(s["t_max"], h + 1)
                if h >= 2:
                    act.wait_ge(s["t_pT_ps"], h - 1)
                for t in range(T):
                    act.activation(pe_[:, h % 2, t, :], SB[h % 2][:, t * S:(t + 1) * S], ACT.Exp, bias=nmax[:, h % 4, t:t + 1]).then_inc(s["t_p"], 1)
                yield
            for j in range(4):
                act.wait_ge(s["t_oT_ps"], j + 1)
                act.activation(flat(oT[:, 2 * j:2 * j + 2, :]), [b3, b4, b5, b6][j][:, :], ACT.Copy).then_inc(s["t_oT"], 1)
            yield

        def t_dve(dve, own):
            b3, b4, b5, b6, b7 = bank[3:8]

            def rope(src, table, i, n):
                pair = src[:, :].rearrange("p (a b) -> p a b", a=2)
                if n >= 2:
                    dve.wait_ge(s["t_kro"], 2)
                    if n >= 3:
                        dve.wait_ge(s["t_ro"], 2 * (n - 2))
                dve.tensor_tensor(rot[:, i, :, :], pair, cs[:, table:table + 2, :], ALU.mult).then_inc(s["t_rot"], 1)
                for half in range(2):
                    last = dve.tensor_tensor(rot2[:, i, half, :], pair[:, half, :], cs[:, table + 1 - half, :], ALU.mult)
                last.then_inc(s["t_rot"], 1)

            dve.wait_ge(s["t_k_ps"], 1)
            rope(b3, 0, 0, 0)
            for g in range(NKV):
                dve.wait_ge(s["t_q_ps"], g + 1)
                rope([b5, b6][g % 2], 2, (g + 1) % 2, g + 1)
            yield

            dve.wait_ge(s["t_ro"], 2 * NKV)

            def pT_out(h):
                dve.wait_ge(s["t_pT_ps"], h + 1)
                if h >= 2:
                    dve.wait_ge(s["t_o_ps"], h - 1)
                dve.tensor_copy(pT[:, h % 2, :, :].rearrange("p a b -> p (a b)"), TB[h % 2][:, :]).then_inc(s["t_pT"], 1)

            def weigh(p):
                if p == 0:
                    for g in range(NKV):
                        dve.wait_ge(s[f"t_qT{g}"], 16 * 8)
                dve.wait_ge(s["t_o_ps"], 2 * p + 2)
                if p >= 2:
                    dve.wait_ge(s["t_o"], p - 1)
                o = OB[:, 0:4 * (HD + 1)].rearrange("p (t h d) -> p t h d", t=T, h=2)
                own.link(dve.reciprocal(rs[:, p % 2, :, :], o[:, :, :, HD]))
                dve.tensor_tensor(ob[:, :, 2 * p:2 * p + 2, :], o[:, :, :, 0:HD],
                                  rs[:, p % 2, :, :].unsqueeze(3).to_broadcast([P, T, 2, HD]), ALU.mult).then_inc(s["t_o"], 1)

            for i in range(NH + 3):
                if i < NH:
                    dve.wait_ge(s["t_s_ps"], i + 1)
                    if i >= 4:
                        dve.wait_ge(s["t_p"], 2 * (i - 3))
                    dve.tensor_reduce(nmax[:, i % 4, :], SB[i % 2][:, :].rearrange("p (t k) -> p t k", t=T), AX, ALU.max,
                                      negate=True).then_inc(s["t_max"], 1)
                if 1 <= i <= NH:
                    pT_out(i - 1)
                if i >= 4 and i % 2 == 0:
                    weigh((i - 4) // 2)
                yield
            dve.wait_ge(s["t_out_ps"], 1)
            own.link(dve.tensor_tensor(flat(x4[:, :, :]), b7[:, :], flat(x3[:, :, :]), ALU.add))
            stats(dve, own, x4, "t1")
            normal(dve, x4, x4, "t1")
            yield

        def t_pool(pool, own):
            for n in range(NKV + 1):
                i = n % 2
                pool.wait_ge(s["t_rot"], 2 * n + 2)
                if n >= 2:
                    pool.wait_ge(s["t_kT"], 16 * 4 * NKV)
                    if n >= 3:
                        pool.wait_ge(s[f"t_qT{n - 3}"], 16 * 8)
                sem = s["t_kro"] if n == 0 else s["t_ro"]
                pool.tensor_tensor(ro[:, i, 0, :], rot[:, i, 0, :], rot[:, i, 1, :], ALU.subtract).then_inc(sem, 1)
                pool.tensor_tensor(ro[:, i, 1, :], rot2[:, i, 0, :], rot2[:, i, 1, :], ALU.add).then_inc(sem, 1)
            yield
            rstd(pool, "t1")
            yield

        def c_pe(pe):
            b3, b4, b5, b6, b7 = bank[3:8]
            pe.wait_ge(s["c2_norm"], T)
            for t in range(T):
                pe.transpose(b6[:, t * P:(t + 1) * P], x2n[:, t, 0:P], ident[:, :])
            for t in range(T):
                last = pe.transpose(b6[0:CTX2, S + t * P:S + (t + 1) * P], x2n[:, t, P:CTX], ident[:, :])
            last.then_inc(s["c_x2T_ps"], 1)
            pe.wait_ge(s["c_x2T"], 2)
            for e in range(2):
                last = mm(pe, b4[:, e * S:(e + 1) * S], [(w_k1[:, 0, e * P:(e + 1) * P], x2T[:, 0, :]),
                                                        (w_k1[0:CTX2, 1, e * P:(e + 1) * P], x2T[0:CTX2, 1, :])])
            last.then_inc(s["c_k_ps"], 1)
            for t in range(T):
                last = mm(pe, b3[:, t * E2:(t + 1) * E2], [(x2T[:, 0, t * P:(t + 1) * P], w_v1[:, 0, :]),
                                                          (x2T[0:CTX2, 1, t * P:(t + 1) * P], w_v1[0:CTX2, 1, :])])
            last.then_inc(s["c_v_ps"], 1)
            pe.wait_ge(s["c_norm"], T)
            turn(pe, x1n, b5, "c_xT_ps")
            pe.wait_ge(s["c_xT"], 2)
            for e in range(2):
                last = mm(pe, b6[:, e * S:(e + 1) * S], [(w_q1[:, k, e * P:(e + 1) * P], xT[:, k, :]) for k in range(KD)])
            last.then_inc(s["c_q_ps"], 1)
            yield
            pe.wait_ge(s["c_q"], 2)
            pe.wait_ge(s["c_k"], 2)
            for t in range(T):
                last = mm(pe, b7[:, t * S:(t + 1) * S], [(q1[:, e, t * P:(t + 1) * P], k1[:, e, :]) for e in range(2)])
            last.then_inc(s["c_s_ps"], 1)
            pe.wait_ge(s["c_p"], 2)
            for k in range(2):
                for t in range(T):
                    last = pe.transpose(b5[:, k * S + t * P:k * S + (t + 1) * P], pe_[:, 0, t, k * P:(k + 1) * P], ident[:, :])
            last.then_inc(s["c_pT_ps"], 1)
            pe.wait_ge(s["c_pT"], 1)
            pe.wait_ge(s["c_v"], 1)
            for e in range(2):
                last = mm(pe, b3[:, e * S:(e + 1) * S], [(v1x[:, k, e * P:(e + 1) * P], pT[:, 0, k, :]) for k in range(2)])
            last.then_inc(s["c_ctx_ps"], 1)
            pe.wait_ge(s["c_ctx"], 1)
            for t in range(T):
                last = mm(pe, b4[:, t * D:(t + 1) * D], [(cT[:, e, t * P:(t + 1) * P], w_o1[:, e, :]) for e in range(2)])
            last.then_inc(s["c_out_ps"], 1)
            yield

        def c_act(act, own):
            b3, b4, b5, b6, b7 = bank[3:8]
            act.wait_ge(s["c_x2T_ps"], 1)
            act.activation(x2T[:, 0, :], b6[:, 0:S], ACT.Identity, bias=ln2_b[:, 0:1], scale=ln2_g[:, 0:1]).then_inc(s["c_x2T"], 1)
            act.activation(x2T[0:CTX2, 1, :], b6[0:CTX2, S:2 * S], ACT.Identity, bias=ln2_b[0:CTX2, 1:2],
                           scale=ln2_g[0:CTX2, 1:2]).then_inc(s["c_x2T"], 1)
            act.wait_ge(s["c_k_ps"], 1)
            for e in range(2):
                act.activation(k1[:, e, :], b4[:, e * S:(e + 1) * S], ACT.Identity, bias=b_k1[:, e:e + 1]).then_inc(s["c_k"], 1)
            act.wait_ge(s["c_xT_ps"], 1)
            for k in range(KD):
                act.activation(xT[:, k, :], b5[:, k * S:(k + 1) * S], ACT.Identity, bias=ln1_b[:, k:k + 1],
                               scale=ln1_g[:, k:k + 1]).then_inc(s["c_xT"], 1)
            act.wait_ge(s["c_q_ps"], 1)
            for e in range(2):
                act.activation(q1[:, e, :], b6[:, e * S:(e + 1) * S], ACT.Identity, bias=b_q1s[:, e:e + 1],
                               scale=1.0 / 16.0).then_inc(s["c_q"], 1)
            yield
            act.wait_ge(s["c_max"], 1)
            for t in range(T):
                act.activation(pe_[:, 0, t, :], b7[:, t * S:(t + 1) * S], ACT.Exp, bias=nmax[:, 0, t:t + 1],
                               accum_out=sums[:, t:t + 1]).then_inc(s["c_p"], 1)
            act.wait_ge(s["c_pT_ps"], 1)
            act.activation(pT[:, 0, :, :].rearrange("p a b -> p (a b)"), b5[:, :], ACT.Copy).then_inc(s["c_pT"], 1)
            act.wait_ge(s["c_ctx_ps"], 1)
            act.activation(flat(cT[:, :, :]), b3[:, :], ACT.Copy).then_inc(s["c_ctx"], 1)
            yield

        def c_dve(dve, own):
            b3, b4, b5, b6, b7 = bank[3:8]
            stats(dve, own, cx, "c2")
            normal(dve, cx, x2n, "c2")
            dve.wait_ge(s["t1_norm"], T)
            stats(dve, own, x4, "c")
            normal(dve, x4, x1n, "c")
            dve.wait_ge(s["c_v_ps"], 1)
            dve.tensor_tensor(v1x[:, :, :], b3[:, :].rearrange("p (t e) -> p t e", t=T),
                              b_v1[:, :].unsqueeze(1).to_broadcast([P, T, E2]), ALU.add).then_inc(s["c_v"], 1)
            yield
            dve.wait_ge(s["c_s_ps"], 1)
            dve.tensor_reduce(nmax[:, 0, :], b7[:, :].rearrange("p (t k) -> p t k", t=T), AX, ALU.max, negate=True).then_inc(s["c_max"], 1)
            dve.wait_ge(s["c_p"], 2)
            own.link(dve.reciprocal(rsum[:, :], sums[:, :]))
            dve.wait_ge(s["c_out_ps"], 1)
            dve.wait_ge(s["c_x4b"], 1)
            for t in range(T):
                own.did(dve.scalar_tensor_tensor(x5[:, t, :], b4[:, t * D:(t + 1) * D], rsum[:, t:t + 1], x4b[:, t, :], ALU.mult, ALU.add))
            own.wait()
            stats(dve, own, x5, "c1")
            normal(dve, x5, x5, "c1")
            yield

        def c_pool(pool, own):
            rstd(pool, "c2")
            rstd(pool, "c")
            pool.wait_ge(s["t1_norm"], T)
            pool.tensor_tensor(x4b[:, :, :], x4[:, :, :], b_o1[:, :].unsqueeze(1).to_broadcast([P, T, D]), ALU.add).then_inc(s["c_x4b"], 1)
            yield
            rstd(pool, "c1")
            yield

        GB = [bank[3], bank[4], bank[6]]

        def l_pe(pe):
            b3, b4, b5, b6, b7 = bank[3:8]
            pe.wait_ge(s["c1_norm"], T)
            turn(pe, x5, b5, "l_xT_ps")
            pe.wait_ge(s["l_xT"], 1)
            for g in range(3):
                for m in range(KD):
                    last = mm(pe, GB[g][:, m * S:(m + 1) * S],
                              [(w_g[:, g, k, m * P:(m + 1) * P], xT[:, k, :]) for k in range(KD)]
                              + [(u_g[:, g, k, m * P:(m + 1) * P], state[:, k, :]) for k in range(KD)])
                last.then_inc(s["l_g_ps"], 1)
            for t in range(T):
                last = mm(pe, b7[:, t * D:(t + 1) * D], [(xT[:, k, t * P:(t + 1) * P], w_ho[:, k, :]) for k in range(KD)])
            last.then_inc(s["l_xw_ps"], 1)
            yield

        def l_act(act, own, b):
            b3, b4, b5, b6, b7 = bank[3:8]
            act.wait_ge(s["l_xT_ps"], 1)
            act.activation(flat(xT[:, :, :]), b5[:, :], ACT.Copy).then_inc(s["l_xT"], 1)
            for g in range(3):
                act.wait_ge(s["l_g_ps"], g + 1)
                for m in range(KD):
                    act.activation(tg[:, g, m, :], GB[g][:, m * S:(m + 1) * S], ACT.Tanh, bias=b_gh[:, g, m:m + 1],
                                   scale=1.0 if g == 2 else 0.5).then_inc(s["l_tanh"], 1)
            act.wait_ge(s["l_xw_ps"], 1)
            act.activation(xw[:, :], b7[:, :], ACT.Copy).then_inc(s["l_xw"], 1)
            yield

        def l_dve(dve, own):
            dve.wait_ge(s["l_tanh"], 2)
            own.did(dve.scalar_tensor_tensor(flat(ug[:, 0, :, :]), flat(tg[:, 0, :, :]), 1.0, flat(state[:, :, :]), ALU.add, ALU.mult))
            dve.wait_ge(s["l_tanh"], 6)
            own.link(dve.scalar_tensor_tensor(flat(ug[:, 1, :, :]), flat(tg[:, 1, :, :]), 1.0, flat(tg[:, 2, :, :]), ALU.add, ALU.mult))
            dve.wait_ge(s["l_g_ps"], 3)
            dve.scalar_tensor_tensor(flat(state[:, :, :]), flat(ug[:, 0, :, :]), 0.5, flat(ug[:, 1, :, :]), ALU.mult, ALU.add).then_inc(s["l_state"], 1)
            yield

        def l_sp(sp, b):
            sp.wait_ge(s["c1_norm"], T)
            sp.dma_start(kept_x[bass.ds(b, 1), :, :].rearrange("a p n -> p (a n)"), flat(x5[:, :, :])).then_inc(s["l_kept"], 16)
            sp.wait_ge(s["l_xw"], 1)
            sp.dma_start(kept_w[bass.ds(b, 1), :, :].rearrange("a p n -> p (a n)"), xw[:, :]).then_inc(s["l_kept"], 16)
            sp.wait_ge(s["l_kept"], 32)
            yield

        FOLDS = []
        for k in range(KD):
            for j in range(2):
                FOLDS.append((w_q[:, k, j * 512:(j + 1) * 512], lora_a[:, 0, k * P:(k + 1) * P], qb[:, j * 512:(j + 1) * 512]))
            FOLDS.append((w_k[:, k, :], lora_a[:, 1, k * P:(k + 1) * P], kb[:, :]))
            FOLDS.append((w_v[:, k, :], lora_a[:, 2, k * P:(k + 1) * P], vb[:, :]))
        for c in range(8):
            FOLDS.append((w_ao[:, c, :], lora_ao[:, c * P:(c + 1) * P], obm[:, :]))

        def ended(eng, n):
            eng.drain().then_inc(arrived, 1)
            eng.wait_ge(phase, n)

        def next_phase(sp):
            sp.wait_ge(arrived, 4)
            sp.sem_clear(range(numbers[0], numbers[-1] + 1))
            sp.sem_clear(arrived)
            sp.sem_inc(phase, 1)

        def run(*gens):
            for g in gens:
                for _ in g:
                    pass

        block = ctx.enter_context(nc.Block())

        @block.sync
        def _(sp):
            first = [(w_in, "w_in"), (w_xp, "w_xp"), (w_out, "w_out"), (conv_w, "conv_w"), (conv_b, "conv_b"), (ln_g, "ln_g"), (ln_b, "ln_b"),
                     (w_dt, "w_dt"), (b_dt, "b_dt"), (a_log, "a_log"), (d_skip, "d_skip")]
            for dst, name in first:
                sp.dma_start(dst[tuple([slice(None)] * len(dst.shape))], A[name]).then_inc(s["loads_mamba"], 16)
            rest = [(wv0, "wv0"), (bv0, "bv0"), (wt0[:, 0, :], "wt0a"), (wt0[0:CTX2, 1, :], "wt0b"), (bt0, "bt0"), (w_gl, "w_gl"), (w_b, "w_b"),
                    (w_i, "w_i"), (w_o, "w_o"), (prio, "prio"), (w_q, "w_q"), (w_k, "w_k"), (w_v, "w_v"), (w_ao, "w_ao"),
                    (lora_a, "lora_a"), (lora_ao, "lora_ao"), (qb, "qb"), (kb, "kb"), (vb, "vb"), (obm, "ob"), (cs, "cs"),
                    (ln1_g, "ln1_g"), (ln1_b, "ln1_b"), (ln2_g[:, 0:1], "ln2_ga"), (ln2_g[0:CTX2, 1:2], "ln2_gb"),
                    (ln2_b[:, 0:1], "ln2_ba"), (ln2_b[0:CTX2, 1:2], "ln2_bb"),
                    (w_q1, "w_q1"), (w_k1[:, 0, :], "w_k1a"), (w_k1[0:CTX2, 1, :], "w_k1b"), (w_v1[:, 0, :], "w_v1a"), (w_v1[0:CTX2, 1, :], "w_v1b"),
                    (w_o1, "w_o1"), (b_q1, "b_q1"), (b_k1, "b_k1"), (w_g, "w_g"), (u_g, "u_g"), (b_g, "b_g"), (w_ho, "w_ho"), (u_ho, "u_ho"),
                    (in_c, "in_c")]
            rows = [(b_gl, "b_gl"), (b_v1, "b_v1"), (b_o1, "b_o1"), (b_ho, "b_ho")]
            for dst, name in rest:
                dst = dst if isinstance(dst, bass.AP) else dst[tuple([slice(None)] * len(dst.shape))]
                sp.dma_start(dst, A[name]).then_inc(s["loads_rest"], 16)
            for dst, name in rows:
                sp.dma_start(dst[:, :], A[name].partition_broadcast(P)).then_inc(s["loads_rest"], 16)
            build.n_first, build.n_rest = len(first), len(rest) + len(rows)
            sp.wait_ge(s["loads_rest"], 16 * (len(rest) + len(rows)))
            next_phase(sp)
            with sp.Fori(0, NB) as b:
                run(a_sp(sp, b), r_sp(sp, b), l_sp(sp, b))
                next_phase(sp)
            for n in range(2):
                rows = slice(4 * n, 4 * n + 4)
                sp.dma_start(XW[:, rows, :], kept_w[rows, :, :].rearrange("b p n -> p b n")).then_inc(s[f"e_load_w{n}"], 16)
                sp.dma_start(XS[:, rows, :], kept_x[rows, :, :].rearrange("b p n -> p b n")).then_inc(s[f"e_load_x{n}"], 16)
            out_v = out.rearrange("b (t p) d -> p (b t) d", p=P)
            for b in range(NB):
                sp.wait_ge(s["e_norm"], 2 * b + 2)
                sp.dma_start(out_v[:, 2 * b:2 * b + 2, :], XS[:, b, :].rearrange("p (t d) -> p t d", t=T)).then_inc(s["e_store"], 16)
            sp.wait_ge(s["e_store"], 16 * NB)

        N_FIRST, N_REST = 16 * build.n_first, 16 * build.n_rest

        @block.gpsimd
        def _(pool):
            own = Own(pool, s["pool_own"])
            own.did(pool.memset(ident[:, :], 0.0))
            own.did(pool.memset(neghalf[:, :], -0.5))
            pool.memset(ones[:, :], 1.0).then_inc(s["prep_pool"], 1)
            pool.memset(v1[:, :, :, HD:HD + 1], 1.0).then_inc(s["prep_pool"], 1)
            own.wait()
            pool.affine_select(out=ident[:, :], in_=ident[:, :], compare_op=ALU.not_equal, fill=1.0, base=0, pattern=[[-1, P]],
                               channel_multiplier=1).then_inc(s["prep_pool"], 1)
            pool.wait_ge(s["prep_pe"], len(FOLDS))
            for i in range(2):
                pool.memset(dA[i][:, :, 0:1], 0.0).then_inc(s["prep_pool"], 1)
            ended(pool, 1)
            with pool.Fori(0, NB) as b:
                own = Own(pool, s["pool_own"])
                run(a_pool(pool, own), b_pool(pool, own), f_pool(pool, own), t_pool(pool, own), c_pool(pool, own))
                ended(pool, b + 2)
            pool.wait_ge(s["e_var"], 1)
            pool.tensor_tensor(e_rs[:, :], e_var[:, :], neghalf[:, :], ALU.pow).then_inc(s["e_rstd"], 1)

        @block.scalar
        def _(act):
            act.wait_ge(s["loads_mamba"], N_FIRST)
            act.activation(flat(a_neg[:, :, :]), flat(a_log[:, :, :]), ACT.Exp).then_inc(s["prep_act"], 1)
            act.wait_ge(s["prep_act"], 1)
            act.activation(flat(a_neg[:, :, :]), flat(a_neg[:, :, :]), ACT.Copy, scale=-1.0).then_inc(s["prep_act"], 1)
            ended(act, 1)
            with act.Fori(0, NB) as b:
                own = Own(act, s["act_own"])
                run(a_act(act, own), b_act(act, own), f_act(act, own), t_act(act, own), c_act(act, own), l_act(act, own, b))
                ended(act, b + 2)
            for i in range(2):
                act.wait_ge(s["e_sum"], i + 1)
                act.activation(flat(XW[:, 4 * i:4 * i + 4, :]), flat(XW[:, 4 * i:4 * i + 4, :]), ACT.Tanh).then_inc(s["e_tanh"], 1)

        @block.vector
        def _(dve):
            own = Own(dve, s["dve_own"])
            dve.wait_ge(s["loads_mamba"], N_FIRST)
            own.did(dve.tensor_scalar(flat(conv_wh[:, :, :]), flat(conv_w[:, :, :]), 0.5, None, ALU.mult))
            own.did(dve.tensor_scalar(conv_bh[:, :], conv_b[:, :], 0.5, None, ALU.mult))
            own.did(dve.tensor_scalar(w_in[:, :, DI:], w_in[:, :, DI:], 0.5, None, ALU.mult))
            dve.wait_ge(s["loads_rest"], N_REST)
            own.did(dve.tensor_scalar(b_q1s[:, :], b_q1[:, :], 1.0 / 16.0, None, ALU.mult))
            own.did(dve.tensor_scalar(flat(b_gh[:, 0:2, :]), flat(b_g[:, 0:2, :]), 0.5, None, ALU.mult))
            own.did(dve.tensor_copy(b_gh[:, 2, :], b_g[:, 2, :]))
            own.did(dve.tensor_scalar(u_g[:, :, :, :].rearrange("p a b c -> p (a b c)"), u_g[:, :, :, :].rearrange("p a b c -> p (a b c)"),
                                      0.5, None, ALU.mult))
            own.did(dve.tensor_scalar(flat(u_ho[:, :, :]), flat(u_ho[:, :, :]), 0.5, None, ALU.mult))
            own.link(dve.memset(state[:, :, :], 2.0))
            for k in range(KD):
                own.did(dve.tensor_scalar(state[:, k, :], state[:, k, :], in_c[:, k:k + 1], None, ALU.mult))
            for n, (dst, _, _) in enumerate(FOLDS):
                dve.wait_ge(s["prep_pe"], n + 1)
                dve.scalar_tensor_tensor(dst, bank[n % 2][:, 0:dst.shape[1]], LSCALE, dst, ALU.mult, ALU.add).then_inc(s["prep_evac"], 1)
            ended(dve, 1)
            with dve.Fori(0, NB) as b:
                own = Own(dve, s["dve_own"])
                run(a_dve(dve, own), b_dve(dve, own), f_dve(dve, own), t_dve(dve, own), c_dve(dve, own), l_dve(dve, own))
                ended(dve, b + 2)
            own = Own(dve, s["dve_own"])
            dve.wait_ge(s["e_cu_ps"], 1)
            own.link(dve.tensor_tensor(cu[:, :].rearrange("p (t d) -> p t d", t=T), bank[0][:, :].rearrange("p (t d) -> p t d", t=T),
                                       b_ho[:, :].unsqueeze(1).to_broadcast([P, T, D]), ALU.add))
            for i in range(2):
                dve.wait_ge(s[f"e_load_w{i}"], 16)
                dve.tensor_tensor(XW[:, 4 * i:4 * i + 4, :], XW[:, 4 * i:4 * i + 4, :], cu[:, :].unsqueeze(1).to_broadcast([P, 4, T * D]),
                                  ALU.add).then_inc(s["e_sum"], 1)
            for i in range(2):
                dve.wait_ge(s["e_tanh"], i + 1)
                dve.wait_ge(s[f"e_load_x{i}"], 16)
                own.link(dve.tensor_tensor(flat(XS[:, 4 * i:4 * i + 4, :]), flat(XS[:, 4 * i:4 * i + 4, :]), flat(XW[:, 4 * i:4 * i + 4, :]), ALU.add))
                for r in range(8 * i, 8 * i + 8):
                    own.did(dve.bn_stats(e_st[:, r, :], XS[:, r // 2, (r % 2) * D:(r % 2 + 1) * D]))
            own.wait()
            for r in range(NB * T):
                own.did(dve.bn_aggr(e_mv[:, r, :], e_st[:, r, :]))
            own.wait()
            dve.tensor_scalar(e_var[:, :], e_mv[:, :, 1], EPS, None, ALU.add).then_inc(s["e_var"], 1)
            dve.wait_ge(s["e_rstd"], 1)
            for r in range(NB * T):
                x = XS[:, r // 2, (r % 2) * D:(r % 2 + 1) * D]
                dve.tensor_scalar(x, x, e_mv[:, r, 0:1], e_rs[:, r:r + 1], ALU.subtract, ALU.mult).then_inc(s["e_norm"], 1)

        @block.tensor
        def _(pe):
            pe.wait_ge(s["loads_rest"], N_REST)
            for n, (dst, l, r) in enumerate(FOLDS):
                if n >= 2:
                    pe.wait_ge(s["prep_evac"], n - 1)
                pe.matmul(bank[n % 2][:, 0:dst.shape[1]], l, r, start=True, stop=True).then_inc(s["prep_pe"], 1)
            ended(pe, 1)
            with pe.Fori(0, NB) as b:
                run(a_pe(pe), b_pe(pe), f_pe(pe), t_pe(pe), c_pe(pe), l_pe(pe))
                ended(pe, b + 2)
            for t in range(T):
                last = mm(pe, bank[0][:, t * D:(t + 1) * D], [(state[:, k, t * P:(t + 1) * P], u_ho[:, k, :]) for k in range(KD)])
            last.then_inc(s["e_cu_ps"], 1)


def arrays_of(i):
    def t(a):
        return np.ascontiguousarray(a)

    def kp(a):
        return t(a.reshape(-1, P, a.shape[1]).transpose(1, 0, 2))

    def cp(a):
        return t(a.reshape(-1, P).T)

    def eo(a, heads):
        return t(a.reshape(heads // GH, GH, HH, 2, -1).transpose(0, 3, 1, 2, 4).reshape(heads * HD, -1))

    xp = i["L0_attn_W_xp"]
    wt = i["L0_xattn_Wt"].T
    g2, b2 = i["L1_xattn_ln2_g"], i["L1_xattn_ln2_b"]
    f = [i[f"L1_ffn_{n}"].T for n in ("wf", "wi", "wc")]
    u = [i[f"L1_ffn_{n}"].T for n in ("uf", "ui", "uc")]
    inv = (np.float32(1.0) / np.float32(10000.0) ** (np.arange(0, HD, 2, dtype=np.float32) / np.float32(HD))).astype(np.float32)
    ang = (np.arange(S, dtype=np.float32)[:, None] * inv[None, :]).astype(np.float32).T.astype(np.float64)
    co, si = np.cos(ang).astype(np.float32), np.sin(ang).astype(np.float32)
    cs = np.stack([co, si, co / np.float32(8), si / np.float32(8)], axis=1)
    return {
        "x": i["x"], "ctx": i["ctx_768"],
        "w_in": kp(i["L0_attn_W_in"]), "w_xp": kp(xp), "w_out": kp(i["L0_attn_W_out"]),
        "conv_w": kp(i["L0_attn_conv_w"]), "conv_b": cp(i["L0_attn_conv_b"]), "ln_g": cp(i["L0_attn_ln_g"]), "ln_b": cp(i["L0_attn_ln_b"]),
        "w_dt": cp(i["L0_attn_W_dt"][0]), "b_dt": cp(i["L0_attn_b_dt"]), "a_log": kp(i["L0_attn_A_log"]), "d_skip": cp(i["L0_attn_D"]),
        "wv0": kp(t(i["L0_xattn_Wv"].T)), "bv0": cp(i["L0_xattn_bv"]), "wt0a": t(wt[:P]), "wt0b": t(wt[P:]), "bt0": cp(i["L0_xattn_bt"]),
        "w_gl": kp(t(np.concatenate([i["L0_ffn_Wg"].T, i["L0_ffn_A"].reshape(NLOW, D).T], axis=1))),
        "b_gl": t(i["L0_ffn_bg"]), "w_b": t(i["L0_ffn_B"].transpose(0, 2, 1).reshape(NLOW, FF)),
        "w_i": kp(t(i["L0_ffn_Wi"].T)), "w_o": kp(t(i["L0_ffn_Wo"].T)),
        "prio": np.tile(np.arange(NE, 0, -1, dtype=np.float32), (P, 1)),
        "w_q": kp(t(eo(i["L1_attn_Wq"], NQ).T)), "w_k": kp(t(eo(i["L1_attn_Wk"], NKV).T)), "w_v": kp(t(i["L1_attn_Wv"].T)),
        "w_ao": kp(t(i["L1_attn_Wo"].T)), "lora_a": t(np.stack([i["L1_attn_qA"], i["L1_attn_kA"], i["L1_attn_vA"]], axis=1)),
        "lora_ao": i["L1_attn_oA"], "qb": t(eo(i["L1_attn_qB"], NQ).T), "kb": t(eo(i["L1_attn_kB"], NKV).T), "vb": t(i["L1_attn_vB"].T),
        "ob": t(i["L1_attn_oB"].T), "cs": t(np.tile(cs, (GH, 1, 1))),
        "ln1_g": cp(i["L1_xattn_ln1_g"]), "ln1_b": cp(i["L1_xattn_ln1_b"]),
        "ln2_ga": t(g2[:P, None]), "ln2_gb": t(g2[P:, None]), "ln2_ba": t(b2[:P, None]), "ln2_bb": t(b2[P:, None]),
        "w_q1": kp(i["L1_xattn_Wq"]), "w_k1a": t(i["L1_xattn_Wk"][:P]), "w_k1b": t(i["L1_xattn_Wk"][P:]),
        "w_v1a": t(i["L1_xattn_Wv"][:P]), "w_v1b": t(i["L1_xattn_Wv"][P:]), "w_o1": kp(i["L1_xattn_Wo"]),
        "b_q1": cp(i["L1_xattn_bq"]), "b_k1": cp(i["L1_xattn_bk"]), "b_v1": i["L1_xattn_bv"], "b_o1": i["L1_xattn_bo"],
        "w_g": t(np.stack([kp(t(a)) for a in f], axis=1)), "u_g": t(np.stack([kp(t(a)) for a in u], axis=1)),
        "b_g": t(np.stack([cp(i[f"L1_ffn_{n}"]) for n in ("bf", "bi", "bc")], axis=1)),
        "w_ho": kp(t(i["L1_ffn_wo"].T)), "u_ho": kp(t(i["L1_ffn_uo"].T)), "b_ho": i["L1_ffn_bo"], "in_c": cp(i["L1_ffn_in_c"]),
    }


def kernel(**inputs):
    import concourse.bacc as _bacc
    from concourse.bass_utils import run_bass_kernel_spmd as _run

    nc = _bacc.Bacc("TRN2", target_bir_lowering=False, num_devices=1)
    arrays = {f"in_{k}": np.ascontiguousarray(v) for k, v in arrays_of({k: np.asarray(v) for k, v in inputs.items()}).items()}
    A = {k[3:]: nc.dram_tensor(k, v.shape, F32, kind="ExternalInput").ap() for k, v in arrays.items()}
    out = nc.dram_tensor("out", (NB, S, D), F32, kind="ExternalOutput").ap()
    build(nc, A, out)
    r = _run(nc, [arrays], core_ids=[0])
    return r.results[0]["out"]
```

```python
from contextlib import ExitStack

import numpy as np

import concourse.bass as bass
from concourse import mybir

F32 = mybir.dt.float32
F32R = mybir.dt.float32r
ALU = mybir.AluOpType
ACT = mybir.ActivationFunctionType
AX = mybir.AxisListType.X

P = 128
NB, S, D = 8, 256, 256
T = S // P
KD = D // P
CTX = 192
CTX2 = CTX - P
DI, NS, TAPS = 512, 16, 4
EC = DI // P
HN = 4
VH = 128
NE, RK = 4, 4
NLOW = NE * RK
PARTS = 4
NPACK = PARTS * NLOW
FF = 1024
FC = FF // P
NQ, NKV, HD = 16, 4, 64
GH = NQ // NKV
HH = HD // 2
LORA = 8
LSCALE = 2.0
E2 = 256
EPS = 1e-5
BIG = 1e8

UH = NS // HN
UNITS = [(c, h) for c in range(EC) for h in range(UH)]

NA = 26
NB_UNITS = 49
AFTER = {1: [0], 3: [1], 4: [2], 5: [3, 4], 7: [5], 9: [6], 11: [7], 13: [8], 14: [9, 10], 15: [11], 18: [12], 19: [13], 26: [14],
         29: [15], 33: [16], 34: [17], 35: [18], 37: [19], 41: [20], 43: [21, 22], 45: [23], 46: [24, 25]}
ORDER = [x for b in range(NB_UNITS) for x in [("B", b)] + [("A", a) for a in AFTER.get(b, [])]]
assert [u for n, u in ORDER if n == "A"] == list(range(NA))

COUNTED = """
loads_mamba loads_rest prep_pool prep_halves prep_act prep_pe prep_evac
dve_own act_own pool_own
a_x a_var a_rstd a_norm a_xnT_ps a_xnT a_in_ps a_tap a_conv a_z_tanh a_silu_z a_xc_tanh a_xc
a_xpj_ps a_xpj a_store a_B a_C a_dtl_ps a_u a_ln a_dt a_dtx a_dA a_dBx a_scan a_hC a_pairs a_four a_y_ps a_gated a_out_ps
a1_norm
b_var b_rstd b_ctx b_cxT_ps b_cxT b_tT_ps b_tT b_xT_ps b_xT b_vT_ps b_vT b_ss_ps b_ss b_rn b_diag b_row_ps b_dots_ps
b1_norm
f_xT_ps f_xT f_gl_ps f_exp f_exp_in f_low f_lowT_ps f_lowT f_wdiag f_w_ps f_wrow f_z1_ps f_z2_ps f_r f_h f_out_ps
f1_norm
t_zero t_xT_ps t_xT t_proj_ps t_proj t_swap_ps t_rot t_kz t_v_ps t_v t_ro t_s_ps t_max t_p t_pT_ps t_pT t_o_ps t_o t_oT_ps t_oT
t_out_ps t1_norm
c_norm c2_norm c_xT_ps c_xT c_x2T_ps c_x2T c_q_ps c_q c_k_ps c_k c_v_ps c_v c_s_ps c_max c_p
c_pT_ps c_pT c_ctx_ps c_ctx c_out_ps c_x4b c_res c1_norm
l_xT_ps l_xT l_g_ps l_u_ps l_tanh l_state l_xw_ps l_xw l_kept e_load_w0 e_load_w1 e_load_x0 e_load_x1
e_cu_ps e_sum e_tanh e_var e_rstd e_norm e_store
""".split()


NORMS = {"a": ("a", 1), "a1": ("a", 2), "b1": ("b", 1), "f1": ("b", 2), "t1": ("b", 3), "c2": ("b", 4), "c": ("b", 5), "c1": ("b", 6)}


class Own:

    def __init__(self, eng, sem):
        self.eng, self.sem, self.n = eng, sem, 0

    def did(self, ins):
        ins.then_inc(self.sem, 1)
        self.n += 1

    def wait(self):
        self.eng.wait_ge(self.sem, self.n)

    def link(self, ins):
        self.did(ins)
        self.wait()


def build(nc, A, out):
    with ExitStack() as ctx:
        def sb(name, shape, dtype=F32):
            return ctx.enter_context(nc.sbuf_tensor(name, shape, dtype))

        phase = ctx.enter_context(nc.semaphore("phase"))
        arrived = ctx.enter_context(nc.semaphore("arrived"))
        s = {n: ctx.enter_context(nc.semaphore(n)) for n in COUNTED}
        numbers = sorted(x.num for x in s.values())
        assert numbers == list(range(numbers[0], numbers[-1] + 1))
        bank = [ctx.enter_context(nc.psum_tensor(f"bank{i}", [P, 512], F32)) for i in range(8)]
        scratch = nc.dram_tensor("xpj_scratch", (2 * NS + 1, S), F32, kind="Internal").ap()
        kept_x = nc.dram_tensor("kept_x", (NB, P, T * D), F32, kind="Internal").ap()
        kept_w = nc.dram_tensor("kept_w", (NB, P, T * D), F32, kind="Internal").ap()

        w_in = sb("w_in", [P, KD, 2 * DI]); w_xp = sb("w_xp", [P, EC, 2 * NS + 1]); w_out = sb("w_out", [P, EC, D])
        conv_w = sb("conv_w", [P, EC, TAPS]); conv_wh = sb("conv_wh", [P, EC, TAPS])
        conv_b = sb("conv_b", [P, EC]); conv_bh = sb("conv_bh", [P, EC])
        ln_g = sb("ln_g", [P, KD]); ln_b = sb("ln_b", [P, KD])
        w_dt = sb("w_dt", [P, EC]); b_dt = sb("b_dt", [P, EC]); a_log = sb("a_log", [P, EC, NS]); a_neg = sb("a_neg", [P, EC, NS])
        d_skip = sb("d_skip", [P, EC])
        wv0 = sb("wv0", [P, KD, VH]); bv0 = sb("bv0", [P, 1]); wt0 = sb("wt0", [P, 2, VH]); bt0 = sb("bt0", [P, 1])
        w_gl = sb("w_gl", [P, KD, NE + NLOW]); b_gl = sb("b_gl", [P, NE]); w_b = sb("w_b", [NPACK, FF], F32R)
        part = sb("part", [NPACK, 2])
        w_i = sb("w_i", [P, KD, FF]); w_o = sb("w_o", [P, FC, D]); prio = sb("prio", [P, NE])
        w_q = sb("w_q", [P, KD, NQ * HD]); w_k = sb("w_k", [P, KD, 2 * NKV * HD]); w_v = sb("w_v", [P, KD, NKV * HD])
        w_ao = sb("w_ao", [P, 8, D])
        cs = sb("cs", [P, 4, S])
        swap = sb("swap", [P, P])
        ln1_g = sb("ln1_g", [P, KD]); ln1_b = sb("ln1_b", [P, KD]); ln2_g = sb("ln2_g", [P, 2]); ln2_b = sb("ln2_b", [P, 2])
        w_q1 = sb("w_q1", [P, KD, E2]); w_k1 = sb("w_k1", [P, 2, E2]); w_v1 = sb("w_v1", [P, 2, E2]); w_o1 = sb("w_o1", [P, 2, D])
        b_q1 = sb("b_q1", [P, 2]); b_q1s = sb("b_q1s", [P, 2]); b_k1 = sb("b_k1", [P, 2]); b_v1 = sb("b_v1", [P, E2]); b_o1 = sb("b_o1", [P, D])
        w_g = sb("w_g", [P, 3, KD, D]); u_g = sb("u_g", [P, 3, KD, D]); b_g = sb("b_g", [P, 3, KD]); b_gh = sb("b_gh", [P, 3, KD])
        w_ho = sb("w_ho", [P, KD, D]); u_ho = sb("u_ho", [P, KD, D]); b_ho = sb("b_ho", [P, D]); in_c = sb("in_c", [P, KD])
        ident = sb("ident", [P, P]); ones = sb("ones", [P, P]); neghalf = sb("neghalf", [P, 16])

        scans = sb("scans", [P, 4 * HN, S])
        heads = sb("heads", [P, 12, S])
        outs = sb("outs", [P, 8, S])
        turns = sb("turns", [P, 8, S])

        lora_ao = outs[0:LORA, 0:4, :].rearrange("p a b -> p (a b)")
        qb = outs[0:LORA, 4:8, :].rearrange("p a b -> p (a b)")
        lora_a = heads[0:LORA, 0:3, :]
        kb = heads[0:LORA, 6:8, :].rearrange("p a b -> p (a b)")
        vb, obm = heads[0:LORA, 4, :], heads[0:LORA, 5, :]

        x0 = sb("x0", [P, T, D])
        conv = sb("conv", [P, EC, S]); zg = sb("zg", [P, EC, S]); xc = sb("xc", [P, EC, S])
        xpj = sb("xpj", [2 * NS + 1, S]); dt = sb("dt", [P, EC, S]); dtx = conv
        Bb = sb("Bb", [P, NS, S]); Cb = sb("Cb", [P, NS, S])
        dA = [scans[:, i * HN:(i + 1) * HN, :] for i in range(2)]
        hb = [scans[:, (2 + i) * HN:(3 + i) * HN, :] for i in range(2)]
        yh = sb("yh", [P, 2, S])
        zdt = hb[0]
        udt = tz = hb[1]
        xn = xT_free = Cb[:, 0:2, :]
        xnT = Cb[:, 2:4, :]
        res = dtx[:, 0:2, :]
        x1 = sb("x1", [P, T, D])
        x2 = sb("x2", [P, T, D]); x3 = sb("x3", [P, T, D]); x4 = x2; x5 = x3
        xT = sb("xT", [P, KD, S]); cx = sb("cx", [P, T, CTX]); cxT = sb("cxT", [P, 2, S])
        sq, rscale = outs[:, 0:2, :], outs[:, 2:4, :]
        tT, vT = outs[:, 4, :], outs[:, 5, :]
        ss = sb("ss", [P, 4]); rn = sb("rn", [P, 4]); diag = outs[:, 6:8, :].rearrange("p i (t q) -> p i t q", t=T)
        sm = sb("sm", [P, 12, T, NE]); sc2 = sb("sc2", [P, 8, T])
        low = sb("low", [P, 2, T, NLOW])
        packed = outs[:, 0, :].rearrange("p (n h w k) -> p n h w k", h=2, w=2, k=NLOW)
        lowT, wrow = sb("lowT", [NPACK, 2, S], F32R), heads[:, 2:4, :]
        r1 = heads[:, 4:8, :].rearrange("p (j a) s -> p j a s", j=2)
        r2 = heads[:, 8:12, :].rearrange("p (j a) s -> p j a s", j=2)
        hT = turns
        rot = [turns[:, 4 * i:4 * i + 4, :].rearrange("p (j a) s -> p j a s", j=2) for i in range(2)]
        projected = [outs[:, 2 * i:2 * i + 2, :] for i in range(4)]
        kz = [[heads[:, g, :] for g in range(NKV)], [cxT[:, 0, :], cxT[:, 1, :], x2[:, 0, :], x2[:, 1, :]]]
        qT = heads[:, 4:12, :].rearrange("p (g j) s -> p g j s", g=NKV)
        v1 = sb("v1", [P, T, NKV, HD + 1])
        nmax = sb("nmax", [P, 4, T]); 
        pe_ = turns[:, 0:4, :].rearrange("p (j a) s -> p j a s", j=2)
        pT = turns[:, 4:8, :].rearrange("p (j a) s -> p j a s", j=2)
        rs = sb("rs", [P, 2, T, 2])
        ob = outs[:, :, :].rearrange("p (t a) (h d) -> p t (a h) d", t=T, d=HD)
        oT = heads[:, 4:12, :]
        x1n, x4b, x2n = turns[:, 2:4, :], turns[:, 6:8, :], outs[:, 6:8, 0:CTX]
        x2T = cxT
        q1, k1, v1x, cT = outs[:, 0:2, :], outs[:, 2:4, :], outs[:, 4:6, :], outs[:, 6:8, :]
        sums = sb("sums", [P, T]); rsum = sb("rsum", [P, T])
        tg = heads[:, 0:6, :].rearrange("p (g k) s -> p g k s", g=3)
        ug = heads[:, 6:10, :].rearrange("p (g k) s -> p g k s", g=2)
        xw = heads[:, 10:12, :].rearrange("p a s -> p (a s)")
        state = sb("state", [P, KD, S])
        cu = x1[:, :, :].rearrange("p a s -> p (a s)")
        XS = Bb[:, :, :].rearrange("p (b t) s -> p b (t s)", t=T)
        XW = Cb[:, :, :].rearrange("p (b t) s -> p b (t s)", t=T)
        ln_sts = [sb(f"ln_st{i}", [P, T, 6]) for i in range(2)]; ln_mv = {}; ln_var = {}; ln_rs = {}
        for tag in ("a", "a1", "b1", "f1", "t1", "c", "c2", "c1"):
            ln_mv[tag] = sb(f"mv_{tag}", [P, T, 2]); ln_var[tag] = sb(f"var_{tag}", [P, T]); ln_rs[tag] = sb(f"rstd_{tag}", [P, T])
        e_st = sb("e_st", [P, NB * T, 6]); e_mv = sb("e_mv", [P, NB * T, 2]); e_var = sb("e_var", [P, NB * T]); e_rs = sb("e_rs", [P, NB * T])

        def stats(dve, own, src, tag):
            ln_st = ln_sts[tag in ("a", "a1")]
            for t in range(T):
                own.did(dve.bn_stats(ln_st[:, t, :], src[:, t, :]))
            own.wait()
            for t in range(T):
                own.did(dve.bn_aggr(ln_mv[tag][:, t, :], ln_st[:, t, :]))
            own.wait()
            dve.tensor_scalar(ln_var[tag][:, :], ln_mv[tag][:, :, 1], EPS, None, ALU.add).then_inc(s[NORMS[tag][0] + "_var"], 1)

        def rstd(pool, tag):
            pool.wait_ge(s[NORMS[tag][0] + "_var"], NORMS[tag][1])
            pool.tensor_tensor(ln_rs[tag][:, :], ln_var[tag][:, :], neghalf[:, 0:T], ALU.pow).then_inc(s[NORMS[tag][0] + "_rstd"], 1)

        def normal(dve, src, dst, tag):
            dve.wait_ge(s[NORMS[tag][0] + "_rstd"], NORMS[tag][1])
            for t in range(T):
                dve.tensor_scalar(dst[:, t, :], src[:, t, :], ln_mv[tag][:, t, 0:1], ln_rs[tag][:, t:t + 1],
                                  ALU.subtract, ALU.mult).then_inc(s[tag + "_norm"], 1)

        def turn(pe, src, bk, sem):
            for k in range(KD):
                for t in range(T):
                    last = pe.transpose(bk[:, k * S + t * P:k * S + t * P + P], src[:, t, k * P:(k + 1) * P], ident[:, :])
            last.then_inc(s[sem], 1)

        def mm(pe, o, pairs, start=True):
            n = len(pairs)
            for i, (l, r) in enumerate(pairs):
                last = pe.matmul(o, l, r, start=(start and i == 0), stop=(i == n - 1), skip_group_check=True)
            return last

        def flat(ap):
            return ap.rearrange("p a b -> p (a b)")

        PA = bank[0:3]

        def a_sp(sp, b):
            yield 0
            sp.dma_start(x0[:, :, :], A["x"][bass.ds(b, 1), :, :].rearrange("a (t p) d -> p (a t) d", p=P)).then_inc(s["a_x"], 16)
            yield 3
            sp.wait_ge(s["a_xpj"], 1)
            sp.dma_start(scratch, xpj[:, :]).then_inc(s["a_store"], 16)
            sp.wait_ge(s["a_store"], 16)
            sp.dma_start(Bb[:, :, :], scratch[0:NS, :].partition_broadcast(P)).then_inc(s["a_B"], 16)
            sp.dma_start(Cb[:, :, :], scratch[NS:2 * NS, :].partition_broadcast(P)).then_inc(s["a_C"], 16)

        def a_dve(dve, own):
            yield 0
            dve.wait_ge(s["a_x"], 16)
            stats(dve, own, x0, "a")
            normal(dve, x0, xn, "a")
            yield 1
            for j in range(2):
                dve.wait_ge(s["a_tap"], 2 * j + 2)
                for k in range(TAPS - 1):
                    d = TAPS - 1 - k
                    for i in range(2):
                        e = 2 * j + i
                        ins = dve.scalar_tensor_tensor(conv[:, e, d:S], PA[1 + j][:, i * S:i * S + S - d], conv_wh[:, e, k:k + 1],
                                                       conv[:, e, d:S], ALU.mult, ALU.add)
                        if k == TAPS - 2:
                            ins.then_inc(s["a_conv"], 1)
                        else:
                            own.did(ins)
                    if k < TAPS - 2:
                        own.wait()
            yield 2
            for j in range(2):
                dve.wait_ge(s["a_z_tanh"], j + 1)
                dve.scalar_tensor_tensor(flat(zg[:, 2 * j:2 * j + 2, :]), flat(tz[:, 2 * j:2 * j + 2, :]), 1.0, [PA[0], PA[1]][j][:, :],
                                         ALU.add, ALU.mult).then_inc(s["a_silu_z"], 1)
            dve.wait_ge(s["a_conv"], EC)
            for e in range(EC):
                dve.wait_ge(s["a_xc_tanh"], e + 1)
                dve.scalar_tensor_tensor(xc[:, e, :], xc[:, e, :], 1.0, conv[:, e, :], ALU.add, ALU.mult).then_inc(s["a_xc"], 1)
            yield 4
            dve.wait_ge(s["a_u"], 1)
            dve.wait_ge(s["a_xc"], EC)
            own.link(dve.tensor_scalar(flat(conv[:, :, :]), flat(udt[:, :, :]), 1.0, 1.0, ALU.add, ALU.subtract))
            own.link(dve.tensor_tensor(flat(conv[:, :, :]), flat(udt[:, :, :]), flat(conv[:, :, :]), ALU.subtract))
            dve.wait_ge(s["a_ln"], 1)
            own.link(dve.tensor_tensor(flat(conv[:, :, :]), flat(conv[:, :, :]), flat(dt[:, :, :]), ALU.add))
            dve.scalar_tensor_tensor(flat(dt[:, :, :]), flat(zdt[:, :, :]), 0.0, flat(conv[:, :, :]), ALU.max, ALU.add).then_inc(s["a_dt"], 1)
            dve.wait_ge(s["a_dt"], 1)
            dve.tensor_tensor(flat(dtx[:, :, :]), flat(dt[:, :, :]), flat(xc[:, :, :]), ALU.mult).then_inc(s["a_dtx"], 1)
            for u, (c, h) in enumerate(UNITS):
                yield 6 + u
                H = hb[u % 2]
                dve.wait_ge(s["a_dA"], u + 1)
                dve.wait_ge(s["a_dBx"], u + 1)
                dve.tensor_tensor_scan(flat(H[:, :, :]), flat(dA[u % 2][:, :, :]), flat(H[:, :, :]), 0.0, ALU.mult, ALU.add).then_inc(s["a_scan"], 1)
                dve.wait_ge(s["a_scan"], u + 1)
                if u == 0:
                    dve.wait_ge(s["a_C"], 16)
                dve.tensor_tensor(flat(H[:, :, :]), flat(H[:, :, :]), flat(Cb[:, h * HN:(h + 1) * HN, :]), ALU.mult).then_inc(s["a_hC"], 1)
                if h == 2 and c >= 1:
                    skip(dve, own, c - 1)
            yield 24
            skip(dve, own, EC - 1)
            yield 25
            dve.wait_ge(s["a_out_ps"], 1)
            own.link(dve.scalar_tensor_tensor(flat(res[:, :, :]), flat(x0[:, :, :]), 2.0, PA[1][:, :], ALU.mult, ALU.add))
            stats(dve, own, res, "a1")
            normal(dve, res, x1, "a1")

        def skip(dve, own, c):
            dve.wait_ge(s["a_y_ps"], UH * (c + 1))
            own.link(dve.scalar_tensor_tensor(xc[:, c, :], xc[:, c, :], d_skip[:, c:c + 1], [PA[0], PA[2]][c % 2][:, 0:S], ALU.mult, ALU.add))
            dve.tensor_tensor(zg[:, c, :], xc[:, c, :], zg[:, c, :], ALU.mult).then_inc(s["a_gated"], 1)

        def a_pool(pool, own):
            yield 0
            rstd(pool, "a")
            yield 5
            pool.wait_ge(s["a_dtx"], 1)
            pool.wait_ge(s["a_B"], 16)

            def four(u):
                H = hb[u % 2]
                pool.wait_ge(s["a_hC"], u + 1)
                if u >= 2:
                    pool.wait_ge(s["a_y_ps"], u - 1)
                pool.tensor_tensor(H[:, 0:2, :], H[:, 0:2, :], H[:, 2:4, :], ALU.add).then_inc(s["a_pairs"], 1)
                pool.wait_ge(s["a_pairs"], u + 1)
                pool.tensor_tensor(yh[:, u % 2, :], H[:, 0, :], H[:, 1, :], ALU.add).then_inc(s["a_four"], 1)

            for u, (c, h) in enumerate(UNITS):
                yield 5 + u
                if u >= 2:
                    four(u - 2)
                    pool.wait_ge(s["a_four"], u - 1)
                pool.tensor_tensor(hb[u % 2][:, :, :], dtx[:, c:c + 1, :].to_broadcast([P, HN, S]), Bb[:, h * HN:(h + 1) * HN, :],
                                   ALU.mult).then_inc(s["a_dBx"], 1)
            for u in range(len(UNITS) - 2, len(UNITS)):
                yield 5 + u + 2
                four(u)
            yield 25
            rstd(pool, "a1")

        def a_act(act, own):
            yield 0
            act.wait_ge(s["a_xnT_ps"], 1)
            for k in range(KD):
                act.activation(xnT[:, k, :], PA[0][:, k * S:(k + 1) * S], ACT.Identity, bias=ln_b[:, k:k + 1],
                               scale=ln_g[:, k:k + 1]).then_inc(s["a_xnT"], 1)
            yield 1
            for j in range(2):
                act.wait_ge(s["a_in_ps"], j + 1)
                for i in range(2):
                    e = 2 * j + i
                    act.activation(conv[:, e, :], PA[1 + j][:, i * S:(i + 1) * S], ACT.Identity, bias=conv_bh[:, e:e + 1],
                                   scale=conv_wh[:, e, TAPS - 1:TAPS]).then_inc(s["a_tap"], 1)
            yield 2
            for j in range(2):
                act.wait_ge(s["a_in_ps"], j + 3)
                act.activation(flat(tz[:, 2 * j:2 * j + 2, :]), [PA[0], PA[1]][j][:, :], ACT.Tanh).then_inc(s["a_z_tanh"], 1)
            for e in range(EC):
                act.wait_ge(s["a_conv"], e + 1)
                act.activation(xc[:, e, :], conv[:, e, :], ACT.Tanh).then_inc(s["a_xc_tanh"], 1)
            yield 3
            act.wait_ge(s["a_xpj_ps"], 1)
            act.activation(xpj[:, :], PA[2][0:2 * NS + 1, 0:S], ACT.Copy).then_inc(s["a_xpj"], 1)
            yield 4
            act.wait_ge(s["a_dtl_ps"], 1)
            for c in range(EC):
                own.did(act.activation(zdt[:, c, :], PA[0][:, 0:S], ACT.Identity, bias=b_dt[:, c:c + 1], scale=w_dt[:, c:c + 1]))
            own.wait()
            own.link(act.activation(flat(udt[:, :, :]), flat(zdt[:, :, :]), ACT.Abs))
            act.activation(flat(udt[:, :, :]), flat(udt[:, :, :]), ACT.Exp, scale=-1.0).then_inc(s["a_u"], 1)
            act.wait_ge(s["a_u"], 1)
            act.activation(flat(dt[:, :, :]), flat(udt[:, :, :]), ACT.Ln, bias=1.0).then_inc(s["a_ln"], 1)
            yield 5
            act.wait_ge(s["a_dt"], 1)
            for u, (c, h) in enumerate(UNITS):
                yield 5 + u
                if u >= 2:
                    act.wait_ge(s["a_scan"], u - 1)
                for j in range(HN):
                    n = h * HN + j
                    ins = act.activation(dA[u % 2][:, j, 1:S], dt[:, c, 1:S], ACT.Exp, scale=a_neg[:, c, n:n + 1])
                ins.then_inc(s["a_dA"], 1)

        def a_pe(pe):
            yield 0
            pe.wait_ge(s["a_norm"], T)
            turn(pe, xn, PA[0], "a_xnT_ps")
            yield 1
            pe.wait_ge(s["a_xnT"], KD)
            for j, bk in enumerate([PA[1], PA[2], PA[0], PA[1]]):
                yield 1 + j // 2
                if j == 3:
                    pe.wait_ge(s["a_conv"], 2)
                for i in range(2):
                    e = 2 * j + i
                    last = mm(pe, bk[:, i * S:(i + 1) * S], [(w_in[:, k, e * P:(e + 1) * P], xnT[:, k, :]) for k in range(KD)])
                last.then_inc(s["a_in_ps"], 1)
            yield 3
            pe.wait_ge(s["a_xc"], EC)
            mm(pe, PA[2][0:2 * NS + 1, 0:S], [(w_xp[:, c, :], xc[:, c, :]) for c in range(EC)]).then_inc(s["a_xpj_ps"], 1)
            yield 4
            pe.wait_ge(s["a_xpj"], 1)
            pe.wait_ge(s["a_silu_z"], 1)
            mm(pe, PA[0][:, 0:S], [(ones[2 * NS:2 * NS + 1, :], xpj[2 * NS:2 * NS + 1, :])]).then_inc(s["a_dtl_ps"], 1)
            yield 8
            pe.wait_ge(s["a_u"], 1)
            for u, (c, h) in enumerate(UNITS):
                yield 8 + u
                pe.wait_ge(s["a_four"], u + 1)
                if h == 0 and c >= 2:
                    pe.wait_ge(s["a_gated"], c - 1)
                pe.matmul([PA[0], PA[2]][c % 2][:, 0:S], ident[:, :], yh[:, u % 2, :], start=(h == 0),
                          stop=(h == UH - 1)).then_inc(s["a_y_ps"], 1)
            yield 24
            pe.wait_ge(s["a_gated"], EC)
            pe.wait_ge(s["a_silu_z"], 2)
            for t in range(T):
                last = mm(pe, PA[1][:, t * D:(t + 1) * D], [(zg[:, c, t * P:(t + 1) * P], w_out[:, c, :]) for c in range(EC)])
            last.then_inc(s["a_out_ps"], 1)

        def load_context(sp, b):
            sp.dma_start(cx[:, :, :], A["ctx"][bass.ds(b, 1), :, :].rearrange("a (t p) d -> p (a t) d", p=P)).then_inc(s["b_ctx"], 16)

        def r_sp(sp, b):
            yield 39
            sp.wait_ge(s["c2_norm"], T)
            load_context(sp, b)

        def b_pe(pe):
            b3, b4, b5, b6, b7 = bank[3:8]
            yield 0
            for t in range(T):
                pe.transpose(b3[:, t * P:(t + 1) * P], cx[:, t, 0:P], ident[:, :])
            for t in range(T):
                last = pe.transpose(b3[0:CTX2, S + t * P:S + (t + 1) * P], cx[:, t, P:CTX], ident[:, :])
            last.then_inc(s["b_cxT_ps"], 1)
            turn(pe, x1, b5, "b_xT_ps")
            yield 1
            pe.wait_ge(s["b_cxT"], 2)
            mm(pe, b4[:, 0:S], [(wt0[:, 0, :], cxT[:, 0, :]), (wt0[0:CTX2, 1, :], cxT[0:CTX2, 1, :])]).then_inc(s["b_tT_ps"], 1)
            pe.wait_ge(s["b_xT"], 1)
            mm(pe, b6[:, 0:S], [(wv0[:, k, :], xT[:, k, :]) for k in range(KD)]).then_inc(s["b_vT_ps"], 1)
            yield 2
            pe.wait_ge(s["b_tT"], 2)
            pe.wait_ge(s["b_vT"], 2)
            for t in range(T):
                mm(pe, b4[:, t * S:(t + 1) * S], [(vT[:, t * P:(t + 1) * P], tT[:, :])]).then_inc(s["b_dots_ps"], 1)
            for i in range(2):
                for t in range(T):
                    last = pe.matmul(b7[:, 2 * i + t:2 * i + t + 1], sq[:, i, t * P:(t + 1) * P], ones[:, 0:1], start=True, stop=True)
            last.then_inc(s["b_ss_ps"], 1)
            yield 3
            pe.wait_ge(s["b_diag"], T)
            mm(pe, b7[:, 0:S], [(ones[:, :], diag[:, 0, :, :].rearrange("p a b -> p (a b)"))]).then_inc(s["b_row_ps"], 1)

        def b_act(act, own):
            b3, b4, b5, b6, b7 = bank[3:8]
            yield 0
            act.wait_ge(s["b_cxT_ps"], 1)
            act.activation(cxT[:, 0, :], b3[:, 0:S], ACT.Copy).then_inc(s["b_cxT"], 1)
            act.activation(cxT[0:CTX2, 1, :], b3[0:CTX2, S:2 * S], ACT.Copy).then_inc(s["b_cxT"], 1)
            act.wait_ge(s["b_xT_ps"], 1)
            act.activation(flat(xT[:, :, :]), b5[:, :], ACT.Copy).then_inc(s["b_xT"], 1)
            yield 1
            act.wait_ge(s["b_tT_ps"], 1)
            act.activation(tT[:, :], b4[:, 0:S], ACT.Identity, bias=bt0[:, :]).then_inc(s["b_tT"], 1)
            act.activation(sq[:, 1, :], b4[:, 0:S], ACT.Square, bias=bt0[:, :]).then_inc(s["b_tT"], 1)
            act.wait_ge(s["b_vT_ps"], 1)
            act.activation(vT[:, :], b6[:, 0:S], ACT.Identity, bias=bv0[:, :]).then_inc(s["b_vT"], 1)
            act.activation(sq[:, 0, :], b6[:, 0:S], ACT.Square, bias=bv0[:, :]).then_inc(s["b_vT"], 1)

        def b_dve(dve, own):
            b3, b4, b5, b6, b7 = bank[3:8]
            yield 2
            dve.wait_ge(s["b_ss_ps"], 1)
            dve.tensor_scalar(ss[:, :], b7[:, 0:4], 1e-38, None, ALU.max).then_inc(s["b_ss"], 1)
            dve.wait_ge(s["b_rn"], 1)
            for t in range(T):
                dve.tensor_scalar(diag[:, 0, t, :], ident[:, :], rn[:, 2 + t:3 + t], None, ALU.mult).then_inc(s["b_diag"], 1)
            yield 3
            dve.wait_ge(s["b_row_ps"], 1)
            for t in range(T):
                own.did(dve.tensor_scalar(rscale[:, t, :], b7[:, 0:S], rn[:, t:t + 1], BIG, ALU.mult, ALU.min))
            own.wait()
            dve.wait_ge(s["b_dots_ps"], T)
            own.link(dve.tensor_tensor(flat(rscale[:, :, :]), flat(rscale[:, :, :]), b4[:, :], ALU.mult))
            own.link(dve.tensor_tensor(flat(x2[:, :, :]), flat(rscale[:, :, :]), flat(x1[:, :, :]), ALU.add))
            stats(dve, own, x2, "b1")
            normal(dve, x2, x2, "b1")

        def b_pool(pool, own):
            yield 2
            pool.wait_ge(s["b_ss"], 1)
            pool.tensor_tensor(rn[:, :], ss[:, :], neghalf[:, 0:4], ALU.pow).then_inc(s["b_rn"], 1)
            yield 3
            rstd(pool, "b1")

        FB = bank[5:8]

        def f_pe(pe):
            b3, b4, b5, b6, b7 = bank[3:8]
            yield 4
            pe.wait_ge(s["b1_norm"], T)
            turn(pe, x2, b5, "f_xT_ps")
            yield 5
            pe.wait_ge(s["f_xT"], 1)
            for t in range(T):
                last = mm(pe, b3[:, t * 20:t * 20 + 20], [(xT[:, k, t * P:(t + 1) * P], w_gl[:, k, :]) for k in range(KD)])
            last.then_inc(s["f_gl_ps"], 1)

            def base(j):
                if j >= 3:
                    pe.wait_ge(s["f_r"], 2 * (j - 3) + 2)
                for i in range(2):
                    f = 2 * j + i
                    for k in range(KD):
                        pe.matmul(FB[j % 3][:, i * S:(i + 1) * S], w_i[:, k, f * P:(f + 1) * P], xT[:, k, :],
                                  start=(i == 0 and k == 0), stop=False, skip_group_check=True)

            def lora(j, slot):
                if slot == 1:
                    pe.wait_ge(s["f_r"], 2 * j + 1)
                for i in range(2):
                    f = 2 * j + i
                    last = pe.matmul(FB[j % 3][:, i * S:(i + 1) * S], w_b[:, f * P:(f + 1) * P], lowT[:, slot, :],
                                     start=False, stop=(slot == 1), skip_group_check=True)
                last.then_inc(s[["f_z1_ps", "f_z2_ps"][slot]], 1)

            for j in range(3):
                base(j)
            yield 6
            pe.wait_ge(s["f_low"], 1)
            for i in range(2):
                for t in range(T):
                    last = pe.transpose(b3[0:NPACK, i * S + t * P:i * S + (t + 1) * P],
                                        packed[:, i * T + t, :, :, :].rearrange("p h w k -> p (h w k)"), ident[:, :])
            last.then_inc(s["f_lowT_ps"], 1)
            pe.wait_ge(s["f_wdiag"], 4)
            mm(pe, b4[:, :], [(ones[:, :], diag[:, :, :, :].rearrange("p a b c -> p (a b c)"))]).then_inc(s["f_w_ps"], 1)
            pe.wait_ge(s["f_lowT"], 1)

            for j in range(FC // 2 + 1):
                yield 7 + j
                if j < FC // 2:
                    if j == 3:
                        base(3)
                    lora(j, 0)
                if j >= 1:
                    lora(j - 1, 1)
            yield 12
            for t in range(T):
                for f in range(FC):
                    if t == 0 and f % 2 == 0:
                        pe.wait_ge(s["f_h"], f // 2 + 1)
                    last = pe.matmul(b3[:, t * D:(t + 1) * D], hT[:, f, t * P:(t + 1) * P], w_o[:, f, :], start=(f == 0), stop=(f == FC - 1))
            last.then_inc(s["f_out_ps"], 1)

        def f_act(act, own):
            b3, b4, b5, b6, b7 = bank[3:8]
            yield 4
            act.wait_ge(s["f_xT_ps"], 1)
            act.activation(flat(xT[:, :, :]), b5[:, :], ACT.Copy).then_inc(s["f_xT"], 1)
            yield 5
            act.wait_ge(s["f_exp_in"], 1)
            act.activation(sm[:, 1, :, :], sm[:, 1, :, :], ACT.Exp).then_inc(s["f_exp"], 1)
            yield 6
            act.wait_ge(s["f_lowT_ps"], 1)
            act.activation(flat(lowT[:, :, :]), b3[0:NPACK, :], ACT.Copy).then_inc(s["f_lowT"], 1)
            act.wait_ge(s["f_w_ps"], 1)
            act.activation(flat(wrow[:, :, :]), b4[:, :], ACT.Copy).then_inc(s["f_wrow"], 1)

        def f_dve(dve, own):
            b3, b4, b5, b6, b7 = bank[3:8]
            yield 5
            dve.wait_ge(s["f_gl_ps"], 1)
            gl = b3[:, 0:2 * 20].rearrange("p (t n) -> p t n", t=T)
            per = [P, T, NE]

            def wide(col):
                return sc2[:, col, :].unsqueeze(2).to_broadcast(per)

            def tile_of(x):
                return x.unsqueeze(1).to_broadcast(per)

            own.did(dve.tensor_copy(low[:, 1, :, :], gl[:, :, NE:]))
            own.link(dve.tensor_tensor(sm[:, 0, :, :], gl[:, :, 0:NE], tile_of(b_gl[:, :]), ALU.add))
            own.link(dve.tensor_reduce(sc2[:, 0, :], sm[:, 0, :, :], AX, ALU.max))
            dve.tensor_tensor(sm[:, 1, :, :], sm[:, 0, :, :], wide(0), ALU.subtract).then_inc(s["f_exp_in"], 1)
            dve.wait_ge(s["f_exp"], 1)
            own.link(dve.tensor_reduce(sc2[:, 1, :], sm[:, 1, :, :], AX, ALU.add))
            own.link(dve.reciprocal(sc2[:, 2, :], sc2[:, 1, :]))
            own.link(dve.tensor_tensor(sm[:, 2, :, :], sm[:, 1, :, :], wide(2), ALU.mult))
            for i, (score, hit, rank, one) in enumerate([(2, 3, 4, 5), (6, 7, 8, 9)]):
                top, best = 3 + 2 * i, 4 + 2 * i
                own.link(dve.tensor_reduce(sc2[:, top, :], sm[:, score, :, :], AX, ALU.max))
                own.link(dve.tensor_tensor(sm[:, hit, :, :], sm[:, score, :, :], wide(top), ALU.is_equal))
                own.link(dve.tensor_tensor(sm[:, rank, :, :], sm[:, hit, :, :], tile_of(prio[:, :]), ALU.mult))
                own.link(dve.tensor_reduce(sc2[:, best, :], sm[:, rank, :, :], AX, ALU.max))
                own.link(dve.tensor_tensor(sm[:, one, :, :], sm[:, rank, :, :], wide(best), ALU.is_equal))
                if i == 0:
                    own.link(dve.scalar_tensor_tensor(sm[:, 6, :, :], sm[:, 5, :, :], -2.0, sm[:, 2, :, :], ALU.mult, ALU.add))
            own.link(dve.tensor_tensor(sm[:, 10, :, :], sm[:, 9, :, :], sm[:, 5, :, :], ALU.subtract))
            for t in range(T):
                for i, one in enumerate([5, 10]):
                    own_or = dve.tensor_tensor(low[:, i, t, :].rearrange("p (e r) -> p e r", e=NE),
                                               low[:, 1, t, :].rearrange("p (e r) -> p e r", e=NE),
                                               sm[:, one, t, :].unsqueeze(2).to_broadcast([P, NE, RK]), ALU.mult)
                    own.did(own_or)
            own.wait()
            flat_low = low[:, :, :, :].rearrange("p i t k -> p (i t) k").unsqueeze(2).to_broadcast([P, 2 * T, 2, NLOW])
            own.link(dve.tensor_copy(packed[:, :, 0, :, :].bitcast(F32R), flat_low))
            dve.tensor_tensor(packed[:, :, 1, :, :], flat_low, packed[:, :, 0, :, :], ALU.subtract).then_inc(s["f_low"], 1)
            for i in range(2):
                for t in range(T):
                    dve.tensor_scalar(diag[:, i, t, :], ident[:, :], sc2[:, 3 + 2 * i, t:t + 1], None, ALU.mult).then_inc(s["f_wdiag"], 1)
            yield 8
            dve.wait_ge(s["f_wrow"], 1)
            for j in range(FC // 2):
                yield 8 + j
                for i, (ps, dst) in enumerate([("f_z1_ps", r1), ("f_z2_ps", r2)]):
                    dve.wait_ge(s[ps], j + 1)
                    if j >= 2:
                        dve.wait_ge(s["f_h"], j - 1)
                    dve.scalar_tensor_tensor(dst[:, j % 2, :, :], FB[j % 3][:, :].rearrange("p (a b) -> p a b", a=2), 0.0,
                                             wrow[:, i:i + 1, :].to_broadcast([P, 2, S]), ALU.max, ALU.mult).then_inc(s["f_r"], 1)
            yield 12
            dve.wait_ge(s["f_out_ps"], 1)
            own.link(dve.tensor_tensor(flat(x3[:, :, :]), b3[:, :], flat(x2[:, :, :]), ALU.add))
            stats(dve, own, x3, "f1")
            normal(dve, x3, x3, "f1")

        def f_pool(pool, own):
            yield 8
            for j in range(FC // 2):
                yield 8 + j
                pool.wait_ge(s["f_r"], 2 * j + 2)
                pool.tensor_tensor(flat(hT[:, 2 * j:2 * j + 2, :]), r1[:, j % 2, :, :].rearrange("p a b -> p (a b)"),
                                   r2[:, j % 2, :, :].rearrange("p a b -> p (a b)"), ALU.add).then_inc(s["f_h"], 1)
            yield 12
            rstd(pool, "f1")

        SB, TB, OB = [bank[3], bank[4]], [bank[5], bank[6]], bank[7]
        NH = NQ

        def t_pe(pe):
            b3, b4, b5, b6, b7 = bank[3:8]
            yield 13
            pe.wait_ge(s["f1_norm"], T)
            turn(pe, x3, b5, "t_xT_ps")
            yield 14
            pe.wait_ge(s["t_xT"], 1)

            def project(n):
                if n >= 2:
                    pe.wait_ge(s["t_proj"], n - 1)
                w, m = (w_k, n) if n < 2 else (w_q, n - 2)
                for i in range(2):
                    f = 2 * m + i
                    last = mm(pe, [b3, b5][n % 2][:, i * S:(i + 1) * S], [(w[:, k, f * P:(f + 1) * P], xT[:, k, :]) for k in range(KD)])
                last.then_inc(s["t_proj_ps"], 1)

            def swapped(n):
                pe.wait_ge(s["t_proj"], n + 1)
                if n >= 2:
                    pe.wait_ge(s["t_rot"], 2 * (n - 2) + 2)
                mm(pe, [b6, b7][n % 2][:, :], [(swap[:, :], flat(projected[n % 4]))]).then_inc(s["t_swap_ps"], 1)

            project(0)
            project(1)
            for t in range(T):
                last = mm(pe, b4[:, t * S:(t + 1) * S], [(xT[:, k, t * P:(t + 1) * P], w_v[:, k, :]) for k in range(KD)])
            last.then_inc(s["t_v_ps"], 1)
            swapped(0)
            for n in range(2, 6):
                yield 14 + (n - 1) // 3
                project(n)
                swapped(n - 1)
            swapped(5)
            yield 16
            pe.wait_ge(s["t_zero"], 3)
            pe.wait_ge(s["t_kz"], 4)
            pe.wait_ge(s["t_rot"], 12)
            pe.wait_ge(s["t_v"], 1)

            def scores(h):
                g, pair = h // GH, (h % GH) // 2
                if h % GH == 0:
                    pe.wait_ge(s["t_ro"], g + 1)
                if h >= 2:
                    pe.wait_ge(s["t_p"], 2 * (h - 1))
                for t in range(T):
                    last = pe.matmul(SB[h % 2][:, t * S:(t + 1) * S], qT[:, g, pair, t * P:(t + 1) * P], kz[h % 2][g],
                                     start=True, stop=True)
                last.then_inc(s["t_s_ps"], 1)

            def turned(h):
                pe.wait_ge(s["t_p"], 2 * h + 2)
                if h >= 2:
                    pe.wait_ge(s["t_pT"], h - 1)
                for k in range(2):
                    for t in range(T):
                        last = pe.transpose(TB[h % 2][:, k * S + t * P:k * S + (t + 1) * P], pe_[:, h % 2, t, k * P:(k + 1) * P], ident[:, :])
                last.then_inc(s["t_pT_ps"], 1)

            def values(h):
                g = h // GH
                pe.wait_ge(s["t_pT"], h + 1)
                if h >= 2 and h % 2 == 0:
                    pe.wait_ge(s["t_o"], h // 2)
                for t in range(T):
                    o = (t * 2 + h % 2) * (HD + 1)
                    for k in range(2):
                        last = pe.matmul(OB[:, o:o + HD + 1], pT[:, h % 2, k, t * P:(t + 1) * P], v1[:, k, g, :], start=(k == 0), stop=(k == 1))
                last.then_inc(s["t_o_ps"], 1)

            for i in range(NH + 3):
                yield 16 + i
                if i < NH:
                    scores(i)
                if 1 <= i <= NH:
                    turned(i - 1)
                if 3 <= i:
                    values(i - 3)
            yield 35
            pe.wait_ge(s["t_o"], NH // 2)
            for c in range(8):
                bk = [b3, b4, b5, b6][(c // 2) % 4]
                for t in range(T):
                    last = pe.transpose(bk[:, (c % 2) * S + t * P:(c % 2) * S + (t + 1) * P],
                                        ob[:, t, 2 * c:2 * c + 2, :].rearrange("p a b -> p (a b)"), ident[:, :])
                if c % 2 == 1:
                    last.then_inc(s["t_oT_ps"], 1)
            yield 36
            pe.wait_ge(s["t_oT"], 4)
            for t in range(T):
                last = mm(pe, b7[:, t * D:(t + 1) * D], [(oT[:, c, t * P:(t + 1) * P], w_ao[:, c, :]) for c in range(8)])
            last.then_inc(s["t_out_ps"], 1)

        def t_act(act, own):
            b3, b4, b5, b6, b7 = bank[3:8]
            yield 13
            act.wait_ge(s["t_xT_ps"], 1)
            act.activation(flat(xT[:, :, :]), b5[:, :], ACT.Copy).then_inc(s["t_xT"], 1)
            for n in range(6):
                yield 14 + n // 3
                act.wait_ge(s["t_proj_ps"], n + 1)
                if n >= 4:
                    act.wait_ge(s["t_rot"], 2 * (n - 4) + 2)
                act.activation(flat(projected[n % 4]), [b3, b5][n % 2][:, :], ACT.Copy).then_inc(s["t_proj"], 1)
                if n == 1:
                    act.wait_ge(s["t_v_ps"], 1)
                    act.activation(v1[:, :, :, 0:HD], b4[:, :].rearrange("p (t g d) -> p t g d", t=T, g=NKV), ACT.Copy).then_inc(s["t_v"], 1)
            yield 16
            act.wait_ge(s["t_ro"], 3)
            for i in range(NH + 1):
                yield 16 + i
                h = i
                if h < NH:
                    act.wait_ge(s["t_max"], h + 1)
                    if h >= 2:
                        act.wait_ge(s["t_pT_ps"], h - 1)
                    for t in range(T):
                        act.activation(pe_[:, h % 2, t, :], SB[h % 2][:, t * S:(t + 1) * S], ACT.Exp, bias=nmax[:, h % 4, t:t + 1]).then_inc(s["t_p"], 1)
                h = i - 1
                if h >= 0:
                    act.wait_ge(s["t_pT_ps"], h + 1)
                    if h == 0:
                        act.wait_ge(s["t_ro"], NKV)
                    if h >= 2:
                        act.wait_ge(s["t_o_ps"], h - 1)
                    act.activation(pT[:, h % 2, :, :].rearrange("p a b -> p (a b)"), TB[h % 2][:, :], ACT.Copy).then_inc(s["t_pT"], 1)
            yield 35
            for j in range(4):
                act.wait_ge(s["t_oT_ps"], j + 1)
                act.activation(flat(oT[:, 2 * j:2 * j + 2, :]), [b3, b4, b5, b6][j][:, :], ACT.Copy).then_inc(s["t_oT"], 1)

        def t_dve(dve, own):
            b3, b4, b5, b6, b7 = bank[3:8]
            yield 13
            dve.wait_ge(s["f_out_ps"], 1)
            dve.memset(heads[HD:P, 0:4, :], 0.0).then_inc(s["t_zero"], 1)
            dve.memset(cxT[0:HD, :, :], 0.0).then_inc(s["t_zero"], 1)
            dve.memset(x2[0:HD, :, :], 0.0).then_inc(s["t_zero"], 1)
            yield 14

            for n in range(6):
                yield 14 + n // 3
                table = 0 if n < 2 else 2
                both = [P, 2, S]
                dve.wait_ge(s["t_proj"], n + 1)
                if n >= 2:
                    if n < 4:
                        dve.wait_ge(s["t_kz"], 2 * (n - 2) + 2)
                    else:
                        dve.wait_ge(s["t_ro"], n - 3)
                dve.tensor_tensor(rot[n % 2][:, 0, :, :], projected[n % 4], cs[:, table:table + 1, :].to_broadcast(both),
                                  ALU.mult).then_inc(s["t_rot"], 1)
                dve.wait_ge(s["t_swap_ps"], n + 1)
                dve.tensor_tensor(rot[n % 2][:, 1, :, :], [b6, b7][n % 2][:, :].rearrange("p (a b) -> p a b", a=2),
                                  cs[:, table + 1:table + 2, :].to_broadcast(both), ALU.mult).then_inc(s["t_rot"], 1)
                if n < 2:
                    dve.wait_ge(s["t_rot"], 2 * n + 2)
                    for dst, half in [(heads[:, 2 * n:2 * n + 2, :], slice(0, HD)), ([cxT[:, :, :], x2[:, :, :]][n], slice(HD, P))]:
                        dve.tensor_tensor(dst[half], rot[n % 2][half, 0, :, :], rot[n % 2][half, 1, :, :], ALU.add).then_inc(s["t_kz"], 1)

            def weigh(p):
                dve.wait_ge(s["t_o_ps"], 2 * p + 2)
                if p >= 2:
                    dve.wait_ge(s["t_o"], p - 1)
                o = OB[:, 0:4 * (HD + 1)].rearrange("p (t h d) -> p t h d", t=T, h=2)
                own.link(dve.reciprocal(rs[:, p % 2, :, :], o[:, :, :, HD]))
                dve.tensor_tensor(ob[:, :, 2 * p:2 * p + 2, :], o[:, :, :, 0:HD],
                                  rs[:, p % 2, :, :].unsqueeze(3).to_broadcast([P, T, 2, HD]), ALU.mult).then_inc(s["t_o"], 1)

            for i in range(NH + 3):
                yield 16 + i
                if i < NH:
                    dve.wait_ge(s["t_s_ps"], i + 1)
                    if i >= 4:
                        dve.wait_ge(s["t_p"], 2 * (i - 3))
                    dve.tensor_reduce(nmax[:, i % 4, :], SB[i % 2][:, :].rearrange("p (t k) -> p t k", t=T), AX, ALU.max,
                                      negate=True).then_inc(s["t_max"], 1)
                if i >= 4 and i % 2 == 0:
                    weigh((i - 4) // 2)
            yield 36
            dve.wait_ge(s["t_out_ps"], 1)
            own.link(dve.tensor_tensor(flat(x4[:, :, :]), b7[:, :], flat(x3[:, :, :]), ALU.add))
            stats(dve, own, x4, "t1")
            normal(dve, x4, x4, "t1")

        def t_pool(pool, own):
            yield 14
            for n in range(2, 6):
                yield 14 + n // 3
                pool.wait_ge(s["t_rot"], 2 * n + 2)
                pool.tensor_tensor(qT[:, n - 2, :, :], rot[n % 2][:, 0, :, :], rot[n % 2][:, 1, :, :], ALU.add).then_inc(s["t_ro"], 1)
            yield 36
            rstd(pool, "t1")

        def c_pe(pe):
            b3, b4, b5, b6, b7 = bank[3:8]
            yield 38
            pe.wait_ge(s["c2_norm"], T)
            for t in range(T):
                pe.transpose(b6[:, t * P:(t + 1) * P], x2n[:, t, 0:P], ident[:, :])
            for t in range(T):
                last = pe.transpose(b6[0:CTX2, S + t * P:S + (t + 1) * P], x2n[:, t, P:CTX], ident[:, :])
            last.then_inc(s["c_x2T_ps"], 1)
            yield 39
            pe.wait_ge(s["c_x2T"], 2)
            for e in range(2):
                last = mm(pe, b4[:, e * S:(e + 1) * S], [(w_k1[:, 0, e * P:(e + 1) * P], x2T[:, 0, :]),
                                                        (w_k1[0:CTX2, 1, e * P:(e + 1) * P], x2T[0:CTX2, 1, :])])
            last.then_inc(s["c_k_ps"], 1)
            for t in range(T):
                last = mm(pe, b3[:, t * E2:(t + 1) * E2], [(x2T[:, 0, t * P:(t + 1) * P], w_v1[:, 0, :]),
                                                          (x2T[0:CTX2, 1, t * P:(t + 1) * P], w_v1[0:CTX2, 1, :])])
            last.then_inc(s["c_v_ps"], 1)
            yield 40
            pe.wait_ge(s["c_norm"], T)
            turn(pe, x1n, b5, "c_xT_ps")
            yield 41
            pe.wait_ge(s["c_xT"], 2)
            for e in range(2):
                last = mm(pe, b6[:, e * S:(e + 1) * S], [(w_q1[:, k, e * P:(e + 1) * P], xT[:, k, :]) for k in range(KD)])
            last.then_inc(s["c_q_ps"], 1)
            yield 42
            pe.wait_ge(s["c_q"], 2)
            pe.wait_ge(s["c_k"], 2)
            for t in range(T):
                last = mm(pe, b7[:, t * S:(t + 1) * S], [(q1[:, e, t * P:(t + 1) * P], k1[:, e, :]) for e in range(2)])
            last.then_inc(s["c_s_ps"], 1)
            yield 43
            pe.wait_ge(s["c_p"], 2)
            for k in range(2):
                for t in range(T):
                    last = pe.transpose(b5[:, k * S + t * P:k * S + (t + 1) * P], pe_[:, 0, t, k * P:(k + 1) * P], ident[:, :])
            last.then_inc(s["c_pT_ps"], 1)
            yield 44
            pe.wait_ge(s["c_pT"], 1)
            pe.wait_ge(s["c_v"], 1)
            for e in range(2):
                last = mm(pe, b3[:, e * S:(e + 1) * S], [(v1x[:, k, e * P:(e + 1) * P], pT[:, 0, k, :]) for k in range(2)])
            last.then_inc(s["c_ctx_ps"], 1)
            yield 45
            pe.wait_ge(s["c_ctx"], 1)
            for t in range(T):
                last = mm(pe, b4[:, t * D:(t + 1) * D], [(cT[:, e, t * P:(t + 1) * P], w_o1[:, e, :]) for e in range(2)])
            last.then_inc(s["c_out_ps"], 1)

        def c_act(act, own):
            b3, b4, b5, b6, b7 = bank[3:8]
            yield 38
            act.wait_ge(s["c_x2T_ps"], 1)
            act.activation(x2T[:, 0, :], b6[:, 0:S], ACT.Identity, bias=ln2_b[:, 0:1], scale=ln2_g[:, 0:1]).then_inc(s["c_x2T"], 1)
            act.activation(x2T[0:CTX2, 1, :], b6[0:CTX2, S:2 * S], ACT.Identity, bias=ln2_b[0:CTX2, 1:2],
                           scale=ln2_g[0:CTX2, 1:2]).then_inc(s["c_x2T"], 1)
            yield 39
            act.wait_ge(s["c_k_ps"], 1)
            for e in range(2):
                act.activation(k1[:, e, :], b4[:, e * S:(e + 1) * S], ACT.Identity, bias=b_k1[:, e:e + 1]).then_inc(s["c_k"], 1)
            yield 40
            act.wait_ge(s["c_xT_ps"], 1)
            for k in range(KD):
                act.activation(xT[:, k, :], b5[:, k * S:(k + 1) * S], ACT.Identity, bias=ln1_b[:, k:k + 1],
                               scale=ln1_g[:, k:k + 1]).then_inc(s["c_xT"], 1)
            yield 41
            act.wait_ge(s["c_q_ps"], 1)
            for e in range(2):
                act.activation(q1[:, e, :], b6[:, e * S:(e + 1) * S], ACT.Identity, bias=b_q1s[:, e:e + 1],
                               scale=1.0 / 16.0).then_inc(s["c_q"], 1)
            yield 42
            act.wait_ge(s["c_max"], 1)
            for t in range(T):
                act.activation(pe_[:, 0, t, :], b7[:, t * S:(t + 1) * S], ACT.Exp, bias=nmax[:, 0, t:t + 1],
                               accum_out=sums[:, t:t + 1]).then_inc(s["c_p"], 1)
            yield 43
            act.wait_ge(s["c_pT_ps"], 1)
            act.activation(pT[:, 0, :, :].rearrange("p a b -> p (a b)"), b5[:, :], ACT.Copy).then_inc(s["c_pT"], 1)
            yield 44
            act.wait_ge(s["c_ctx_ps"], 1)
            act.activation(flat(cT[:, :, :]), b3[:, :], ACT.Copy).then_inc(s["c_ctx"], 1)

        def c_dve(dve, own):
            b3, b4, b5, b6, b7 = bank[3:8]
            yield 37
            stats(dve, own, cx, "c2")
            normal(dve, cx, x2n, "c2")
            dve.wait_ge(s["t1_norm"], T)
            stats(dve, own, x4, "c")
            normal(dve, x4, x1n, "c")
            yield 40
            dve.wait_ge(s["c_v_ps"], 1)
            dve.tensor_tensor(v1x[:, :, :], b3[:, :].rearrange("p (t e) -> p t e", t=T),
                              b_v1[:, :].unsqueeze(1).to_broadcast([P, T, E2]), ALU.add).then_inc(s["c_v"], 1)
            yield 42
            dve.wait_ge(s["c_s_ps"], 1)
            dve.tensor_reduce(nmax[:, 0, :], b7[:, :].rearrange("p (t k) -> p t k", t=T), AX, ALU.max, negate=True).then_inc(s["c_max"], 1)
            dve.wait_ge(s["c_p"], 2)
            own.link(dve.reciprocal(rsum[:, :], sums[:, :]))
            yield 45
            dve.wait_ge(s["c_out_ps"], 1)
            dve.wait_ge(s["c_x4b"], 1)
            for t in range(T):
                last = dve.scalar_tensor_tensor(x5[:, t, :], b4[:, t * D:(t + 1) * D], rsum[:, t:t + 1], x4b[:, t, :], ALU.mult, ALU.add)
                if t == T - 1:
                    last.then_inc(s["c_res"], 1)
                else:
                    own.did(last)
            own.wait()
            dve.wait_ge(s["c_res"], 1)
            stats(dve, own, x5, "c1")
            normal(dve, x5, x5, "c1")

        def c_pool(pool, own):
            yield 37
            rstd(pool, "c2")
            rstd(pool, "c")
            pool.wait_ge(s["t1_norm"], T)
            pool.tensor_tensor(x4b[:, :, :], x4[:, :, :], b_o1[:, :].unsqueeze(1).to_broadcast([P, T, D]), ALU.add).then_inc(s["c_x4b"], 1)
            yield 45
            rstd(pool, "c1")

        GB = [bank[3], bank[4], bank[6]]

        def l_pe(pe):
            b3, b4, b5, b6, b7 = bank[3:8]
            yield 46
            pe.wait_ge(s["c_res"], 1)
            for g in range(3):
                for m in range(KD):
                    for k in range(KD):
                        last = pe.matmul(GB[g][:, m * S:(m + 1) * S], u_g[:, g, k, m * P:(m + 1) * P], state[:, k, :],
                                         start=(m == 0 and k == 0), stop=False, skip_group_check=True)
            last.then_inc(s["l_u_ps"], 1)
            pe.wait_ge(s["c1_norm"], T)
            turn(pe, x5, b5, "l_xT_ps")
            yield 47
            pe.wait_ge(s["l_xT"], 1)
            for g in range(3):
                for m in range(KD):
                    for k in range(KD):
                        last = pe.matmul(GB[g][:, m * S:(m + 1) * S], w_g[:, g, k, m * P:(m + 1) * P], xT[:, k, :],
                                         start=False, stop=(k == KD - 1), skip_group_check=True)
                last.then_inc(s["l_g_ps"], 1)
            yield 48
            for t in range(T):
                last = mm(pe, b7[:, t * D:(t + 1) * D], [(xT[:, k, t * P:(t + 1) * P], w_ho[:, k, :]) for k in range(KD)])
            last.then_inc(s["l_xw_ps"], 1)

        def l_act(act, own, b):
            b3, b4, b5, b6, b7 = bank[3:8]
            yield 46
            act.wait_ge(s["l_xT_ps"], 1)
            act.activation(flat(xT[:, :, :]), b5[:, :], ACT.Copy).then_inc(s["l_xT"], 1)
            yield 47
            for g in range(3):
                act.wait_ge(s["l_g_ps"], g + 1)
                for m in range(KD):
                    act.activation(tg[:, g, m, :], GB[g][:, m * S:(m + 1) * S], ACT.Tanh, bias=b_gh[:, g, m:m + 1],
                                   scale=1.0 if g == 2 else 0.5).then_inc(s["l_tanh"], 1)
            yield 48
            act.wait_ge(s["l_xw_ps"], 1)
            act.activation(xw[:, :], b7[:, :], ACT.Copy).then_inc(s["l_xw"], 1)

        def l_dve(dve, own):
            yield 47
            dve.wait_ge(s["l_tanh"], 2)
            own.did(dve.scalar_tensor_tensor(flat(ug[:, 0, :, :]), flat(tg[:, 0, :, :]), 1.0, flat(state[:, :, :]), ALU.add, ALU.mult))
            dve.wait_ge(s["l_tanh"], 6)
            own.link(dve.scalar_tensor_tensor(flat(ug[:, 1, :, :]), flat(tg[:, 1, :, :]), 1.0, flat(tg[:, 2, :, :]), ALU.add, ALU.mult))
            dve.wait_ge(s["l_u_ps"], 1)
            dve.scalar_tensor_tensor(flat(state[:, :, :]), flat(ug[:, 0, :, :]), 0.5, flat(ug[:, 1, :, :]), ALU.mult, ALU.add).then_inc(s["l_state"], 1)

        def l_sp(sp, b):
            yield 46
            sp.wait_ge(s["c1_norm"], T)
            sp.dma_start(kept_x[bass.ds(b, 1), :, :].rearrange("a p n -> p (a n)"), flat(x5[:, :, :])).then_inc(s["l_kept"], 16)
            yield 48
            sp.wait_ge(s["l_xw"], 1)
            sp.dma_start(kept_w[bass.ds(b, 1), :, :].rearrange("a p n -> p (a n)"), xw[:, :]).then_inc(s["l_kept"], 16)
            sp.wait_ge(s["l_kept"], 32)

        FOLDS = []
        for k in range(KD):
            for j in range(2):
                FOLDS.append((w_q[:, k, j * 512:(j + 1) * 512], lora_a[:, 0, k * P:(k + 1) * P], qb[:, j * 512:(j + 1) * 512]))
            FOLDS.append((w_k[:, k, :], lora_a[:, 1, k * P:(k + 1) * P], kb[:, :]))
            FOLDS.append((w_v[:, k, :], lora_a[:, 2, k * P:(k + 1) * P], vb[:, :]))
        for c in range(8):
            FOLDS.append((w_ao[:, c, :], lora_ao[:, c * P:(c + 1) * P], obm[:, :]))

        def whole(x):
            return x if isinstance(x, bass.AP) else x[tuple([slice(None)] * len(x.shape))]

        FIRST = [(w_in, "w_in"), (w_xp, "w_xp"), (w_out, "w_out"), (conv_w, "conv_w"), (conv_b, "conv_b"), (ln_g, "ln_g"), (ln_b, "ln_b"),
                 (w_dt, "w_dt"), (b_dt, "b_dt"), (a_log, "a_log"), (d_skip, "d_skip")]
        REST = [(whole(x), name) for x, name in [
            (wv0, "wv0"), (bv0, "bv0"), (wt0[:, 0, :], "wt0a"), (wt0[0:CTX2, 1, :], "wt0b"), (bt0, "bt0"), (w_gl, "w_gl"), (part, "part"),
            (w_i, "w_i"), (w_o, "w_o"), (prio, "prio"), (w_q, "w_q"), (w_k, "w_k"), (w_v, "w_v"), (w_ao, "w_ao"),
            (lora_a, "lora_a"), (lora_ao, "lora_ao"), (qb, "qb"), (kb, "kb"), (vb, "vb"), (obm, "ob"), (cs, "cs"), (swap, "swap"),
            (ln1_g, "ln1_g"), (ln1_b, "ln1_b"), (ln2_g[:, 0:1], "ln2_ga"), (ln2_g[0:CTX2, 1:2], "ln2_gb"),
            (ln2_b[:, 0:1], "ln2_ba"), (ln2_b[0:CTX2, 1:2], "ln2_bb"),
            (w_q1, "w_q1"), (w_k1[:, 0, :], "w_k1a"), (w_k1[0:CTX2, 1, :], "w_k1b"), (w_v1[:, 0, :], "w_v1a"), (w_v1[0:CTX2, 1, :], "w_v1b"),
            (w_o1, "w_o1"), (b_q1, "b_q1"), (b_k1, "b_k1"), (w_g, "w_g"), (u_g, "u_g"), (b_g, "b_g"), (w_ho, "w_ho"), (u_ho, "u_ho"),
            (in_c, "in_c")]]
        REST += [(turns[NLOW * i:NLOW * (i + 1), 0:4, :].rearrange("p a b -> p (a b)"), "w_b") for i in range(PARTS)]
        ROWS = [(b_gl, "b_gl"), (b_v1, "b_v1"), (b_o1, "b_o1"), (b_ho, "b_ho")]
        N_FIRST, N_REST = 16 * len(FIRST), 16 * (len(REST) + len(ROWS))

        def ended(eng, n):
            eng.drain().then_inc(arrived, 1)
            eng.wait_ge(phase, n)

        def next_phase(sp):
            sp.wait_ge(arrived, 4)
            sp.sem_clear(range(numbers[0], numbers[-1] + 1))
            sp.sem_clear(arrived)
            sp.sem_inc(phase, 1)

        def merged(order, mamba, rest):
            streams = {"A": chained(mamba), "B": chained(rest)}
            at = {k: next(g, 999) for k, g in streams.items()}
            for name, unit in order:
                while at[name] <= unit:
                    at[name] = next(streams[name], 999)

        def chained(parts):
            for g in parts:
                yield from g

        ONLY_A = [("A", u) for u in range(NA)]
        ONLY_B = [("B", u) for u in range(NB_UNITS)]

        def program(eng, parts_a, parts_b):
            with eng.Fori(0, NB - 1) as b:
                merged(ORDER, parts_a(b + 1), parts_b(b))
                ended(eng, b + 2)
            merged(ONLY_B, [], parts_b(NB - 1))
            ended(eng, NB + 1)

        block = ctx.enter_context(nc.Block())

        @block.sync
        def _(sp):
            for dst, name in FIRST:
                sp.dma_start(dst[tuple([slice(None)] * len(dst.shape))], A[name]).then_inc(s["loads_mamba"], 16)
            gen = a_sp(sp, 0)
            next(gen)
            next(gen)
            load_context(sp, 0)
            for dst, name in REST:
                sp.dma_start(dst, A[name]).then_inc(s["loads_rest"], 16)
            for dst, name in ROWS:
                sp.dma_start(dst[:, :], A[name].partition_broadcast(P)).then_inc(s["loads_rest"], 16)
            for _ in gen:
                pass
            sp.wait_ge(s["b_ctx"], 16)
            next_phase(sp)
            with sp.Fori(0, NB - 1) as b:
                merged(ORDER, [a_sp(sp, b + 1)], [r_sp(sp, b + 1), l_sp(sp, b)])
                sp.wait_ge(s["b_ctx"], 16)
                next_phase(sp)
            merged(ONLY_B, [], [l_sp(sp, NB - 1)])
            next_phase(sp)
            for n in range(2):
                rows = slice(4 * n, 4 * n + 4)
                sp.dma_start(XW[:, rows, :], kept_w[rows, :, :].rearrange("b p n -> p b n")).then_inc(s[f"e_load_w{n}"], 16)
                sp.dma_start(XS[:, rows, :], kept_x[rows, :, :].rearrange("b p n -> p b n")).then_inc(s[f"e_load_x{n}"], 16)
            out_v = out.rearrange("b (t p) d -> p (b t) d", p=P)
            for b in range(NB):
                sp.wait_ge(s["e_norm"], 2 * b + 2)
                sp.dma_start(out_v[:, 2 * b:2 * b + 2, :], XS[:, b, :].rearrange("p (t d) -> p t d", t=T)).then_inc(s["e_store"], 16)
            sp.wait_ge(s["e_store"], 16 * NB)

        @block.gpsimd
        def _(pool):
            own = Own(pool, s["pool_own"])
            own.did(pool.memset(ident[:, :], 0.0))
            own.did(pool.memset(neghalf[:, :], -0.5))
            pool.memset(ones[:, :], 1.0).then_inc(s["prep_pool"], 1)
            for i in range(2):
                pool.memset(dA[i][:, :, 0:1], 0.0).then_inc(s["prep_pool"], 1)
            pool.memset(v1[:, :, :, HD:HD + 1], 1.0).then_inc(s["prep_pool"], 1)
            own.wait()
            pool.affine_select(out=ident[:, :], in_=ident[:, :], compare_op=ALU.not_equal, fill=1.0, base=0, pattern=[[-1, P]],
                               channel_multiplier=1).then_inc(s["prep_pool"], 1)
            merged(ONLY_A, [a_pool(pool, own)], [])
            ended(pool, 1)

            def parts_a(b):
                return [a_pool(pool, Own(pool, s["pool_own"]))]

            def parts_b(b):
                own = Own(pool, s["pool_own"])
                return [b_pool(pool, own), f_pool(pool, own), t_pool(pool, own), c_pool(pool, own)]

            program(pool, parts_a, parts_b)
            pool.wait_ge(s["e_var"], 1)
            pool.tensor_tensor(e_rs[:, :], e_var[:, :], neghalf[:, :], ALU.pow).then_inc(s["e_rstd"], 1)

        @block.scalar
        def _(act):
            own = Own(act, s["act_own"])
            act.wait_ge(s["loads_mamba"], N_FIRST)
            act.activation(flat(a_neg[:, :, :]), flat(a_log[:, :, :]), ACT.Exp).then_inc(s["prep_act"], 1)
            act.wait_ge(s["prep_act"], 1)
            act.activation(flat(a_neg[:, :, :]), flat(a_neg[:, :, :]), ACT.Copy, scale=-1.0).then_inc(s["prep_act"], 1)
            act.wait_ge(s["prep_act"], 2)
            act.wait_ge(s["prep_halves"], 3)
            act.wait_ge(s["prep_pool"], 3)
            merged(ONLY_A, [a_act(act, own)], [])
            ended(act, 1)
            program(act, lambda b: [a_act(act, Own(act, s["act_own"]))],
                    lambda b: [b_act(act, None), f_act(act, None), t_act(act, None), c_act(act, None), l_act(act, None, b)])
            for i in range(2):
                act.wait_ge(s["e_sum"], i + 1)
                act.activation(flat(XW[:, 4 * i:4 * i + 4, :]), flat(XW[:, 4 * i:4 * i + 4, :]), ACT.Tanh).then_inc(s["e_tanh"], 1)

        @block.vector
        def _(dve):
            own = Own(dve, s["dve_own"])
            dve.wait_ge(s["loads_mamba"], N_FIRST)
            dve.tensor_scalar(flat(conv_wh[:, :, :]), flat(conv_w[:, :, :]), 0.5, None, ALU.mult).then_inc(s["prep_halves"], 1)
            dve.tensor_scalar(conv_bh[:, :], conv_b[:, :], 0.5, None, ALU.mult).then_inc(s["prep_halves"], 1)
            dve.tensor_scalar(w_in[:, :, DI:], w_in[:, :, DI:], 0.5, None, ALU.mult).then_inc(s["prep_halves"], 1)
            dve.wait_ge(s["prep_halves"], 3)
            merged(ONLY_A, [a_dve(dve, own)], [])
            dve.wait_ge(s["loads_rest"], N_REST)
            own.did(dve.tensor_scalar(b_q1s[:, :], b_q1[:, :], 1.0 / 16.0, None, ALU.mult))
            own.did(dve.tensor_scalar(flat(b_gh[:, 0:2, :]), flat(b_g[:, 0:2, :]), 0.5, None, ALU.mult))
            own.did(dve.tensor_copy(b_gh[:, 2, :], b_g[:, 2, :]))
            own.did(dve.tensor_scalar(u_g[:, :, :, :].rearrange("p a b c -> p (a b c)"), u_g[:, :, :, :].rearrange("p a b c -> p (a b c)"),
                                      0.5, None, ALU.mult))
            own.did(dve.tensor_scalar(flat(u_ho[:, :, :]), flat(u_ho[:, :, :]), 0.5, None, ALU.mult))
            own.link(dve.memset(state[:, :, :], 2.0))
            for k in range(KD):
                own.did(dve.tensor_scalar(state[:, k, :], state[:, k, :], in_c[:, k:k + 1], None, ALU.mult))
            whole_b, high_b = [turns[0:NPACK, 4 * i:4 * i + 4, :].rearrange("p a b -> p (a b)") for i in range(2)]
            own.link(dve.tensor_copy(high_b.bitcast(F32R), whole_b))
            own.link(dve.tensor_scalar(whole_b, whole_b, part[:, 0:1], None, ALU.mult))
            own.did(dve.scalar_tensor_tensor(w_b[:, :], high_b, part[:, 1:2], whole_b, ALU.mult, ALU.add))
            for n, (dst, _, _) in enumerate(FOLDS):
                dve.wait_ge(s["prep_pe"], n + 1)
                dve.scalar_tensor_tensor(dst, bank[3 + n % 2][:, 0:dst.shape[1]], LSCALE, dst, ALU.mult, ALU.add).then_inc(s["prep_evac"], 1)
            ended(dve, 1)
            with dve.Fori(0, NB - 1) as b:
                own = Own(dve, s["dve_own"])
                merged(ORDER, [a_dve(dve, own)], [b_dve(dve, own), f_dve(dve, own), t_dve(dve, own), c_dve(dve, own), l_dve(dve, own)])
                ended(dve, b + 2)
            own = Own(dve, s["dve_own"])
            merged(ONLY_B, [], [b_dve(dve, own), f_dve(dve, own), t_dve(dve, own), c_dve(dve, own), l_dve(dve, own)])
            ended(dve, NB + 1)
            own = Own(dve, s["dve_own"])
            dve.wait_ge(s["e_cu_ps"], 1)
            own.link(dve.tensor_tensor(cu[:, :].rearrange("p (t d) -> p t d", t=T), bank[0][:, :].rearrange("p (t d) -> p t d", t=T),
                                       b_ho[:, :].unsqueeze(1).to_broadcast([P, T, D]), ALU.add))
            for i in range(2):
                dve.wait_ge(s[f"e_load_w{i}"], 16)
                dve.tensor_tensor(XW[:, 4 * i:4 * i + 4, :], XW[:, 4 * i:4 * i + 4, :], cu[:, :].unsqueeze(1).to_broadcast([P, 4, T * D]),
                                  ALU.add).then_inc(s["e_sum"], 1)
            for i in range(2):
                dve.wait_ge(s["e_tanh"], i + 1)
                dve.wait_ge(s[f"e_load_x{i}"], 16)
                own.link(dve.tensor_tensor(flat(XS[:, 4 * i:4 * i + 4, :]), flat(XS[:, 4 * i:4 * i + 4, :]), flat(XW[:, 4 * i:4 * i + 4, :]), ALU.add))
                for r in range(8 * i, 8 * i + 8):
                    own.did(dve.bn_stats(e_st[:, r, :], XS[:, r // 2, (r % 2) * D:(r % 2 + 1) * D]))
            own.wait()
            for r in range(NB * T):
                own.did(dve.bn_aggr(e_mv[:, r, :], e_st[:, r, :]))
            own.wait()
            dve.tensor_scalar(e_var[:, :], e_mv[:, :, 1], EPS, None, ALU.add).then_inc(s["e_var"], 1)
            dve.wait_ge(s["e_rstd"], 1)
            for r in range(NB * T):
                x = XS[:, r // 2, (r % 2) * D:(r % 2 + 1) * D]
                dve.tensor_scalar(x, x, e_mv[:, r, 0:1], e_rs[:, r:r + 1], ALU.subtract, ALU.mult).then_inc(s["e_norm"], 1)

        @block.tensor
        def _(pe):
            pe.wait_ge(s["prep_pool"], 5)
            pe.wait_ge(s["prep_halves"], 3)
            merged(ONLY_A, [a_pe(pe)], [])
            pe.wait_ge(s["loads_rest"], N_REST)
            for n, (dst, l, r) in enumerate(FOLDS):
                if n >= 2:
                    pe.wait_ge(s["prep_evac"], n - 1)
                pe.matmul(bank[3 + n % 2][:, 0:dst.shape[1]], l, r, start=True, stop=True).then_inc(s["prep_pe"], 1)
            ended(pe, 1)
            program(pe, lambda b: [a_pe(pe)], lambda b: [b_pe(pe), f_pe(pe), t_pe(pe), c_pe(pe), l_pe(pe)])
            for t in range(T):
                last = mm(pe, bank[0][:, t * D:(t + 1) * D], [(state[:, k, t * P:(t + 1) * P], u_ho[:, k, :]) for k in range(KD)])
            last.then_inc(s["e_cu_ps"], 1)


def arrays_of(i):
    def t(a):
        return np.ascontiguousarray(a)

    def kp(a):
        return t(a.reshape(-1, P, a.shape[1]).transpose(1, 0, 2))

    def cp(a):
        return t(a.reshape(-1, P).T)

    def eo(a, heads):
        return t(a.reshape(heads, HH, 2, -1).transpose(0, 2, 1, 3).reshape(heads * HD, -1))

    def twice(a):
        return t(np.repeat(a.reshape(NKV, 1, HD, -1), 2, axis=1).reshape(2 * NKV * HD, -1))

    xp = i["L0_attn_W_xp"]
    wt = i["L0_xattn_Wt"].T
    g2, b2 = i["L1_xattn_ln2_g"], i["L1_xattn_ln2_b"]
    f = [i[f"L1_ffn_{n}"].T for n in ("wf", "wi", "wc")]
    u = [i[f"L1_ffn_{n}"].T for n in ("uf", "ui", "uc")]
    inv = (np.float32(1.0) / np.float32(10000.0) ** (np.arange(0, HD, 2, dtype=np.float32) / np.float32(HD))).astype(np.float32)
    ang = (np.arange(S, dtype=np.float32)[:, None] * inv[None, :]).astype(np.float32).T.astype(np.float64)
    co, si = np.cos(ang).astype(np.float32), np.sin(ang).astype(np.float32)
    co, si = np.concatenate([co, co]), np.concatenate([-si, si])
    cs = np.stack([co, si, co / np.float32(8), si / np.float32(8)], axis=1)
    swap = np.eye(P, dtype=np.float32)[np.arange(P) ^ HH]
    return {
        "x": i["x"], "ctx": i["ctx_768"],
        "w_in": kp(i["L0_attn_W_in"]), "w_xp": kp(xp), "w_out": kp(i["L0_attn_W_out"]),
        "conv_w": kp(i["L0_attn_conv_w"]), "conv_b": cp(i["L0_attn_conv_b"]), "ln_g": cp(i["L0_attn_ln_g"]), "ln_b": cp(i["L0_attn_ln_b"]),
        "w_dt": cp(i["L0_attn_W_dt"][0]), "b_dt": cp(i["L0_attn_b_dt"]), "a_log": kp(i["L0_attn_A_log"]), "d_skip": cp(i["L0_attn_D"]),
        "wv0": kp(t(i["L0_xattn_Wv"].T)), "bv0": cp(i["L0_xattn_bv"]), "wt0a": t(wt[:P]), "wt0b": t(wt[P:]), "bt0": cp(i["L0_xattn_bt"]),
        "w_gl": kp(t(np.concatenate([i["L0_ffn_Wg"].T, i["L0_ffn_A"].reshape(NLOW, D).T], axis=1))),
        "b_gl": t(i["L0_ffn_bg"]), "w_b": t(i["L0_ffn_B"].transpose(0, 2, 1).reshape(NLOW, FF)),
        "w_i": kp(t(i["L0_ffn_Wi"].T)), "w_o": kp(t(i["L0_ffn_Wo"].T)),
        "part": np.repeat(np.array([[0, 1], [1, -1], [0, 1], [1, -1]], dtype=np.float32), NLOW, axis=0),
        "prio": np.tile(np.arange(NE, 0, -1, dtype=np.float32), (P, 1)),
        "w_q": kp(t(eo(i["L1_attn_Wq"], NQ).T)), "w_k": kp(t(twice(eo(i["L1_attn_Wk"], NKV)).T)), "w_v": kp(t(i["L1_attn_Wv"].T)),
        "w_ao": kp(t(i["L1_attn_Wo"].T)), "lora_a": t(np.stack([i["L1_attn_qA"], i["L1_attn_kA"], i["L1_attn_vA"]], axis=1)),
        "lora_ao": i["L1_attn_oA"], "qb": t(eo(i["L1_attn_qB"], NQ).T), "kb": t(twice(eo(i["L1_attn_kB"], NKV)).T), "vb": t(i["L1_attn_vB"].T),
        "ob": t(i["L1_attn_oB"].T), "cs": t(np.tile(cs, (2, 1, 1))), "swap": t(swap),
        "ln1_g": cp(i["L1_xattn_ln1_g"]), "ln1_b": cp(i["L1_xattn_ln1_b"]),
        "ln2_ga": t(g2[:P, None]), "ln2_gb": t(g2[P:, None]), "ln2_ba": t(b2[:P, None]), "ln2_bb": t(b2[P:, None]),
        "w_q1": kp(i["L1_xattn_Wq"]), "w_k1a": t(i["L1_xattn_Wk"][:P]), "w_k1b": t(i["L1_xattn_Wk"][P:]),
        "w_v1a": t(i["L1_xattn_Wv"][:P]), "w_v1b": t(i["L1_xattn_Wv"][P:]), "w_o1": kp(i["L1_xattn_Wo"]),
        "b_q1": cp(i["L1_xattn_bq"]), "b_k1": cp(i["L1_xattn_bk"]), "b_v1": i["L1_xattn_bv"], "b_o1": i["L1_xattn_bo"],
        "w_g": t(np.stack([kp(t(a)) for a in f], axis=1)), "u_g": t(np.stack([kp(t(a)) for a in u], axis=1)),
        "b_g": t(np.stack([cp(i[f"L1_ffn_{n}"]) for n in ("bf", "bi", "bc")], axis=1)),
        "w_ho": kp(t(i["L1_ffn_wo"].T)), "u_ho": kp(t(i["L1_ffn_uo"].T)), "b_ho": i["L1_ffn_bo"], "in_c": cp(i["L1_ffn_in_c"]),
    }


def kernel(**inputs):
    import concourse.bacc as _bacc
    from concourse.bass_utils import run_bass_kernel_spmd as _run

    nc = _bacc.Bacc("TRN2", target_bir_lowering=False, num_devices=1)
    arrays = {f"in_{k}": np.ascontiguousarray(v) for k, v in arrays_of({k: np.asarray(v) for k, v in inputs.items()}).items()}
    A = {k[3:]: nc.dram_tensor(k, v.shape, F32, kind="ExternalInput").ap() for k, v in arrays.items()}
    out = nc.dram_tensor("out", (NB, S, D), F32, kind="ExternalOutput").ap()
    build(nc, A, out)
    r = _run(nc, [arrays], core_ids=[0])
    return r.results[0]["out"]
```

```python
from contextlib import ExitStack

import numpy as np

import concourse.bass as bass
from concourse import mybir

F32 = mybir.dt.float32
F32R = mybir.dt.float32r
ALU = mybir.AluOpType
ACT = mybir.ActivationFunctionType
AX = mybir.AxisListType.X

P = 128
NB, S, D = 8, 256, 256
T = S // P
KD = D // P
CTX = 192
CTX2 = CTX - P
DI, NS, TAPS = 512, 16, 4
EC = DI // P
HN = 4
VH = 128
NE, RK = 4, 4
NLOW = NE * RK
PARTS = 4
NPACK = PARTS * NLOW
FF = 1024
FC = FF // P
NQ, NKV, HD = 16, 4, 64
GH = NQ // NKV
HH = HD // 2
LORA = 8
LSCALE = 2.0
E2 = 256
EPS = 1e-5
BIG = 1e8

UH = NS // HN
UNITS = [(c, h) for c in range(EC) for h in range(UH)]

NA = 45


def at(k):
    return 5 + 2 * k


NB_UNITS = 49
AFTER = {
    "pe": [1, 3, 4, 5, 5, 6, 11, 11, 11, 11, 11, 12, 13, 14, 14, 15, 15, 15, 15, 18, 21, 22, 23, 27, 29, 29, 31, 32, 32, 35, 38, 38,
           38, 40, 41, 41, 41, 43, 44, 44, 44, 45, 45, 46, 46],
    "act": [1, 3, 4, 5, 6, 9, 11, 11, 11, 11, 11, 12, 13, 13, 13, 13, 13, 13, 15, 18, 21, 22, 23, 27, 29, 29, 31, 33, 33, 35, 35, 35,
            35, 37, 38, 41, 41, 43, 44, 44, 44, 45, 45, 46, 46],
    "dve": [1, 3, 4, 5, 9, 9, 11, 11, 11, 11, 11, 12, 13, 13, 13, 14, 14, 15, 15, 18, 21, 22, 23, 27, 29, 29, 31, 33, 33, 35, 35, 35,
            35, 37, 38, 41, 42, 44, 44, 44, 44, 45, 45, 46, 46],
    "pool": [1, 3, 4, 5, 5, 9, 11, 11, 11, 11, 11, 12, 13, 13, 13, 14, 14, 15, 15, 18, 21, 22, 23, 27, 29, 29, 31, 33, 33, 35, 35, 35,
             35, 37, 38, 41, 41, 43, 44, 44, 44, 45, 45, 46, 46],
    "sp": [1, 3, 4, 5, 5, 6, 11, 11, 11, 11, 11, 12, 13, 13, 13, 13, 13, 13, 15, 18, 21, 22, 23, 27, 29, 29, 31, 33, 33, 35, 35, 35,
           35, 37, 38, 41, 41, 43, 44, 44, 44, 45, 45, 46, 46],
}


def order(engine):
    return [x for b in range(NB_UNITS) for x in [("B", b)] + [("A", a) for a in range(NA) if AFTER[engine][a] == b]]


COUNTED = """
loads_mamba loads_loras loads_rest prep_pool prep_halves prep_act prep_pe prep_evac
dve_own act_own pool_own
a_x a_var a_rstd a_norm a_xnT_ps a_xnT a_in_ps a_tap a_conv a_z_tanh a_silu_z a_xc_tanh a_xc
a_xpj_ps a_xpj a_store a_B a_C a_dtl_ps a_u a_ln a_dt a_dtx a_dA a_dBx a_scan a_hC a_pairs a_four a_y_ps a_gated a_out_ps
a1_norm
b_var b_rstd b_ctx b_cxT_ps b_cxT b_tT_ps b_tT b_xT_ps b_xT b_vT_ps b_vT b_ss_ps b_ss b_rn b_diag b_row_ps b_dots_ps
b1_norm
f_xT_ps f_xT f_gl_ps f_exp f_exp_in f_low f_lowT_ps f_lowT f_wdiag f_w_ps f_wrow f_z1_ps f_z2_ps f_r f_h f_out_ps
f1_norm
t_zero t_xT_ps t_xT t_proj_ps t_rot t_kr t_ro t_kT_ps t_kz t_v_ps t_v t_qT_ps t_qT t_s_ps t_max t_p t_pT_ps t_pT t_o_ps t_o t_oT_ps t_oT
t_out_ps t1_norm
c_norm c2_norm c_xT_ps c_xT c_x2T_ps c_x2T c_q_ps c_q c_k_ps c_k c_v_ps c_v c_s_ps c_max c_p
c_pT_ps c_pT c_ctx_ps c_ctx c_out_ps c_x4b c_res c1_norm
l_xT_ps l_xT l_g_ps l_u_ps l_tanh l_state l_xw_ps l_xw l_kept e_load
e_cu_ps e_sum e_tanh e_var e_rstd e_norm e_store
""".split()


NORMS = {"a": ("a", 1), "a1": ("a", 2), "b1": ("b", 1), "f1": ("b", 2), "c2": ("b", 3), "t1": ("b", 4), "c": ("b", 5), "c1": ("b", 6)}


class Own:

    def __init__(self, eng, sem):
        self.eng, self.sem, self.n = eng, sem, 0

    def did(self, ins):
        ins.then_inc(self.sem, 1)
        self.n += 1

    def wait(self):
        self.eng.wait_ge(self.sem, self.n)

    def link(self, ins):
        self.did(ins)
        self.wait()


def build(nc, A, out):
    with ExitStack() as ctx:
        def sb(name, shape, dtype=F32):
            return ctx.enter_context(nc.sbuf_tensor(name, shape, dtype))

        phase = ctx.enter_context(nc.semaphore("phase"))
        arrived = ctx.enter_context(nc.semaphore("arrived"))
        s = {n: ctx.enter_context(nc.semaphore(n)) for n in COUNTED}
        numbers = sorted(x.num for x in s.values())
        assert numbers == list(range(numbers[0], numbers[-1] + 1))
        bank = [ctx.enter_context(nc.psum_tensor(f"bank{i}", [P, 512], F32)) for i in range(8)]
        scratch = nc.dram_tensor("xpj_scratch", (2 * NS + 1, S), F32, kind="Internal").ap()
        kept_x = nc.dram_tensor("kept_x", (NB, P, T * D), F32, kind="Internal").ap()
        kept_w = nc.dram_tensor("kept_w", (NB, P, T * D), F32, kind="Internal").ap()

        w_in = sb("w_in", [P, KD, 2 * DI]); w_xp = sb("w_xp", [P, EC, 2 * NS + 1]); w_out = sb("w_out", [P, EC, D])
        conv_w = sb("conv_w", [P, EC, TAPS]); conv_wh = sb("conv_wh", [P, EC, TAPS])
        conv_b = sb("conv_b", [P, EC]); conv_bh = sb("conv_bh", [P, EC])
        ln_g = sb("ln_g", [P, KD]); ln_b = sb("ln_b", [P, KD])
        w_dt = sb("w_dt", [P, EC]); b_dt = sb("b_dt", [P, EC]); a_log = sb("a_log", [P, EC, NS]); a_neg = sb("a_neg", [P, EC, NS])
        d_skip = sb("d_skip", [P, EC])
        wv0 = sb("wv0", [P, KD, VH]); bv0 = sb("bv0", [P, 1]); wt0 = sb("wt0", [P, 2, VH]); bt0 = sb("bt0", [P, 1])
        w_gl = sb("w_gl", [P, KD, NE + NLOW]); b_gl = sb("b_gl", [P, NE]); w_b = sb("w_b", [NPACK, FF], F32R)
        part = sb("part", [NPACK, 2])
        w_i = sb("w_i", [P, KD, FF]); w_o = sb("w_o", [P, FC, D]); prio = sb("prio", [P, NE])
        w_q = sb("w_q", [P, KD, NQ * HD]); w_k = sb("w_k", [P, KD, NKV * HD]); w_v = sb("w_v", [P, KD, NKV * HD])
        w_ao = sb("w_ao", [P, 8, D])
        rope = sb("rope", [P, T, 2, 3, HH])
        ln1_g = sb("ln1_g", [P, KD]); ln1_b = sb("ln1_b", [P, KD]); ln2_g = sb("ln2_g", [P, 2]); ln2_b = sb("ln2_b", [P, 2])
        w_q1 = sb("w_q1", [P, KD, E2]); w_k1 = sb("w_k1", [P, 2, E2]); w_v1 = sb("w_v1", [P, 2, E2]); w_o1 = sb("w_o1", [P, 2, D])
        b_q1 = sb("b_q1", [P, 2]); b_q1s = sb("b_q1s", [P, 2]); b_k1 = sb("b_k1", [P, 2]); b_v1 = sb("b_v1", [P, E2]); b_o1 = sb("b_o1", [P, D])
        w_g = sb("w_g", [P, 3, KD, D]); u_g = sb("u_g", [P, 3, KD, D]); b_g = sb("b_g", [P, 3, KD]); b_gh = sb("b_gh", [P, 3, KD])
        w_ho = sb("w_ho", [P, KD, D]); u_ho = sb("u_ho", [P, KD, D]); b_ho = sb("b_ho", [P, D]); in_c = sb("in_c", [P, KD])
        ident = sb("ident", [P, P]); ones = sb("ones", [P, P]); neghalf = sb("neghalf", [P, 16])

        scans = sb("scans", [P, 4 * HN, S])
        heads = sb("heads", [P, 12, S])
        outs = sb("outs", [P, 8, S])
        turns = sb("turns", [P, 8, S])

        lora_ao = outs[0:LORA, 0:4, :].rearrange("p a b -> p (a b)")
        qb = outs[0:LORA, 4:8, :].rearrange("p a b -> p (a b)")
        lora_a = heads[0:LORA, 0:3, :]
        kb, vb, obm = heads[0:LORA, 3, :], heads[0:LORA, 4, :], heads[0:LORA, 5, :]

        x0 = sb("x0", [P, T, D])
        conv = sb("conv", [P, EC, S]); zg = sb("zg", [P, EC, S]); xc = sb("xc", [P, EC, S])
        xpj = sb("xpj", [2 * NS + 1, S]); dt = sb("dt", [P, EC, S]); dtx = conv
        Bb = sb("Bb", [P, NS, S]); Cb = sb("Cb", [P, NS, S])
        dA = [scans[:, i * HN:(i + 1) * HN, :] for i in range(2)]
        hb = [scans[:, (2 + i) * HN:(3 + i) * HN, :] for i in range(2)]
        yh = sb("yh", [P, 2, S])
        zdt = hb[0]
        udt = tz = hb[1]
        xn = xT_free = Cb[:, 0:2, :]
        xnT = Cb[:, 2:4, :]
        res = dtx[:, 0:2, :]
        x1 = sb("x1", [P, T, D])
        x2 = sb("x2", [P, T, D]); x3 = sb("x3", [P, T, D]); x4 = x2; x5 = x3
        xT = sb("xT", [P, KD, S]); cx = sb("cx", [P, T, CTX]); cxT = sb("cxT", [P, 2, S])
        sq, rscale = outs[:, 0:2, :], outs[:, 2:4, :]
        tT, vT = outs[:, 4, :], outs[:, 5, :]
        ss = sb("ss", [P, 4]); rn = sb("rn", [P, 4]); diag = outs[:, 6:8, :].rearrange("p i (t q) -> p i t q", t=T)
        sm = sb("sm", [P, 12, T, NE]); sc2 = sb("sc2", [P, 8, T])
        low = sb("low", [P, 2, T, NLOW])
        packed = outs[:, 0, :].rearrange("p (n h w k) -> p n h w k", h=2, w=2, k=NLOW)
        lowT, wrow = sb("lowT", [NPACK, 2, S], F32R), heads[:, 2:4, :]
        r1 = heads[:, 4:8, :].rearrange("p (j a) s -> p j a s", j=2)
        r2 = heads[:, 8:12, :].rearrange("p (j a) s -> p j a s", j=2)
        hT = turns
        rot = [turns[:, 4 * i:4 * i + 4, :].rearrange("p (j a) s -> p j (a s)", j=2) for i in range(2)]
        keys = outs[:, 0:3, :].rearrange("p a s -> p (a s)")[:, 0:T * (NKV + 1) * HD].rearrange("p (t n) -> p t n", t=T)
        queries = [outs[:, 3 + 2 * i:5 + 2 * i, :].rearrange("p a s -> p (a s)") for i in range(2)]
        kz = [[heads[:, g, :] for g in range(NKV)], [x2[:, 1, :], cxT[:, 0, :], cxT[:, 1, :], x2[:, 0, :]]]
        qT = heads[:, 4:12, :].rearrange("p (g j) s -> p g j s", g=NKV)
        v1 = sb("v1", [P, T, NKV, HD + 1])
        nmax = sb("nmax", [P, 4, T]); 
        pe_ = turns[:, 0:4, :].rearrange("p (j a) s -> p j a s", j=2)
        pT = turns[:, 4:8, :].rearrange("p (j a) s -> p j a s", j=2)
        rs = sb("rs", [P, 2, T, 2])
        ob = outs[:, :, :].rearrange("p (t a) (h d) -> p t (a h) d", t=T, d=HD)
        oT = heads[:, 4:12, :]
        x1n, x4b, x2n = turns[:, 2:4, :], turns[:, 6:8, :], outs[:, 6:8, 0:CTX]
        x2T = cxT
        q1, k1, v1x, cT = outs[:, 0:2, :], outs[:, 2:4, :], outs[:, 4:6, :], outs[:, 6:8, :]
        sums = sb("sums", [P, T]); rsum = sb("rsum", [P, T])
        tg = heads[:, 0:6, :].rearrange("p (g k) s -> p g k s", g=3)
        ug = heads[:, 6:10, :].rearrange("p (g k) s -> p g k s", g=2)
        xw = heads[:, 10:12, :].rearrange("p a s -> p (a s)")
        state = sb("state", [P, KD, S])
        cu = x1[:, :, :].rearrange("p a s -> p (a s)")
        XS = Bb[:, :, :].rearrange("p (b t) s -> p b (t s)", t=T)
        XW = Cb[:, :, :].rearrange("p (b t) s -> p b (t s)", t=T)
        x5_last = Bb[:, 2 * NB - 2:2 * NB, :]
        ln_sts = [sb(f"ln_st{i}", [P, T, 6]) for i in range(2)]; ln_mv = {}; ln_var = {}; ln_rs = {}
        for tag in ("a", "a1", "b1", "f1", "t1", "c", "c2", "c1"):
            ln_mv[tag] = sb(f"mv_{tag}", [P, T, 2]); ln_var[tag] = sb(f"var_{tag}", [P, T]); ln_rs[tag] = sb(f"rstd_{tag}", [P, T])
        e_st = sb("e_st", [P, NB * T, 6]); e_mv = sb("e_mv", [P, NB * T, 2]); e_var = sb("e_var", [P, NB * T]); e_rs = sb("e_rs", [P, NB * T])

        def stats(dve, own, src, tag):
            ln_st = ln_sts[tag in ("a", "a1")]
            for t in range(T):
                own.did(dve.bn_stats(ln_st[:, t, :], src[:, t, :]))
            own.wait()
            for t in range(T):
                own.did(dve.bn_aggr(ln_mv[tag][:, t, :], ln_st[:, t, :]))
            own.wait()
            dve.tensor_scalar(ln_var[tag][:, :], ln_mv[tag][:, :, 1], EPS, None, ALU.add).then_inc(s[NORMS[tag][0] + "_var"], 1)

        def rstd(pool, tag):
            pool.wait_ge(s[NORMS[tag][0] + "_var"], NORMS[tag][1])
            pool.tensor_tensor(ln_rs[tag][:, :], ln_var[tag][:, :], neghalf[:, 0:T], ALU.pow).then_inc(s[NORMS[tag][0] + "_rstd"], 1)

        def normal(dve, src, dst, tag):
            dve.wait_ge(s[NORMS[tag][0] + "_rstd"], NORMS[tag][1])
            for t in range(T):
                dve.tensor_scalar(dst[:, t, :], src[:, t, :], ln_mv[tag][:, t, 0:1], ln_rs[tag][:, t:t + 1],
                                  ALU.subtract, ALU.mult).then_inc(s[tag + "_norm"], 1)

        def turn(pe, src, bk, sem):
            for k in range(KD):
                for t in range(T):
                    last = pe.transpose(bk[:, k * S + t * P:k * S + t * P + P], src[:, t, k * P:(k + 1) * P], ident[:, :])
            last.then_inc(s[sem], 1)

        def mm(pe, o, pairs, start=True):
            n = len(pairs)
            for i, (l, r) in enumerate(pairs):
                last = pe.matmul(o, l, r, start=(start and i == 0), stop=(i == n - 1), skip_group_check=True)
            return last

        def flat(ap):
            return ap.rearrange("p a b -> p (a b)")

        PA = bank[0:3]

        def a_sp(sp, b):
            yield 0
            sp.dma_start(x0[:, :, :], A["x"][bass.ds(b, 1), :, :].rearrange("a (t p) d -> p (a t) d", p=P)).then_inc(s["a_x"], 16)
            yield 3
            sp.wait_ge(s["a_xpj"], 1)
            sp.dma_start(scratch, xpj[:, :]).then_inc(s["a_store"], 16)
            sp.wait_ge(s["a_store"], 16)
            sp.dma_start(Bb[:, :, :], scratch[0:NS, :].partition_broadcast(P)).then_inc(s["a_B"], 16)
            sp.dma_start(Cb[:, :, :], scratch[NS:2 * NS, :].partition_broadcast(P)).then_inc(s["a_C"], 16)

        def a_dve(dve, own, alone=False):
            yield 0
            dve.wait_ge(s["a_x"], 16)
            stats(dve, own, x0, "a")
            normal(dve, x0, xn, "a")
            yield 1
            for j in range(2):
                dve.wait_ge(s["a_tap"], 2 * j + 2)
                for k in range(TAPS - 1):
                    d = TAPS - 1 - k
                    for i in range(2):
                        e = 2 * j + i
                        ins = dve.scalar_tensor_tensor(conv[:, e, d:S], PA[1 + j][:, i * S:i * S + S - d], conv_wh[:, e, k:k + 1],
                                                       conv[:, e, d:S], ALU.mult, ALU.add)
                        if k == TAPS - 2:
                            ins.then_inc(s["a_conv"], 1)
                        else:
                            own.did(ins)
                    if k < TAPS - 2:
                        own.wait()
            yield 2
            for j in range(2):
                dve.wait_ge(s["a_z_tanh"], j + 1)
                dve.scalar_tensor_tensor(flat(zg[:, 2 * j:2 * j + 2, :]), flat(tz[:, 2 * j:2 * j + 2, :]), 1.0, [PA[0], PA[1]][j][:, :],
                                         ALU.add, ALU.mult).then_inc(s["a_silu_z"], 1)
            dve.wait_ge(s["a_conv"], EC)
            for e in range(EC):
                dve.wait_ge(s["a_xc_tanh"], e + 1)
                dve.scalar_tensor_tensor(xc[:, e, :], xc[:, e, :], 1.0, conv[:, e, :], ALU.add, ALU.mult).then_inc(s["a_xc"], 1)
            yield 4
            dve.wait_ge(s["a_u"], 1)
            dve.wait_ge(s["a_xc"], EC)
            own.link(dve.tensor_scalar(flat(conv[:, :, :]), flat(udt[:, :, :]), 1.0, 1.0, ALU.add, ALU.subtract))
            own.link(dve.tensor_tensor(flat(conv[:, :, :]), flat(udt[:, :, :]), flat(conv[:, :, :]), ALU.subtract))
            dve.wait_ge(s["a_ln"], 1)
            own.link(dve.tensor_tensor(flat(conv[:, :, :]), flat(conv[:, :, :]), flat(dt[:, :, :]), ALU.add))
            dve.scalar_tensor_tensor(flat(dt[:, :, :]), flat(zdt[:, :, :]), 0.0, flat(conv[:, :, :]), ALU.max, ALU.add).then_inc(s["a_dt"], 1)
            dve.wait_ge(s["a_dt"], 1)
            dve.tensor_tensor(flat(dtx[:, :, :]), flat(dt[:, :, :]), flat(xc[:, :, :]), ALU.mult).then_inc(s["a_dtx"], 1)
            for u, (c, h) in enumerate(UNITS):
                yield at(u + 1)
                H = hb[u % 2]
                dve.wait_ge(s["a_dA"], u + 1)
                dve.wait_ge(s["a_dBx"], u + 1)
                dve.tensor_tensor_scan(flat(H[:, :, :]), flat(dA[u % 2][:, :, :]), flat(H[:, :, :]), 0.0, ALU.mult, ALU.add).then_inc(s["a_scan"], 1)
                yield at(u + 1) + 1
                dve.wait_ge(s["a_scan"], u + 1)
                if u == 0:
                    dve.wait_ge(s["a_C"], 16)
                dve.tensor_tensor(flat(H[:, :, :]), flat(H[:, :, :]), flat(Cb[:, h * HN:(h + 1) * HN, :]), ALU.mult).then_inc(s["a_hC"], 1)
                if alone:
                    dve.wait_ge(s["a_hC"], u + 1)
                    dve.tensor_tensor(H[:, 0:2, :], H[:, 0:2, :], H[:, 2:4, :], ALU.add).then_inc(s["a_pairs"], 1)
                if h == 2 and c >= 1:
                    yield at(u + 2)
                    skip(dve, own, c - 1)
            yield at(len(UNITS) + 3)
            skip(dve, own, EC - 1)
            yield at(len(UNITS) + 3) + 1
            dve.wait_ge(s["a_out_ps"], 1)
            own.link(dve.scalar_tensor_tensor(flat(res[:, :, :]), flat(x0[:, :, :]), 2.0, PA[1][:, :], ALU.mult, ALU.add))
            stats(dve, own, res, "a1")
            normal(dve, res, x1, "a1")

        def skip(dve, own, c):
            dve.wait_ge(s["a_y_ps"], UH * (c + 1))
            own.link(dve.scalar_tensor_tensor(xc[:, c, :], xc[:, c, :], d_skip[:, c:c + 1], [PA[0], PA[2]][c % 2][:, 0:S], ALU.mult, ALU.add))
            dve.tensor_tensor(zg[:, c, :], xc[:, c, :], zg[:, c, :], ALU.mult).then_inc(s["a_gated"], 1)

        def a_pool(pool, own, alone=False):
            yield 0
            rstd(pool, "a")
            yield 5
            pool.wait_ge(s["a_dtx"], 1)
            pool.wait_ge(s["a_B"], 16)

            def four(u):
                H = hb[u % 2]
                pool.wait_ge(s["a_hC"], u + 1)
                if u >= 2:
                    pool.wait_ge(s["a_y_ps"], u - 1)
                pool.tensor_tensor(H[:, 0:2, :], H[:, 0:2, :], H[:, 2:4, :], ALU.add).then_inc(s["a_pairs"], 1)
                pool.wait_ge(s["a_pairs"], u + 1)
                pool.tensor_tensor(yh[:, u % 2, :], H[:, 0, :], H[:, 1, :], ALU.add).then_inc(s["a_four"], 1)

            for u, (c, h) in enumerate(UNITS):
                yield at(u)
                if u >= 2:
                    if alone:
                        pool.wait_ge(s["a_y_ps"], u - 1)
                    else:
                        four(u - 2)
                        pool.wait_ge(s["a_four"], u - 1)
                pool.tensor_tensor(hb[u % 2][:, :, :], dtx[:, c:c + 1, :].to_broadcast([P, HN, S]), Bb[:, h * HN:(h + 1) * HN, :],
                                   ALU.mult).then_inc(s["a_dBx"], 1)
            for u in range(len(UNITS) - 2, len(UNITS)):
                yield at(u + 2)
                if not alone:
                    four(u)
            yield at(len(UNITS) + 3) + 1
            rstd(pool, "a1")

        def a_act(act, own):
            yield 0
            act.wait_ge(s["a_xnT_ps"], 1)
            for k in range(KD):
                act.activation(xnT[:, k, :], PA[0][:, k * S:(k + 1) * S], ACT.Identity, bias=ln_b[:, k:k + 1],
                               scale=ln_g[:, k:k + 1]).then_inc(s["a_xnT"], 1)
            yield 1
            for j in range(2):
                act.wait_ge(s["a_in_ps"], j + 1)
                for i in range(2):
                    e = 2 * j + i
                    act.activation(conv[:, e, :], PA[1 + j][:, i * S:(i + 1) * S], ACT.Identity, bias=conv_bh[:, e:e + 1],
                                   scale=conv_wh[:, e, TAPS - 1:TAPS]).then_inc(s["a_tap"], 1)
            yield 2
            for j in range(2):
                act.wait_ge(s["a_in_ps"], j + 3)
                act.activation(flat(tz[:, 2 * j:2 * j + 2, :]), [PA[0], PA[1]][j][:, :], ACT.Tanh).then_inc(s["a_z_tanh"], 1)
            for e in range(EC):
                act.wait_ge(s["a_conv"], e + 1)
                act.activation(xc[:, e, :], conv[:, e, :], ACT.Tanh).then_inc(s["a_xc_tanh"], 1)
            yield 3
            act.wait_ge(s["a_xpj_ps"], 1)
            act.activation(xpj[:, :], PA[2][0:2 * NS + 1, 0:S], ACT.Copy).then_inc(s["a_xpj"], 1)
            yield 4
            act.wait_ge(s["a_dtl_ps"], 1)
            for c in range(EC):
                own.did(act.activation(zdt[:, c, :], PA[0][:, 0:S], ACT.Identity, bias=b_dt[:, c:c + 1], scale=w_dt[:, c:c + 1]))
            own.wait()
            own.link(act.activation(flat(udt[:, :, :]), flat(zdt[:, :, :]), ACT.Abs))
            act.activation(flat(udt[:, :, :]), flat(udt[:, :, :]), ACT.Exp, scale=-1.0).then_inc(s["a_u"], 1)
            act.wait_ge(s["a_u"], 1)
            act.activation(flat(dt[:, :, :]), flat(udt[:, :, :]), ACT.Ln, bias=1.0).then_inc(s["a_ln"], 1)
            yield 5
            act.wait_ge(s["a_dt"], 1)
            for u, (c, h) in enumerate(UNITS):
                yield at(u)
                if u >= 2:
                    act.wait_ge(s["a_scan"], u - 1)
                for j in range(HN):
                    if j == HN // 2:
                        yield at(u) + 1
                    n = h * HN + j
                    ins = act.activation(dA[u % 2][:, j, 1:S], dt[:, c, 1:S], ACT.Exp, scale=a_neg[:, c, n:n + 1])
                ins.then_inc(s["a_dA"], 1)

        def a_pe(pe, alone=False):
            yield 0
            pe.wait_ge(s["a_norm"], T)
            turn(pe, xn, PA[0], "a_xnT_ps")
            yield 1
            pe.wait_ge(s["a_xnT"], KD)
            for j, bk in enumerate([PA[1], PA[2], PA[0], PA[1]]):
                yield 1 + j // 2
                if j == 3:
                    pe.wait_ge(s["a_conv"], 2)
                for i in range(2):
                    e = 2 * j + i
                    last = mm(pe, bk[:, i * S:(i + 1) * S], [(w_in[:, k, e * P:(e + 1) * P], xnT[:, k, :]) for k in range(KD)])
                last.then_inc(s["a_in_ps"], 1)
            yield 3
            pe.wait_ge(s["a_xc"], EC)
            mm(pe, PA[2][0:2 * NS + 1, 0:S], [(w_xp[:, c, :], xc[:, c, :]) for c in range(EC)]).then_inc(s["a_xpj_ps"], 1)
            yield 4
            pe.wait_ge(s["a_xpj"], 1)
            pe.wait_ge(s["a_silu_z"], 1)
            mm(pe, PA[0][:, 0:S], [(ones[2 * NS:2 * NS + 1, :], xpj[2 * NS:2 * NS + 1, :])]).then_inc(s["a_dtl_ps"], 1)
            yield at(3)
            pe.wait_ge(s["a_u"], 1)
            for u, (c, h) in enumerate(UNITS):
                yield at(u + 3)
                pe.wait_ge(s["a_pairs" if alone else "a_four"], u + 1)
                if h == 0 and c >= 2:
                    pe.wait_ge(s["a_gated"], c - 1)
                sums_of = [hb[u % 2][:, 0, :], hb[u % 2][:, 1, :]] if alone else [yh[:, u % 2, :]]
                for i, part_sum in enumerate(sums_of):
                    last = pe.matmul([PA[0], PA[2]][c % 2][:, 0:S], ident[:, :], part_sum, start=(h == 0 and i == 0),
                                     stop=(h == UH - 1 and i == len(sums_of) - 1))
                last.then_inc(s["a_y_ps"], 1)
            yield at(len(UNITS) + 3)
            pe.wait_ge(s["a_gated"], EC)
            pe.wait_ge(s["a_silu_z"], 2)
            for t in range(T):
                last = mm(pe, PA[1][:, t * D:(t + 1) * D], [(zg[:, c, t * P:(t + 1) * P], w_out[:, c, :]) for c in range(EC)])
            last.then_inc(s["a_out_ps"], 1)

        def load_context(sp, b):
            sp.dma_start(cx[:, :, :], A["ctx"][bass.ds(b, 1), :, :].rearrange("a (t p) d -> p (a t) d", p=P)).then_inc(s["b_ctx"], 16)

        def r_sp(sp, b):
            yield 39
            sp.wait_ge(s["c2_norm"], T)
            load_context(sp, b)

        def b_pe(pe):
            b3, b4, b5, b6, b7 = bank[3:8]
            yield 0
            for t in range(T):
                pe.transpose(b3[:, t * P:(t + 1) * P], cx[:, t, 0:P], ident[:, :])
            for t in range(T):
                last = pe.transpose(b3[0:CTX2, S + t * P:S + (t + 1) * P], cx[:, t, P:CTX], ident[:, :])
            last.then_inc(s["b_cxT_ps"], 1)
            turn(pe, x1, b5, "b_xT_ps")
            yield 1
            pe.wait_ge(s["b_cxT"], 2)
            mm(pe, b4[:, 0:S], [(wt0[:, 0, :], cxT[:, 0, :]), (wt0[0:CTX2, 1, :], cxT[0:CTX2, 1, :])]).then_inc(s["b_tT_ps"], 1)
            pe.wait_ge(s["b_xT"], 1)
            mm(pe, b6[:, 0:S], [(wv0[:, k, :], xT[:, k, :]) for k in range(KD)]).then_inc(s["b_vT_ps"], 1)
            yield 2
            pe.wait_ge(s["b_tT"], 2)
            pe.wait_ge(s["b_vT"], 2)
            for t in range(T):
                mm(pe, b4[:, t * S:(t + 1) * S], [(vT[:, t * P:(t + 1) * P], tT[:, :])]).then_inc(s["b_dots_ps"], 1)
            for i in range(2):
                for t in range(T):
                    last = pe.matmul(b7[:, 2 * i + t:2 * i + t + 1], sq[:, i, t * P:(t + 1) * P], ones[:, 0:1], start=True, stop=True)
            last.then_inc(s["b_ss_ps"], 1)
            yield 3
            pe.wait_ge(s["b_diag"], T)
            mm(pe, b7[:, 0:S], [(ones[:, :], diag[:, 0, :, :].rearrange("p a b -> p (a b)"))]).then_inc(s["b_row_ps"], 1)

        def b_act(act, own):
            b3, b4, b5, b6, b7 = bank[3:8]
            yield 0
            act.wait_ge(s["b_cxT_ps"], 1)
            act.activation(cxT[:, 0, :], b3[:, 0:S], ACT.Copy).then_inc(s["b_cxT"], 1)
            act.activation(cxT[0:CTX2, 1, :], b3[0:CTX2, S:2 * S], ACT.Copy).then_inc(s["b_cxT"], 1)
            act.wait_ge(s["b_xT_ps"], 1)
            act.activation(flat(xT[:, :, :]), b5[:, :], ACT.Copy).then_inc(s["b_xT"], 1)
            yield 1
            act.wait_ge(s["b_tT_ps"], 1)
            act.activation(tT[:, :], b4[:, 0:S], ACT.Identity, bias=bt0[:, :]).then_inc(s["b_tT"], 1)
            act.activation(sq[:, 1, :], b4[:, 0:S], ACT.Square, bias=bt0[:, :]).then_inc(s["b_tT"], 1)
            act.wait_ge(s["b_vT_ps"], 1)
            act.activation(vT[:, :], b6[:, 0:S], ACT.Identity, bias=bv0[:, :]).then_inc(s["b_vT"], 1)
            act.activation(sq[:, 0, :], b6[:, 0:S], ACT.Square, bias=bv0[:, :]).then_inc(s["b_vT"], 1)

        def b_dve(dve, own):
            b3, b4, b5, b6, b7 = bank[3:8]
            yield 2
            dve.wait_ge(s["b_ss_ps"], 1)
            dve.tensor_scalar(ss[:, :], b7[:, 0:4], 1e-38, None, ALU.max).then_inc(s["b_ss"], 1)
            dve.wait_ge(s["b_rn"], 1)
            for t in range(T):
                dve.tensor_scalar(diag[:, 0, t, :], ident[:, :], rn[:, 2 + t:3 + t], None, ALU.mult).then_inc(s["b_diag"], 1)
            yield 3
            dve.wait_ge(s["b_row_ps"], 1)
            for t in range(T):
                own.did(dve.tensor_scalar(rscale[:, t, :], b7[:, 0:S], rn[:, t:t + 1], BIG, ALU.mult, ALU.min))
            own.wait()
            dve.wait_ge(s["b_dots_ps"], T)
            own.link(dve.tensor_tensor(flat(rscale[:, :, :]), flat(rscale[:, :, :]), b4[:, :], ALU.mult))
            own.link(dve.tensor_tensor(flat(x2[:, :, :]), flat(rscale[:, :, :]), flat(x1[:, :, :]), ALU.add))
            stats(dve, own, x2, "b1")
            normal(dve, x2, x2, "b1")

        def b_pool(pool, own):
            yield 2
            pool.wait_ge(s["b_ss"], 1)
            pool.tensor_tensor(rn[:, :], ss[:, :], neghalf[:, 0:4], ALU.pow).then_inc(s["b_rn"], 1)
            yield 3
            rstd(pool, "b1")

        FB = bank[5:8]

        def f_pe(pe):
            b3, b4, b5, b6, b7 = bank[3:8]
            yield 4
            pe.wait_ge(s["b1_norm"], T)
            turn(pe, x2, b5, "f_xT_ps")
            yield 5
            pe.wait_ge(s["f_xT"], 1)
            for t in range(T):
                last = mm(pe, b3[:, t * 20:t * 20 + 20], [(xT[:, k, t * P:(t + 1) * P], w_gl[:, k, :]) for k in range(KD)])
            last.then_inc(s["f_gl_ps"], 1)

            def base(j):
                if j >= 3:
                    pe.wait_ge(s["f_r"], 2 * (j - 3) + 2)
                for i in range(2):
                    f = 2 * j + i
                    for k in range(KD):
                        pe.matmul(FB[j % 3][:, i * S:(i + 1) * S], w_i[:, k, f * P:(f + 1) * P], xT[:, k, :],
                                  start=(i == 0 and k == 0), stop=False, skip_group_check=True)

            def lora(j, slot):
                if slot == 1:
                    pe.wait_ge(s["f_r"], 2 * j + 1)
                for i in range(2):
                    f = 2 * j + i
                    last = pe.matmul(FB[j % 3][:, i * S:(i + 1) * S], w_b[:, f * P:(f + 1) * P], lowT[:, slot, :],
                                     start=False, stop=(slot == 1), skip_group_check=True)
                last.then_inc(s[["f_z1_ps", "f_z2_ps"][slot]], 1)

            for j in range(3):
                base(j)
            yield 6
            pe.wait_ge(s["f_low"], 1)
            for i in range(2):
                for t in range(T):
                    last = pe.transpose(b3[0:NPACK, i * S + t * P:i * S + (t + 1) * P],
                                        packed[:, i * T + t, :, :, :].rearrange("p h w k -> p (h w k)"), ident[:, :])
            last.then_inc(s["f_lowT_ps"], 1)
            pe.wait_ge(s["f_wdiag"], 4)
            mm(pe, b4[:, :], [(ones[:, :], diag[:, :, :, :].rearrange("p a b c -> p (a b c)"))]).then_inc(s["f_w_ps"], 1)
            pe.wait_ge(s["f_lowT"], 1)

            for j in range(FC // 2 + 1):
                yield 7 + j
                if j < FC // 2:
                    if j == 3:
                        base(3)
                    lora(j, 0)
                if j >= 1:
                    lora(j - 1, 1)
            yield 12
            for t in range(T):
                for f in range(FC):
                    if t == 0 and f % 2 == 0:
                        pe.wait_ge(s["f_h"], f // 2 + 1)
                    last = pe.matmul(b3[:, t * D:(t + 1) * D], hT[:, f, t * P:(t + 1) * P], w_o[:, f, :], start=(f == 0), stop=(f == FC - 1))
            last.then_inc(s["f_out_ps"], 1)

        def f_act(act, own):
            b3, b4, b5, b6, b7 = bank[3:8]
            yield 4
            act.wait_ge(s["f_xT_ps"], 1)
            act.activation(flat(xT[:, :, :]), b5[:, :], ACT.Copy).then_inc(s["f_xT"], 1)
            yield 5
            act.wait_ge(s["f_exp_in"], 1)
            act.activation(sm[:, 1, :, :], sm[:, 1, :, :], ACT.Exp).then_inc(s["f_exp"], 1)
            yield 6
            act.wait_ge(s["f_lowT_ps"], 1)
            act.activation(flat(lowT[:, :, :]), b3[0:NPACK, :], ACT.Copy).then_inc(s["f_lowT"], 1)
            act.wait_ge(s["f_w_ps"], 1)
            act.activation(flat(wrow[:, :, :]), b4[:, :], ACT.Copy).then_inc(s["f_wrow"], 1)

        def f_dve(dve, own):
            b3, b4, b5, b6, b7 = bank[3:8]
            yield 5
            dve.wait_ge(s["f_gl_ps"], 1)
            gl = b3[:, 0:2 * 20].rearrange("p (t n) -> p t n", t=T)
            per = [P, T, NE]

            def wide(col):
                return sc2[:, col, :].unsqueeze(2).to_broadcast(per)

            def tile_of(x):
                return x.unsqueeze(1).to_broadcast(per)

            own.did(dve.tensor_copy(low[:, 1, :, :], gl[:, :, NE:]))
            own.link(dve.tensor_tensor(sm[:, 0, :, :], gl[:, :, 0:NE], tile_of(b_gl[:, :]), ALU.add))
            own.link(dve.tensor_reduce(sc2[:, 0, :], sm[:, 0, :, :], AX, ALU.max))
            dve.tensor_tensor(sm[:, 1, :, :], sm[:, 0, :, :], wide(0), ALU.subtract).then_inc(s["f_exp_in"], 1)
            dve.wait_ge(s["f_exp"], 1)
            own.link(dve.tensor_reduce(sc2[:, 1, :], sm[:, 1, :, :], AX, ALU.add))
            own.link(dve.reciprocal(sc2[:, 2, :], sc2[:, 1, :]))
            own.link(dve.tensor_tensor(sm[:, 2, :, :], sm[:, 1, :, :], wide(2), ALU.mult))
            for i, (score, hit, rank, one) in enumerate([(2, 3, 4, 5), (6, 7, 8, 9)]):
                top, best = 3 + 2 * i, 4 + 2 * i
                own.link(dve.tensor_reduce(sc2[:, top, :], sm[:, score, :, :], AX, ALU.max))
                own.link(dve.tensor_tensor(sm[:, hit, :, :], sm[:, score, :, :], wide(top), ALU.is_equal))
                own.link(dve.tensor_tensor(sm[:, rank, :, :], sm[:, hit, :, :], tile_of(prio[:, :]), ALU.mult))
                own.link(dve.tensor_reduce(sc2[:, best, :], sm[:, rank, :, :], AX, ALU.max))
                own.link(dve.tensor_tensor(sm[:, one, :, :], sm[:, rank, :, :], wide(best), ALU.is_equal))
                if i == 0:
                    own.link(dve.scalar_tensor_tensor(sm[:, 6, :, :], sm[:, 5, :, :], -2.0, sm[:, 2, :, :], ALU.mult, ALU.add))
            own.link(dve.tensor_tensor(sm[:, 10, :, :], sm[:, 9, :, :], sm[:, 5, :, :], ALU.subtract))
            for t in range(T):
                for i, one in enumerate([5, 10]):
                    own_or = dve.tensor_tensor(low[:, i, t, :].rearrange("p (e r) -> p e r", e=NE),
                                               low[:, 1, t, :].rearrange("p (e r) -> p e r", e=NE),
                                               sm[:, one, t, :].unsqueeze(2).to_broadcast([P, NE, RK]), ALU.mult)
                    own.did(own_or)
            own.wait()
            flat_low = low[:, :, :, :].rearrange("p i t k -> p (i t) k").unsqueeze(2).to_broadcast([P, 2 * T, 2, NLOW])
            own.link(dve.tensor_copy(packed[:, :, 0, :, :].bitcast(F32R), flat_low))
            dve.tensor_tensor(packed[:, :, 1, :, :], flat_low, packed[:, :, 0, :, :], ALU.subtract).then_inc(s["f_low"], 1)
            for i in range(2):
                for t in range(T):
                    dve.tensor_scalar(diag[:, i, t, :], ident[:, :], sc2[:, 3 + 2 * i, t:t + 1], None, ALU.mult).then_inc(s["f_wdiag"], 1)
            yield 8
            dve.wait_ge(s["f_wrow"], 1)
            for j in range(FC // 2):
                yield 8 + j
                for i, (ps, dst) in enumerate([("f_z1_ps", r1), ("f_z2_ps", r2)]):
                    dve.wait_ge(s[ps], j + 1)
                    if j >= 2:
                        dve.wait_ge(s["f_h"], j - 1)
                    dve.scalar_tensor_tensor(dst[:, j % 2, :, :], FB[j % 3][:, :].rearrange("p (a b) -> p a b", a=2), 0.0,
                                             wrow[:, i:i + 1, :].to_broadcast([P, 2, S]), ALU.max, ALU.mult).then_inc(s["f_r"], 1)
            yield 12
            dve.wait_ge(s["f_out_ps"], 1)
            own.link(dve.tensor_tensor(flat(x3[:, :, :]), b3[:, :], flat(x2[:, :, :]), ALU.add))
            stats(dve, own, x3, "f1")
            normal(dve, x3, x3, "f1")

        def f_pool(pool, own):
            yield 8
            for j in range(FC // 2):
                yield 8 + j
                pool.wait_ge(s["f_r"], 2 * j + 2)
                pool.tensor_tensor(flat(hT[:, 2 * j:2 * j + 2, :]), r1[:, j % 2, :, :].rearrange("p a b -> p (a b)"),
                                   r2[:, j % 2, :, :].rearrange("p a b -> p (a b)"), ALU.add).then_inc(s["f_h"], 1)
            yield 12
            rstd(pool, "f1")

        SB, TB, OB = [bank[3], bank[4]], [bank[5], bank[6]], bank[7]
        NH = NQ

        def t_pe(pe):
            b3, b4, b5, b6, b7 = bank[3:8]
            yield 13
            pe.wait_ge(s["f1_norm"], T)
            turn(pe, x3, b5, "t_xT_ps")
            yield 14
            pe.wait_ge(s["t_xT"], 1)

            def project(n):
                if n >= 3:
                    pe.wait_ge(s["t_rot"], 6 + 3 * (n - 2))
                if n == 0:
                    for t in range(T):
                        last = mm(pe, b3[:, t * S:(t + 1) * S], [(xT[:, k, t * P:(t + 1) * P], w_k[:, k, :]) for k in range(KD)])
                else:
                    hf, t = (n - 1) // 2, (n - 1) % 2
                    last = mm(pe, [b5, b6][(n - 1) % 2][:, :], [(xT[:, k, t * P:(t + 1) * P], w_q[:, k, hf * 512:(hf + 1) * 512]) for k in range(KD)])
                last.then_inc(s["t_proj_ps"], 1)

            def turned_queries(n):
                pe.wait_ge(s["t_ro"], n)
                if n == 1:
                    pe.wait_ge(s["t_v"], 1)
                elif n == 2:
                    pe.wait_ge(s["t_kz"], 4)
                else:
                    pe.wait_ge(s["t_qT"], n - 2)
                for f in range(4):
                    last = pe.transpose([b4, b7][(n - 1) % 2][:, f * P:(f + 1) * P], queries[n % 2][:, f * P:(f + 1) * P], ident[:, :])
                last.then_inc(s["t_qT_ps"], 1)

            project(0)
            project(1)
            for t in range(T):
                last = mm(pe, b4[:, t * S:(t + 1) * S], [(xT[:, k, t * P:(t + 1) * P], w_v[:, k, :]) for k in range(KD)])
            last.then_inc(s["t_v_ps"], 1)
            project(2)
            pe.wait_ge(s["t_kr"], 2)
            for g in range(NKV):
                for t in range(T):
                    last = pe.transpose([b3, b7][g // 2][:, (g % 2) * S + t * P:(g % 2) * S + (t + 1) * P], keys[:, t, g * HD:(g + 2) * HD], ident[:, :])
            last.then_inc(s["t_kT_ps"], 1)
            yield 15
            project(3)
            turned_queries(1)
            project(4)
            for n in range(2, 5):
                turned_queries(n)
            yield 16
            pe.wait_ge(s["t_zero"], 3)
            pe.wait_ge(s["t_kz"], 4)
            pe.wait_ge(s["t_qT"], 4)
            pe.wait_ge(s["t_rot"], 18)

            def scores(h):
                g, pair = h // GH, (h % GH) // 2
                if h >= 2:
                    pe.wait_ge(s["t_p"], 2 * (h - 1))
                for t in range(T):
                    last = pe.matmul(SB[h % 2][:, t * S:(t + 1) * S], qT[:, g, pair, t * P:(t + 1) * P], kz[h % 2][g],
                                     start=True, stop=True)
                last.then_inc(s["t_s_ps"], 1)

            def turned(h):
                pe.wait_ge(s["t_p"], 2 * h + 2)
                if h >= 2:
                    pe.wait_ge(s["t_pT"], h - 1)
                for k in range(2):
                    for t in range(T):
                        last = pe.transpose(TB[h % 2][:, k * S + t * P:k * S + (t + 1) * P], pe_[:, h % 2, t, k * P:(k + 1) * P], ident[:, :])
                last.then_inc(s["t_pT_ps"], 1)

            def values(h):
                g = h // GH
                pe.wait_ge(s["t_pT"], h + 1)
                if h >= 2 and h % 2 == 0:
                    pe.wait_ge(s["t_o"], h // 2)
                for t in range(T):
                    o = (t * 2 + h % 2) * (HD + 1)
                    for k in range(2):
                        last = pe.matmul(OB[:, o:o + HD + 1], pT[:, h % 2, k, t * P:(t + 1) * P], v1[:, k, g, :], start=(k == 0), stop=(k == 1))
                last.then_inc(s["t_o_ps"], 1)

            for i in range(NH + 3):
                yield 16 + i
                if i < NH:
                    scores(i)
                if 1 <= i <= NH:
                    turned(i - 1)
                if 3 <= i:
                    values(i - 3)
            yield 35
            pe.wait_ge(s["t_o"], NH // 2)
            for c in range(8):
                bk = [b3, b4, b5, b6][(c // 2) % 4]
                for t in range(T):
                    last = pe.transpose(bk[:, (c % 2) * S + t * P:(c % 2) * S + (t + 1) * P],
                                        ob[:, t, 2 * c:2 * c + 2, :].rearrange("p a b -> p (a b)"), ident[:, :])
                if c % 2 == 1:
                    last.then_inc(s["t_oT_ps"], 1)
            yield 36
            pe.wait_ge(s["t_oT"], 4)
            for t in range(T):
                last = mm(pe, b7[:, t * D:(t + 1) * D], [(oT[:, c, t * P:(t + 1) * P], w_ao[:, c, :]) for c in range(8)])
            last.then_inc(s["t_out_ps"], 1)

        def t_act(act, own):
            b3, b4, b5, b6, b7 = bank[3:8]
            yield 13
            act.wait_ge(s["t_xT_ps"], 1)
            act.activation(flat(xT[:, :, :]), b5[:, :], ACT.Copy).then_inc(s["t_xT"], 1)
            yield 14
            act.wait_ge(s["t_v_ps"], 1)
            act.activation(v1[:, :, :, 0:HD], b4[:, :].rearrange("p (t g d) -> p t g d", t=T, g=NKV), ACT.Copy).then_inc(s["t_v"], 1)
            act.wait_ge(s["t_kT_ps"], 1)
            for bk, even, odd in [(b3, heads[:, 0:2, :], cxT), (b7, heads[:, 2:4, :], x2)]:
                for dst, half in [(even, slice(0, HD)), (odd, slice(HD, P))]:
                    act.activation(dst[half, :, :], bk[half, :].rearrange("p (a b) -> p a b", a=2), ACT.Copy).then_inc(s["t_kz"], 1)
            yield 15
            for n in range(1, 5):
                hf, t = (n - 1) // 2, (n - 1) % 2
                act.wait_ge(s["t_qT_ps"], n)
                act.activation(heads[:, 4 + 4 * hf:8 + 4 * hf, t * P:(t + 1) * P], [b4, b7][(n - 1) % 2][:, :].rearrange("p (f q) -> p f q", f=4),
                               ACT.Copy).then_inc(s["t_qT"], 1)
            yield 16
            for i in range(NH + 1):
                yield 16 + i
                h = i
                if h < NH:
                    act.wait_ge(s["t_max"], h + 1)
                    if h >= 2:
                        act.wait_ge(s["t_pT_ps"], h - 1)
                    for t in range(T):
                        act.activation(pe_[:, h % 2, t, :], SB[h % 2][:, t * S:(t + 1) * S], ACT.Exp, bias=nmax[:, h % 4, t:t + 1]).then_inc(s["t_p"], 1)
                h = i - 1
                if h >= 0:
                    act.wait_ge(s["t_pT_ps"], h + 1)
                    if h >= 2:
                        act.wait_ge(s["t_o_ps"], h - 1)
                    act.activation(pT[:, h % 2, :, :].rearrange("p a b -> p (a b)"), TB[h % 2][:, :], ACT.Copy).then_inc(s["t_pT"], 1)
            yield 35
            for j in range(4):
                act.wait_ge(s["t_oT_ps"], j + 1)
                act.activation(flat(oT[:, 2 * j:2 * j + 2, :]), [b3, b4, b5, b6][j][:, :], ACT.Copy).then_inc(s["t_oT"], 1)

        def t_dve(dve, own):
            b3, b4, b5, b6, b7 = bank[3:8]
            yield 13
            dve.wait_ge(s["f_out_ps"], 1)
            dve.memset(heads[HD:P, 0:4, :], 0.0).then_inc(s["t_zero"], 1)
            dve.memset(cxT[0:HD, :, :], 0.0).then_inc(s["t_zero"], 1)
            dve.memset(x2[0:HD, :, :], 0.0).then_inc(s["t_zero"], 1)
            yield 14

            def products(x, r, heads_of, tile, scale):
                cos, sin, neg = [rope[:, tile, scale, i, :].unsqueeze(1) for i in range(3)]
                x, out_cos, out_sin = [a.rearrange("p (h b r) -> p h b r", b=2, r=HH) for a in (x, r[0], r[1])]
                per = [P, heads_of, HH]
                dve.tensor_tensor(out_cos.rearrange("p h b r -> p (h b) r"), x.rearrange("p h b r -> p (h b) r"),
                                  cos.to_broadcast([P, 2 * heads_of, HH]), ALU.mult).then_inc(s["t_rot"], 1)
                dve.tensor_tensor(out_sin[:, :, 0, :], x[:, :, 1, :], neg.to_broadcast(per), ALU.mult).then_inc(s["t_rot"], 1)
                dve.tensor_tensor(out_sin[:, :, 1, :], x[:, :, 0, :], sin.to_broadcast(per), ALU.mult).then_inc(s["t_rot"], 1)

            for n in range(5):
                yield 14 if n < 3 else 15
                dve.wait_ge(s["t_proj_ps"], n + 1)
                if n == 2:
                    dve.wait_ge(s["t_kr"], 2)
                elif n > 2:
                    dve.wait_ge(s["t_ro"], n - 2)
                if n == 0:
                    for t in range(T):
                        cols = slice(t * S, (t + 1) * S)
                        products(b3[:, cols], [rot[0][:, j, cols] for j in range(2)], NKV, t, 0)
                else:
                    products([b5, b6][(n - 1) % 2][:, :], [rot[n % 2][:, j, :] for j in range(2)], 8, (n - 1) % 2, 1)

            yield 16

            def weigh(p):
                dve.wait_ge(s["t_o_ps"], 2 * p + 2)
                if p >= 2:
                    dve.wait_ge(s["t_o"], p - 1)
                o = OB[:, 0:4 * (HD + 1)].rearrange("p (t h d) -> p t h d", t=T, h=2)
                own.link(dve.reciprocal(rs[:, p % 2, :, :], o[:, :, :, HD]))
                dve.tensor_tensor(ob[:, :, 2 * p:2 * p + 2, :], o[:, :, :, 0:HD],
                                  rs[:, p % 2, :, :].unsqueeze(3).to_broadcast([P, T, 2, HD]), ALU.mult).then_inc(s["t_o"], 1)

            for i in range(NH + 3):
                yield 16 + i
                if i < NH:
                    dve.wait_ge(s["t_s_ps"], i + 1)
                    if i >= 4:
                        dve.wait_ge(s["t_p"], 2 * (i - 3))
                    dve.tensor_reduce(nmax[:, i % 4, :], SB[i % 2][:, :].rearrange("p (t k) -> p t k", t=T), AX, ALU.max,
                                      negate=True).then_inc(s["t_max"], 1)
                if i >= 4 and i % 2 == 0:
                    weigh((i - 4) // 2)
            yield 36
            stats(dve, own, cx, "c2")
            dve.wait_ge(s["t_oT_ps"], 4)
            normal(dve, cx, x2n, "c2")
            dve.wait_ge(s["t_out_ps"], 1)
            own.link(dve.tensor_tensor(flat(x4[:, :, :]), b7[:, :], flat(x3[:, :, :]), ALU.add))
            stats(dve, own, x4, "t1")
            normal(dve, x4, x4, "t1")

        def t_pool(pool, own):
            yield 14
            yield 14
            pool.wait_ge(s["t_rot"], 6)
            cos_k, sin_k = [rot[0][:, j, :].rearrange("p (t n) -> p t n", t=T) for j in range(2)]
            pool.tensor_tensor(keys[:, :, 0:S], cos_k, sin_k, ALU.add).then_inc(s["t_kr"], 1)
            pool.tensor_tensor(keys[:, :, S:S + HD], cos_k[:, :, 0:HD], sin_k[:, :, 0:HD], ALU.add).then_inc(s["t_kr"], 1)
            for n in range(1, 5):
                yield 14 if n < 3 else 15
                pool.wait_ge(s["t_rot"], 6 + 3 * n)
                if n >= 3:
                    pool.wait_ge(s["t_qT_ps"], n - 2)
                pool.tensor_tensor(queries[n % 2], rot[n % 2][:, 0, :], rot[n % 2][:, 1, :], ALU.add).then_inc(s["t_ro"], 1)
            yield 36
            rstd(pool, "c2")
            rstd(pool, "t1")

        def c_pe(pe):
            b3, b4, b5, b6, b7 = bank[3:8]
            yield 38
            pe.wait_ge(s["c2_norm"], T)
            for t in range(T):
                pe.transpose(b6[:, t * P:(t + 1) * P], x2n[:, t, 0:P], ident[:, :])
            for t in range(T):
                last = pe.transpose(b6[0:CTX2, S + t * P:S + (t + 1) * P], x2n[:, t, P:CTX], ident[:, :])
            last.then_inc(s["c_x2T_ps"], 1)
            yield 39
            pe.wait_ge(s["c_x2T"], 2)
            for e in range(2):
                last = mm(pe, b4[:, e * S:(e + 1) * S], [(w_k1[:, 0, e * P:(e + 1) * P], x2T[:, 0, :]),
                                                        (w_k1[0:CTX2, 1, e * P:(e + 1) * P], x2T[0:CTX2, 1, :])])
            last.then_inc(s["c_k_ps"], 1)
            for t in range(T):
                last = mm(pe, b3[:, t * E2:(t + 1) * E2], [(x2T[:, 0, t * P:(t + 1) * P], w_v1[:, 0, :]),
                                                          (x2T[0:CTX2, 1, t * P:(t + 1) * P], w_v1[0:CTX2, 1, :])])
            last.then_inc(s["c_v_ps"], 1)
            yield 40
            pe.wait_ge(s["c_norm"], T)
            turn(pe, x1n, b5, "c_xT_ps")
            yield 41
            pe.wait_ge(s["c_xT"], 2)
            for e in range(2):
                last = mm(pe, b6[:, e * S:(e + 1) * S], [(w_q1[:, k, e * P:(e + 1) * P], xT[:, k, :]) for k in range(KD)])
            last.then_inc(s["c_q_ps"], 1)
            yield 42
            pe.wait_ge(s["c_q"], 2)
            pe.wait_ge(s["c_k"], 2)
            for t in range(T):
                last = mm(pe, b7[:, t * S:(t + 1) * S], [(q1[:, e, t * P:(t + 1) * P], k1[:, e, :]) for e in range(2)])
            last.then_inc(s["c_s_ps"], 1)
            yield 43
            pe.wait_ge(s["c_p"], 2)
            for k in range(2):
                for t in range(T):
                    last = pe.transpose(b5[:, k * S + t * P:k * S + (t + 1) * P], pe_[:, 0, t, k * P:(k + 1) * P], ident[:, :])
            last.then_inc(s["c_pT_ps"], 1)
            yield 44
            pe.wait_ge(s["c_pT"], 1)
            pe.wait_ge(s["c_v"], 1)
            for e in range(2):
                last = mm(pe, b3[:, e * S:(e + 1) * S], [(v1x[:, k, e * P:(e + 1) * P], pT[:, 0, k, :]) for k in range(2)])
            last.then_inc(s["c_ctx_ps"], 1)
            yield 45
            pe.wait_ge(s["c_ctx"], 1)
            for t in range(T):
                last = mm(pe, b4[:, t * D:(t + 1) * D], [(cT[:, e, t * P:(t + 1) * P], w_o1[:, e, :]) for e in range(2)])
            last.then_inc(s["c_out_ps"], 1)

        def c_act(act, own):
            b3, b4, b5, b6, b7 = bank[3:8]
            yield 38
            act.wait_ge(s["c_x2T_ps"], 1)
            act.activation(x2T[:, 0, :], b6[:, 0:S], ACT.Identity, bias=ln2_b[:, 0:1], scale=ln2_g[:, 0:1]).then_inc(s["c_x2T"], 1)
            act.activation(x2T[0:CTX2, 1, :], b6[0:CTX2, S:2 * S], ACT.Identity, bias=ln2_b[0:CTX2, 1:2],
                           scale=ln2_g[0:CTX2, 1:2]).then_inc(s["c_x2T"], 1)
            yield 39
            act.wait_ge(s["c_k_ps"], 1)
            for e in range(2):
                act.activation(k1[:, e, :], b4[:, e * S:(e + 1) * S], ACT.Identity, bias=b_k1[:, e:e + 1]).then_inc(s["c_k"], 1)
            yield 40
            act.wait_ge(s["c_xT_ps"], 1)
            for k in range(KD):
                act.activation(xT[:, k, :], b5[:, k * S:(k + 1) * S], ACT.Identity, bias=ln1_b[:, k:k + 1],
                               scale=ln1_g[:, k:k + 1]).then_inc(s["c_xT"], 1)
            yield 41
            act.wait_ge(s["c_q_ps"], 1)
            for e in range(2):
                act.activation(q1[:, e, :], b6[:, e * S:(e + 1) * S], ACT.Identity, bias=b_q1s[:, e:e + 1],
                               scale=1.0 / 16.0).then_inc(s["c_q"], 1)
            yield 42
            act.wait_ge(s["c_max"], 1)
            for t in range(T):
                act.activation(pe_[:, 0, t, :], b7[:, t * S:(t + 1) * S], ACT.Exp, bias=nmax[:, 0, t:t + 1],
                               accum_out=sums[:, t:t + 1]).then_inc(s["c_p"], 1)
            yield 43
            act.wait_ge(s["c_pT_ps"], 1)
            act.activation(pT[:, 0, :, :].rearrange("p a b -> p (a b)"), b5[:, :], ACT.Copy).then_inc(s["c_pT"], 1)
            yield 44
            act.wait_ge(s["c_ctx_ps"], 1)
            act.activation(flat(cT[:, :, :]), b3[:, :], ACT.Copy).then_inc(s["c_ctx"], 1)

        def c_dve(dve, own, x5=x5):
            b3, b4, b5, b6, b7 = bank[3:8]
            yield 37
            dve.wait_ge(s["t1_norm"], T)
            stats(dve, own, x4, "c")
            normal(dve, x4, x1n, "c")
            yield 40
            dve.wait_ge(s["c_v_ps"], 1)
            dve.tensor_tensor(v1x[:, :, :], b3[:, :].rearrange("p (t e) -> p t e", t=T),
                              b_v1[:, :].unsqueeze(1).to_broadcast([P, T, E2]), ALU.add).then_inc(s["c_v"], 1)
            yield 42
            dve.wait_ge(s["c_s_ps"], 1)
            dve.tensor_reduce(nmax[:, 0, :], b7[:, :].rearrange("p (t k) -> p t k", t=T), AX, ALU.max, negate=True).then_inc(s["c_max"], 1)
            dve.wait_ge(s["c_p"], 2)
            own.link(dve.reciprocal(rsum[:, :], sums[:, :]))
            yield 45
            dve.wait_ge(s["c_out_ps"], 1)
            dve.wait_ge(s["c_x4b"], 1)
            for t in range(T):
                last = dve.scalar_tensor_tensor(x5[:, t, :], b4[:, t * D:(t + 1) * D], rsum[:, t:t + 1], x4b[:, t, :], ALU.mult, ALU.add)
                if t == T - 1:
                    last.then_inc(s["c_res"], 1)
                else:
                    own.did(last)
            own.wait()
            dve.wait_ge(s["c_res"], 1)
            stats(dve, own, x5, "c1")
            normal(dve, x5, x5, "c1")

        def c_pool(pool, own):
            yield 37
            rstd(pool, "c")
            pool.wait_ge(s["t1_norm"], T)
            pool.tensor_tensor(x4b[:, :, :], x4[:, :, :], b_o1[:, :].unsqueeze(1).to_broadcast([P, T, D]), ALU.add).then_inc(s["c_x4b"], 1)
            yield 45
            rstd(pool, "c1")

        GB = [bank[3], bank[4], bank[6]]

        def l_pe(pe, x5=x5):
            b3, b4, b5, b6, b7 = bank[3:8]
            yield 46
            pe.wait_ge(s["c_res"], 1)
            for g in range(3):
                for m in range(KD):
                    for k in range(KD):
                        last = pe.matmul(GB[g][:, m * S:(m + 1) * S], u_g[:, g, k, m * P:(m + 1) * P], state[:, k, :],
                                         start=(m == 0 and k == 0), stop=False, skip_group_check=True)
            last.then_inc(s["l_u_ps"], 1)
            pe.wait_ge(s["c1_norm"], T)
            turn(pe, x5, b5, "l_xT_ps")
            yield 47
            pe.wait_ge(s["l_xT"], 1)
            for t in range(T):
                last = mm(pe, b7[:, t * D:(t + 1) * D], [(xT[:, k, t * P:(t + 1) * P], w_ho[:, k, :]) for k in range(KD)])
            last.then_inc(s["l_xw_ps"], 1)
            for g in range(3):
                for m in range(KD):
                    for k in range(KD):
                        last = pe.matmul(GB[g][:, m * S:(m + 1) * S], w_g[:, g, k, m * P:(m + 1) * P], xT[:, k, :],
                                         start=False, stop=(k == KD - 1), skip_group_check=True)
                last.then_inc(s["l_g_ps"], 1)

        def l_act(act, own, b, xw=xw):
            b3, b4, b5, b6, b7 = bank[3:8]
            yield 46
            act.wait_ge(s["l_xT_ps"], 1)
            act.activation(flat(xT[:, :, :]), b5[:, :], ACT.Copy).then_inc(s["l_xT"], 1)
            yield 47
            act.wait_ge(s["l_xw_ps"], 1)
            act.activation(xw, b7[:, :], ACT.Copy).then_inc(s["l_xw"], 1)
            for g in range(3):
                act.wait_ge(s["l_g_ps"], g + 1)
                for m in range(KD):
                    act.activation(tg[:, g, m, :], GB[g][:, m * S:(m + 1) * S], ACT.Tanh, bias=b_gh[:, g, m:m + 1],
                                   scale=1.0 if g == 2 else 0.5).then_inc(s["l_tanh"], 1)

        def l_dve(dve, own):
            yield 47
            dve.wait_ge(s["l_tanh"], 2)
            own.did(dve.scalar_tensor_tensor(flat(ug[:, 0, :, :]), flat(tg[:, 0, :, :]), 1.0, flat(state[:, :, :]), ALU.add, ALU.mult))
            dve.wait_ge(s["l_tanh"], 6)
            own.link(dve.scalar_tensor_tensor(flat(ug[:, 1, :, :]), flat(tg[:, 1, :, :]), 1.0, flat(tg[:, 2, :, :]), ALU.add, ALU.mult))
            dve.wait_ge(s["l_u_ps"], 1)
            dve.scalar_tensor_tensor(flat(state[:, :, :]), flat(ug[:, 0, :, :]), 0.5, flat(ug[:, 1, :, :]), ALU.mult, ALU.add).then_inc(s["l_state"], 1)

        def l_sp(sp, b):
            yield 46
            sp.wait_ge(s["c1_norm"], T)
            sp.dma_start(kept_x[bass.ds(b, 1), :, :].rearrange("a p n -> p (a n)"), flat(x5[:, :, :])).then_inc(s["l_kept"], 16)
            yield 47
            sp.wait_ge(s["l_xw"], 1)
            sp.dma_start(kept_w[bass.ds(b, 1), :, :].rearrange("a p n -> p (a n)"), xw[:, :]).then_inc(s["l_kept"], 16)
            sp.wait_ge(s["l_kept"], 32)

        FOLDS = []
        for k in range(KD):
            for j in range(2):
                FOLDS.append((w_q[:, k, j * 512:(j + 1) * 512], lora_a[:, 0, k * P:(k + 1) * P], qb[:, j * 512:(j + 1) * 512]))
            FOLDS.append((w_k[:, k, :], lora_a[:, 1, k * P:(k + 1) * P], kb[:, :]))
            FOLDS.append((w_v[:, k, :], lora_a[:, 2, k * P:(k + 1) * P], vb[:, :]))
        for c in range(8):
            FOLDS.append((w_ao[:, c, :], lora_ao[:, c * P:(c + 1) * P], obm[:, :]))

        folds_at = {0: [-1], NA - 2: [len(FOLDS)]}
        for n in range(len(FOLDS)):
            folds_at.setdefault(at(3) + (3 * n) // 2, []).append(n)

        def fold_pe(pe):
            yield -1
            pe.wait_ge(s["prep_halves"], 3)
            for n, (dst, l, r) in enumerate(FOLDS):
                yield n
                if n == 0:
                    pe.wait_ge(s["loads_loras"], N_LORAS)
                if n >= 2:
                    pe.wait_ge(s["prep_evac"], n - 1)
                pe.matmul(bank[3 + n % 2][:, 0:dst.shape[1]], l, r, start=True, stop=True).then_inc(s["prep_pe"], 1)

        def fold_dve(dve, own):
            yield -1
            dve.wait_ge(s["loads_mamba"], N_FIRST)
            dve.tensor_scalar(flat(conv_wh[:, :, :]), flat(conv_w[:, :, :]), 0.5, None, ALU.mult).then_inc(s["prep_halves"], 1)
            dve.tensor_scalar(conv_bh[:, :], conv_b[:, :], 0.5, None, ALU.mult).then_inc(s["prep_halves"], 1)
            dve.tensor_scalar(w_in[:, :, DI:], w_in[:, :, DI:], 0.5, None, ALU.mult).then_inc(s["prep_halves"], 1)
            dve.wait_ge(s["prep_halves"], 3)
            for n, (dst, _, _) in enumerate(FOLDS):
                yield n
                dve.wait_ge(s["prep_pe"], n + 1)
                dve.scalar_tensor_tensor(dst, bank[3 + n % 2][:, 0:dst.shape[1]], LSCALE, dst, ALU.mult, ALU.add).then_inc(s["prep_evac"], 1)
            yield len(FOLDS)
            dve.wait_ge(s["loads_rest"], N_REST)
            own.did(dve.tensor_scalar(b_q1s[:, :], b_q1[:, :], 1.0 / 16.0, None, ALU.mult))
            own.did(dve.tensor_scalar(flat(b_gh[:, 0:2, :]), flat(b_g[:, 0:2, :]), 0.5, None, ALU.mult))
            own.did(dve.tensor_copy(b_gh[:, 2, :], b_g[:, 2, :]))
            own.did(dve.tensor_scalar(u_g[:, :, :, :].rearrange("p a b c -> p (a b c)"), u_g[:, :, :, :].rearrange("p a b c -> p (a b c)"),
                                      0.5, None, ALU.mult))
            own.did(dve.tensor_scalar(flat(u_ho[:, :, :]), flat(u_ho[:, :, :]), 0.5, None, ALU.mult))
            own.link(dve.memset(state[:, :, :], 2.0))
            for k in range(KD):
                own.did(dve.tensor_scalar(state[:, k, :], state[:, k, :], in_c[:, k:k + 1], None, ALU.mult))
            whole_b, high_b = [turns[0:NPACK, 4 * i:4 * i + 4, :].rearrange("p a b -> p (a b)") for i in range(2)]
            own.link(dve.tensor_copy(high_b.bitcast(F32R), whole_b))
            own.link(dve.tensor_scalar(whole_b, whole_b, part[:, 0:1], None, ALU.mult))
            own.did(dve.scalar_tensor_tensor(w_b[:, :], high_b, part[:, 1:2], whole_b, ALU.mult, ALU.add))

        def whole(x):
            return x if isinstance(x, bass.AP) else x[tuple([slice(None)] * len(x.shape))]

        FIRST = [(w_in, "w_in"), (w_xp, "w_xp"), (w_out, "w_out"), (conv_w, "conv_w"), (conv_b, "conv_b"), (ln_g, "ln_g"), (ln_b, "ln_b"),
                 (w_dt, "w_dt"), (b_dt, "b_dt"), (a_log, "a_log"), (d_skip, "d_skip")]
        LORAS = [(whole(x), name) for x, name in [
            (w_q, "w_q"), (w_k, "w_k"), (w_v, "w_v"), (w_ao, "w_ao"),
            (lora_a, "lora_a"), (lora_ao, "lora_ao"), (qb, "qb"), (kb, "kb"), (vb, "vb"), (obm, "ob")]]
        REST = [(whole(x), name) for x, name in [
            (wv0, "wv0"), (bv0, "bv0"), (wt0[:, 0, :], "wt0a"), (wt0[0:CTX2, 1, :], "wt0b"), (bt0, "bt0"), (w_gl, "w_gl"), (part, "part"),
            (w_i, "w_i"), (w_o, "w_o"), (prio, "prio"), (rope, "rope"),
            (ln1_g, "ln1_g"), (ln1_b, "ln1_b"), (ln2_g[:, 0:1], "ln2_ga"), (ln2_g[0:CTX2, 1:2], "ln2_gb"),
            (ln2_b[:, 0:1], "ln2_ba"), (ln2_b[0:CTX2, 1:2], "ln2_bb"),
            (w_q1, "w_q1"), (w_k1[:, 0, :], "w_k1a"), (w_k1[0:CTX2, 1, :], "w_k1b"), (w_v1[:, 0, :], "w_v1a"), (w_v1[0:CTX2, 1, :], "w_v1b"),
            (w_o1, "w_o1"), (b_q1, "b_q1"), (b_k1, "b_k1"), (w_g, "w_g"), (u_g, "u_g"), (b_g, "b_g"), (w_ho, "w_ho"), (u_ho, "u_ho"),
            (in_c, "in_c")]]
        REST += [(turns[NLOW * i:NLOW * (i + 1), 0:4, :].rearrange("p a b -> p (a b)"), "w_b") for i in range(PARTS)]
        ROWS = [(b_gl, "b_gl"), (b_v1, "b_v1"), (b_o1, "b_o1"), (b_ho, "b_ho")]
        N_FIRST, N_LORAS, N_REST = 16 * len(FIRST), 16 * len(LORAS), 16 * (len(REST) + len(ROWS))

        def ended(eng, n):
            eng.drain().then_inc(arrived, 1)
            eng.wait_ge(phase, n)

        def next_phase(sp):
            sp.wait_ge(arrived, 4)
            sp.sem_clear(range(numbers[0], numbers[-1] + 1))
            sp.sem_clear(arrived)
            sp.sem_inc(phase, 1)

        def merged(order, mamba, rest):
            streams = {"A": chained(mamba), "B": chained(rest)}
            at = {k: next(g, 999) for k, g in streams.items()}
            for name, unit in order:
                while at[name] <= unit:
                    at[name] = next(streams[name], 999)

        def chained(parts):
            for g in parts:
                yield from g

        WITH_FOLDS = [x for u in range(NA) for x in [("A", u)] + [("B", n) for n in folds_at.get(u, [])]]
        ONLY_B = [("B", u) for u in range(NB_UNITS)]

        def program(eng, name, parts_a, parts_b, parts_last):
            with eng.Fori(0, NB - 1) as b:
                merged(order(name), parts_a(b + 1), parts_b(b))
                ended(eng, b + 2)
            merged(ONLY_B, [], parts_last)
            ended(eng, NB + 1)

        block = ctx.enter_context(nc.Block())

        @block.sync
        def _(sp):
            gen = a_sp(sp, 0)
            next(gen)
            next(gen)
            for dst, name in FIRST:
                sp.dma_start(dst[tuple([slice(None)] * len(dst.shape))], A[name]).then_inc(s["loads_mamba"], 16)
            for dst, name in LORAS:
                sp.dma_start(dst, A[name]).then_inc(s["loads_loras"], 16)
            for _ in gen:
                pass
            load_context(sp, 0)
            for dst, name in REST:
                sp.dma_start(dst, A[name]).then_inc(s["loads_rest"], 16)
            for dst, name in ROWS:
                sp.dma_start(dst[:, :], A[name].partition_broadcast(P)).then_inc(s["loads_rest"], 16)
            sp.wait_ge(s["b_ctx"], 16)
            next_phase(sp)
            with sp.Fori(0, NB - 1) as b:
                merged(order("sp"), [a_sp(sp, b + 1)], [r_sp(sp, b + 1), l_sp(sp, b)])
                sp.wait_ge(s["b_ctx"], 16)
                next_phase(sp)
            for kept, dst in [(kept_w, XW), (kept_x, XS)]:
                sp.dma_start(dst[:, 0:NB - 1, :], kept[0:NB - 1, :, :].rearrange("b p n -> p b n")).then_inc(s["e_load"], 16)
            sp.wait_ge(s["e_load"], 32)
            next_phase(sp)
            out_v = out.rearrange("b (t p) d -> p (b t) d", p=P)
            for b in range(NB):
                sp.wait_ge(s["e_norm"], 2 * b + 2)
                sp.dma_start(out_v[:, 2 * b:2 * b + 2, :], XS[:, b, :].rearrange("p (t d) -> p t d", t=T)).then_inc(s["e_store"], 16)
            sp.wait_ge(s["e_store"], 16 * NB)

        @block.gpsimd
        def _(pool):
            own = Own(pool, s["pool_own"])
            own.did(pool.memset(ident[:, :], 0.0))
            own.did(pool.memset(neghalf[:, :], -0.5))
            pool.memset(ones[:, :], 1.0).then_inc(s["prep_pool"], 1)
            for i in range(2):
                pool.memset(dA[i][:, :, 0:1], 0.0).then_inc(s["prep_pool"], 1)
            pool.memset(v1[:, :, :, HD:HD + 1], 1.0).then_inc(s["prep_pool"], 1)
            own.wait()
            pool.affine_select(out=ident[:, :], in_=ident[:, :], compare_op=ALU.not_equal, fill=1.0, base=0, pattern=[[-1, P]],
                               channel_multiplier=1).then_inc(s["prep_pool"], 1)
            merged(WITH_FOLDS, [a_pool(pool, own, alone=True)], [])
            ended(pool, 1)

            def parts_a(b):
                return [a_pool(pool, Own(pool, s["pool_own"]))]

            def parts_b(b):
                own = Own(pool, s["pool_own"])
                return [b_pool(pool, own), f_pool(pool, own), t_pool(pool, own), c_pool(pool, own)]

            program(pool, "pool", parts_a, parts_b, parts_b(NB - 1))
            for i in range(2):
                half = slice(NB * i, NB * (i + 1))
                pool.wait_ge(s["e_var"], i + 1)
                pool.tensor_tensor(e_rs[:, half], e_var[:, half], neghalf[:, half], ALU.pow).then_inc(s["e_rstd"], 1)

        @block.scalar
        def _(act):
            own = Own(act, s["act_own"])
            act.wait_ge(s["loads_mamba"], N_FIRST)
            act.activation(flat(a_neg[:, :, :]), flat(a_log[:, :, :]), ACT.Exp).then_inc(s["prep_act"], 1)
            act.wait_ge(s["prep_act"], 1)
            act.activation(flat(a_neg[:, :, :]), flat(a_neg[:, :, :]), ACT.Copy, scale=-1.0).then_inc(s["prep_act"], 1)
            act.wait_ge(s["prep_act"], 2)
            act.wait_ge(s["prep_halves"], 3)
            act.wait_ge(s["prep_pool"], 3)
            merged(WITH_FOLDS, [a_act(act, own)], [])
            ended(act, 1)
            program(act, "act", lambda b: [a_act(act, Own(act, s["act_own"]))],
                    lambda b: [b_act(act, None), f_act(act, None), t_act(act, None), c_act(act, None), l_act(act, None, b)],
                    [b_act(act, None), f_act(act, None), t_act(act, None), c_act(act, None), l_act(act, None, NB - 1, XW[:, NB - 1, :])])
            for i in range(2):
                act.wait_ge(s["e_sum"], i + 1)
                act.activation(flat(XW[:, 4 * i:4 * i + 4, :]), flat(XW[:, 4 * i:4 * i + 4, :]), ACT.Tanh).then_inc(s["e_tanh"], 1)

        @block.vector
        def _(dve):
            own = Own(dve, s["dve_own"])
            merged(WITH_FOLDS, [a_dve(dve, own, alone=True)], [fold_dve(dve, own)])
            ended(dve, 1)
            with dve.Fori(0, NB - 1) as b:
                own = Own(dve, s["dve_own"])
                merged(order("dve"), [a_dve(dve, own)], [b_dve(dve, own), f_dve(dve, own), t_dve(dve, own), c_dve(dve, own), l_dve(dve, own)])
                ended(dve, b + 2)
            own = Own(dve, s["dve_own"])
            merged(ONLY_B, [], [b_dve(dve, own), f_dve(dve, own), t_dve(dve, own), c_dve(dve, own, x5_last), l_dve(dve, own)])
            ended(dve, NB + 1)
            own = Own(dve, s["dve_own"])
            dve.wait_ge(s["e_cu_ps"], 1)
            own.link(dve.tensor_tensor(cu[:, :].rearrange("p (t d) -> p t d", t=T), bank[0][:, :].rearrange("p (t d) -> p t d", t=T),
                                       b_ho[:, :].unsqueeze(1).to_broadcast([P, T, D]), ALU.add))
            for i in range(2):
                dve.tensor_tensor(XW[:, 4 * i:4 * i + 4, :], XW[:, 4 * i:4 * i + 4, :], cu[:, :].unsqueeze(1).to_broadcast([P, 4, T * D]),
                                  ALU.add).then_inc(s["e_sum"], 1)
            for i in range(2):
                rows = range(NB * i, NB * (i + 1))
                dve.wait_ge(s["e_tanh"], i + 1)
                own.link(dve.tensor_tensor(flat(XS[:, 4 * i:4 * i + 4, :]), flat(XS[:, 4 * i:4 * i + 4, :]), flat(XW[:, 4 * i:4 * i + 4, :]), ALU.add))
                for r in rows:
                    own.did(dve.bn_stats(e_st[:, r, :], XS[:, r // 2, (r % 2) * D:(r % 2 + 1) * D]))
                own.wait()
                for r in rows:
                    own.did(dve.bn_aggr(e_mv[:, r, :], e_st[:, r, :]))
                own.wait()
                half = slice(NB * i, NB * (i + 1))
                dve.tensor_scalar(e_var[:, half], e_mv[:, half, 1], EPS, None, ALU.add).then_inc(s["e_var"], 1)
            for i in range(2):
                dve.wait_ge(s["e_rstd"], i + 1)
                for r in range(NB * i, NB * (i + 1)):
                    x = XS[:, r // 2, (r % 2) * D:(r % 2 + 1) * D]
                    dve.tensor_scalar(x, x, e_mv[:, r, 0:1], e_rs[:, r:r + 1], ALU.subtract, ALU.mult).then_inc(s["e_norm"], 1)

        @block.tensor
        def _(pe):
            pe.wait_ge(s["prep_pool"], 5)
            merged(WITH_FOLDS, [a_pe(pe, alone=True)], [fold_pe(pe)])
            ended(pe, 1)
            program(pe, "pe", lambda b: [a_pe(pe)], lambda b: [b_pe(pe), f_pe(pe), t_pe(pe), c_pe(pe), l_pe(pe)],
                    [b_pe(pe), f_pe(pe), t_pe(pe), c_pe(pe), l_pe(pe, x5_last)])
            for t in range(T):
                last = mm(pe, bank[0][:, t * D:(t + 1) * D], [(state[:, k, t * P:(t + 1) * P], u_ho[:, k, :]) for k in range(KD)])
            last.then_inc(s["e_cu_ps"], 1)


def arrays_of(i):
    def t(a):
        return np.ascontiguousarray(a)

    def kp(a):
        return t(a.reshape(-1, P, a.shape[1]).transpose(1, 0, 2))

    def cp(a):
        return t(a.reshape(-1, P).T)

    def eo(a, heads):
        return t(a.reshape(heads, HH, 2, -1).transpose(0, 2, 1, 3).reshape(heads * HD, -1))

    xp = i["L0_attn_W_xp"]
    wt = i["L0_xattn_Wt"].T
    g2, b2 = i["L1_xattn_ln2_g"], i["L1_xattn_ln2_b"]
    f = [i[f"L1_ffn_{n}"].T for n in ("wf", "wi", "wc")]
    u = [i[f"L1_ffn_{n}"].T for n in ("uf", "ui", "uc")]
    inv = (np.float32(1.0) / np.float32(10000.0) ** (np.arange(0, HD, 2, dtype=np.float32) / np.float32(HD))).astype(np.float32)
    ang = (np.arange(S, dtype=np.float32)[:, None] * inv[None, :]).astype(np.float32).astype(np.float64)
    co, si = np.cos(ang).astype(np.float32), np.sin(ang).astype(np.float32)
    rope = np.stack([co, si, -si], axis=1)
    rope = np.stack([rope, rope / np.float32(8)], axis=1).reshape(T, P, 2, 3, HH).transpose(1, 0, 2, 3, 4)
    return {
        "x": i["x"], "ctx": i["ctx_768"],
        "w_in": kp(i["L0_attn_W_in"]), "w_xp": kp(xp), "w_out": kp(i["L0_attn_W_out"]),
        "conv_w": kp(i["L0_attn_conv_w"]), "conv_b": cp(i["L0_attn_conv_b"]), "ln_g": cp(i["L0_attn_ln_g"]), "ln_b": cp(i["L0_attn_ln_b"]),
        "w_dt": cp(i["L0_attn_W_dt"][0]), "b_dt": cp(i["L0_attn_b_dt"]), "a_log": kp(i["L0_attn_A_log"]), "d_skip": cp(i["L0_attn_D"]),
        "wv0": kp(t(i["L0_xattn_Wv"].T)), "bv0": cp(i["L0_xattn_bv"]), "wt0a": t(wt[:P]), "wt0b": t(wt[P:]), "bt0": cp(i["L0_xattn_bt"]),
        "w_gl": kp(t(np.concatenate([i["L0_ffn_Wg"].T, i["L0_ffn_A"].reshape(NLOW, D).T], axis=1))),
        "b_gl": t(i["L0_ffn_bg"]), "w_b": t(i["L0_ffn_B"].transpose(0, 2, 1).reshape(NLOW, FF)),
        "w_i": kp(t(i["L0_ffn_Wi"].T)), "w_o": kp(t(i["L0_ffn_Wo"].T)),
        "part": np.repeat(np.array([[0, 1], [1, -1], [0, 1], [1, -1]], dtype=np.float32), NLOW, axis=0),
        "prio": np.tile(np.arange(NE, 0, -1, dtype=np.float32), (P, 1)),
        "w_q": kp(t(eo(i["L1_attn_Wq"], NQ).T)), "w_k": kp(t(eo(i["L1_attn_Wk"], NKV).T)), "w_v": kp(t(i["L1_attn_Wv"].T)),
        "w_ao": kp(t(i["L1_attn_Wo"].T)), "lora_a": t(np.stack([i["L1_attn_qA"], i["L1_attn_kA"], i["L1_attn_vA"]], axis=1)),
        "lora_ao": i["L1_attn_oA"], "qb": t(eo(i["L1_attn_qB"], NQ).T), "kb": t(eo(i["L1_attn_kB"], NKV).T), "vb": t(i["L1_attn_vB"].T),
        "ob": t(i["L1_attn_oB"].T), "rope": t(rope),
        "ln1_g": cp(i["L1_xattn_ln1_g"]), "ln1_b": cp(i["L1_xattn_ln1_b"]),
        "ln2_ga": t(g2[:P, None]), "ln2_gb": t(g2[P:, None]), "ln2_ba": t(b2[:P, None]), "ln2_bb": t(b2[P:, None]),
        "w_q1": kp(i["L1_xattn_Wq"]), "w_k1a": t(i["L1_xattn_Wk"][:P]), "w_k1b": t(i["L1_xattn_Wk"][P:]),
        "w_v1a": t(i["L1_xattn_Wv"][:P]), "w_v1b": t(i["L1_xattn_Wv"][P:]), "w_o1": kp(i["L1_xattn_Wo"]),
        "b_q1": cp(i["L1_xattn_bq"]), "b_k1": cp(i["L1_xattn_bk"]), "b_v1": i["L1_xattn_bv"], "b_o1": i["L1_xattn_bo"],
        "w_g": t(np.stack([kp(t(a)) for a in f], axis=1)), "u_g": t(np.stack([kp(t(a)) for a in u], axis=1)),
        "b_g": t(np.stack([cp(i[f"L1_ffn_{n}"]) for n in ("bf", "bi", "bc")], axis=1)),
        "w_ho": kp(t(i["L1_ffn_wo"].T)), "u_ho": kp(t(i["L1_ffn_uo"].T)), "b_ho": i["L1_ffn_bo"], "in_c": cp(i["L1_ffn_in_c"]),
    }


def kernel(**inputs):
    import concourse.bacc as _bacc
    from concourse.bass_utils import run_bass_kernel_spmd as _run

    nc = _bacc.Bacc("TRN2", target_bir_lowering=False, num_devices=1)
    arrays = {f"in_{k}": np.ascontiguousarray(v) for k, v in arrays_of({k: np.asarray(v) for k, v in inputs.items()}).items()}
    A = {k[3:]: nc.dram_tensor(k, v.shape, F32, kind="ExternalInput").ap() for k, v in arrays.items()}
    out = nc.dram_tensor("out", (NB, S, D), F32, kind="ExternalOutput").ap()
    build(nc, A, out)
    r = _run(nc, [arrays], core_ids=[0])
    return r.results[0]["out"]
```
